# Optimizing a Trainium2 kernel written in Bass

```python
import numpy as np
import jax
import jax.numpy as jnp

def _softmax(x, axis=-1):
    return jax.nn.softmax(x, axis=axis)

def _gelu(x):
    return jax.nn.gelu(x, approximate=True)

def _silu(x):
    return jax.nn.silu(x)

def _sigmoid(x):
    return jax.nn.sigmoid(x)

def _layernorm(x, axis=-1, eps=1e-05):
    m = jnp.mean(x, axis=axis, keepdims=True)
    v = jnp.var(x, axis=axis, keepdims=True)
    return (x - m) / jnp.sqrt(v + eps)

def _scatter_add(tgt, idx, src, axis=0):
    return tgt.at[idx].add(src)

def _segment_sum(src, seg, n):
    return jax.ops.segment_sum(src, seg, n)
kernel_name = 'mk_hybrid_d1_jaxref_r8_dfbbc5'

def setup_inputs(seed: int=0):
    np.random.seed(seed)
    _w = jnp.asarray

    def _L0_attn_a_setup():
        import jax, jax.numpy as jnp
        import numpy as np
        from jax import lax
        key = jax.random.key(seed)
        ks = jax.random.split(key, 8)
        B, L, H = (2, 128, 256)
        E = 2
        d = H * E
        S = 16
        R = 128
        sc = lambda fan_in: 1.0 / np.sqrt(fan_in)
        return {'x': jax.random.normal(ks[0], (B, L, H), jnp.float32), 'W_in': jax.random.normal(ks[1], (H, 2 * d), jnp.float32) * sc(H), 'conv_w': jax.random.normal(ks[2], (d, 1, 3), jnp.float32) * sc(3), 'conv_b': jnp.zeros((d,), jnp.float32), 'W_x': jax.random.normal(ks[3], (d, R + 2 * S), jnp.float32) * sc(d), 'W_dt': jax.random.normal(ks[4], (R, d), jnp.float32) * sc(R), 'b_dt': jnp.zeros((d,), jnp.float32), 'A_log': jnp.log(jnp.tile(jnp.arange(1, S + 1, dtype=jnp.float32), (d, 1))), 'D': jnp.ones((d,), jnp.float32), 'W_out': jax.random.normal(ks[5], (d, H), jnp.float32) * sc(d)}
    _L0_attn_a_in = _L0_attn_a_setup()

    def _L0_attn_b_setup():
        import jax, jax.numpy as jnp
        import numpy as np
        N_HEADS = 16
        D_HEAD = 128
        D_MODEL = 256
        MAXLEN = 256
        key = jax.random.key(seed)
        ks = jax.random.split(key, 9)
        b, t = (2, 256)
        hd = N_HEADS * D_HEAD
        init = 0.02
        return {'x': jax.random.normal(ks[0], (b, t, D_MODEL), dtype=jnp.float32), 'Wq': jax.random.normal(ks[1], (D_MODEL, hd), dtype=jnp.float32) * init, 'bq': jnp.zeros((hd,), dtype=jnp.float32), 'Wk': jax.random.normal(ks[2], (D_MODEL, hd), dtype=jnp.float32) * init, 'bk': jnp.zeros((hd,), dtype=jnp.float32), 'Wv': jax.random.normal(ks[3], (D_MODEL, hd), dtype=jnp.float32) * init, 'bv': jnp.zeros((hd,), dtype=jnp.float32), 'Wo': jax.random.normal(ks[4], (hd, D_MODEL), dtype=jnp.float32) * init, 'bo': jnp.zeros((D_MODEL,), dtype=jnp.float32)}
    _L0_attn_b_in = _L0_attn_b_setup()

    def _L0_ffn_setup():
        import jax, jax.numpy as jnp
        import numpy as np
        HIDDEN = 256
        INTER = 688
        LUT_SIZE = 16

        def _ghost_linear(x, idx, lut):
            w = lut[idx]
            return jnp.einsum('bsh,oh->bso', x, w)
        key = jax.random.key(seed)
        k_x, k_lut, k_g, k_u, k_d = jax.random.split(key, 5)
        x = jax.random.normal(k_x, (2, 512, HIDDEN), dtype=jnp.float32)
        lut = jax.random.normal(k_lut, (LUT_SIZE,), dtype=jnp.float32) * 0.02
        gate_idx = jax.random.randint(k_g, (INTER, HIDDEN), 0, LUT_SIZE, dtype=jnp.int32)
        up_idx = jax.random.randint(k_u, (INTER, HIDDEN), 0, LUT_SIZE, dtype=jnp.int32)
        down_idx = jax.random.randint(k_d, (HIDDEN, INTER), 0, LUT_SIZE, dtype=jnp.int32)
        return {'x': x, 'lut': lut, 'gate_idx': gate_idx, 'up_idx': up_idx, 'down_idx': down_idx}
    _L0_ffn_in = _L0_ffn_setup()
    _d = {'L0_attn_a_x': _L0_attn_a_in['x'], 'L0_attn_a_W_in': _L0_attn_a_in['W_in'], 'L0_attn_a_conv_w': _L0_attn_a_in['conv_w'], 'L0_attn_a_conv_b': _L0_attn_a_in['conv_b'], 'L0_attn_a_W_x': _L0_attn_a_in['W_x'], 'L0_attn_a_W_dt': _L0_attn_a_in['W_dt'], 'L0_attn_a_b_dt': _L0_attn_a_in['b_dt'], 'L0_attn_a_A_log': _L0_attn_a_in['A_log'], 'L0_attn_a_D': _L0_attn_a_in['D'], 'L0_attn_a_W_out': _L0_attn_a_in['W_out'], 'L0_attn_b_Wq': _L0_attn_b_in['Wq'], 'L0_attn_b_bq': _L0_attn_b_in['bq'], 'L0_attn_b_Wk': _L0_attn_b_in['Wk'], 'L0_attn_b_bk': _L0_attn_b_in['bk'], 'L0_attn_b_Wv': _L0_attn_b_in['Wv'], 'L0_attn_b_bv': _L0_attn_b_in['bv'], 'L0_attn_b_Wo': _L0_attn_b_in['Wo'], 'L0_attn_b_bo': _L0_attn_b_in['bo'], 'L0_ffn_lut': _L0_ffn_in['lut'], 'L0_ffn_gate_idx': _L0_ffn_in['gate_idx'], 'L0_ffn_up_idx': _L0_ffn_in['up_idx'], 'L0_ffn_down_idx': _L0_ffn_in['down_idx']}
    _x0 = _d['L0_attn_a_x']
    _d['L0_attn_a_x'] = jax.random.normal(jax.random.fold_in(jax.random.key(seed), 1), (1, 1024, 256), dtype=_x0.dtype)
    del _x0
    return _d

def reference(L0_attn_a_x, L0_attn_a_W_in, L0_attn_a_conv_w, L0_attn_a_conv_b, L0_attn_a_W_x, L0_attn_a_W_dt, L0_attn_a_b_dt, L0_attn_a_A_log, L0_attn_a_D, L0_attn_a_W_out, L0_attn_b_Wq, L0_attn_b_bq, L0_attn_b_Wk, L0_attn_b_bk, L0_attn_b_Wv, L0_attn_b_bv, L0_attn_b_Wo, L0_attn_b_bo, L0_ffn_lut, L0_ffn_gate_idx, L0_ffn_up_idx, L0_ffn_down_idx):

    def _L0_attn_a_ref(x, W_in, conv_w, conv_b, W_x, W_dt, b_dt, A_log, D, W_out):
        import jax, jax.numpy as jnp
        import numpy as np
        from jax import lax
        d = conv_b.shape[0]
        S = A_log.shape[1]
        R = W_dt.shape[0]
        xz = x @ W_in
        xp, z = jnp.split(xz, 2, axis=-1)
        xc = lax.conv_general_dilated(jnp.transpose(xp, (0, 2, 1)), conv_w, (1,), [(1, 1)], feature_group_count=d, dimension_numbers=('NCH', 'OIH', 'NCH'))
        xc = jnp.transpose(xc + conv_b[None, :, None], (0, 2, 1))
        xc = jax.nn.silu(xc)
        x_dbl = xc @ W_x
        dt_in = x_dbl[..., :R]
        Bm = x_dbl[..., R:R + S]
        Cm = x_dbl[..., R + S:]
        dt = jax.nn.softplus(dt_in @ W_dt + b_dt)
        A = -jnp.exp(A_log)

        def step(h, ins):
            u_t, dt_t, B_t, C_t = ins
            dA = jnp.exp(dt_t[:, :, None] * A)
            h = dA * h + dt_t[:, :, None] * B_t[:, None, :] * u_t[:, :, None]
            y_t = jnp.einsum('bds,bs->bd', h, C_t)
            return (h, y_t)
        h0 = jnp.zeros((x.shape[0], d, S), xc.dtype)
        xsT = (jnp.swapaxes(xc, 0, 1), jnp.swapaxes(dt, 0, 1), jnp.swapaxes(Bm, 0, 1), jnp.swapaxes(Cm, 0, 1))
        _, yT = lax.scan(step, h0, xsT)
        y = jnp.swapaxes(yT, 0, 1) + xc * D
        y = y * jax.nn.silu(z)
        return y @ W_out

    def _L0_attn_b_ref(x, Wq, bq, Wk, bk, Wv, bv, Wo, bo):
        import jax, jax.numpy as jnp
        import numpy as np
        N_HEADS = 16
        D_HEAD = 128
        D_MODEL = 256
        MAXLEN = 256
        b, t, _ = x.shape
        h, dh = (N_HEADS, D_HEAD)
        scale = 1.0 / np.sqrt(dh).astype(np.float32)
        q = (x @ Wq + bq).reshape(b, h, t, dh)
        k = (x @ Wk + bk).reshape(b, t, h, dh).transpose(0, 2, 3, 1)
        v = (x @ Wv + bv).reshape(b, t, h, dh).transpose(0, 2, 1, 3)
        logits = jnp.einsum('bhtd,bhds->bhts', q, k) * scale
        mask = jnp.triu(jnp.full((t, t), -jnp.inf, dtype=x.dtype), k=1)
        weights = jax.nn.softmax(logits + mask, axis=-1)
        out = jnp.einsum('bhts,bhsd->bhtd', weights, v)
        out = out.transpose(0, 2, 1, 3).reshape(b, t, h * dh)
        return out @ Wo + bo

    def _L0_ffn_ref(x, lut, gate_idx, up_idx, down_idx):
        import jax, jax.numpy as jnp
        import numpy as np
        HIDDEN = 256
        INTER = 688
        LUT_SIZE = 16

        def _ghost_linear(x, idx, lut):
            w = lut[idx]
            return jnp.einsum('bsh,oh->bso', x, w)
        gate = _ghost_linear(x, gate_idx, lut)
        up = _ghost_linear(x, up_idx, lut)
        h = jax.nn.silu(gate) * up
        return _ghost_linear(h, down_idx, lut)
    x = L0_attn_a_x
    x = x + _L0_attn_a_ref(_layernorm(x, axis=-1), L0_attn_a_W_in, L0_attn_a_conv_w, L0_attn_a_conv_b, L0_attn_a_W_x, L0_attn_a_W_dt, L0_attn_a_b_dt, L0_attn_a_A_log, L0_attn_a_D, L0_attn_a_W_out)
    x = x + _L0_ffn_ref(_layernorm(x, axis=-1), L0_ffn_lut, L0_ffn_gate_idx, L0_ffn_up_idx, L0_ffn_down_idx)
    x = x + _L0_attn_b_ref(_layernorm(x, axis=-1), L0_attn_b_Wq, L0_attn_b_bq, L0_attn_b_Wk, L0_attn_b_bk, L0_attn_b_Wv, L0_attn_b_bv, L0_attn_b_Wo, L0_attn_b_bo)
    x = x + _L0_ffn_ref(_layernorm(x, axis=-1), L0_ffn_lut, L0_ffn_gate_idx, L0_ffn_up_idx, L0_ffn_down_idx)
    return x

_drawn_inputs = setup_inputs


def setup_inputs(seed=0):
    import zlib

    import numpy as np

    out = dict(_drawn_inputs(seed))
    spreads = {'L0_attn_a_conv_b': (0.0, 0.1),
     'L0_attn_a_b_dt': (0.0, 0.333),
     'L0_attn_a_D': (1.0, 0.2),
     'L0_attn_b_bq': (0.0, 0.8),
     'L0_attn_b_bk': (0.0, 0.8),
     'L0_attn_b_bv': (0.0, 0.1),
     'L0_attn_b_bo': (0.0, 0.1)}
    factors = {'L0_attn_b_Wq': 8.0, 'L0_attn_b_Wk': 8.0}
    for name, (base, spread) in spreads.items():
        noise = np.random.default_rng([zlib.crc32(name.encode()), seed]).standard_normal(out[name].shape)
        drawn = base * np.exp(spread * noise) if base else spread * noise
        out[name] = jnp.asarray(drawn.astype(out[name].dtype))
    for name, factor in factors.items():
        out[name] = (out[name] * factor).astype(out[name].dtype)
    return out
```

```python
from contextlib import ExitStack

import numpy as np

import concourse.bass as bass
from concourse import mybir

ALU = mybir.AluOpType
ACT = mybir.ActivationFunctionType
F32 = mybir.dt.float32
F32R = mybir.dt.float32r
BF16 = mybir.dt.bfloat16
I32 = mybir.dt.int32
AX_X = mybir.AxisListType.X

P = 128
BANK = 512
SLAB = 256
EPS = 1e-5
MASKED = -2e38


class SbufPlan:

    def __init__(self, nc, start, end):
        self.nc, self.at, self.end = nc, start, end

    def tile(self, name, shape, dtype=F32):
        size = {F32: 4, F32R: 4, I32: 4, BF16: 2}[dtype]
        for n in shape[1:]:
            size *= n
        t = self.nc.alloc_sbuf_tensor_at(name, list(shape), dtype, offset=self.at)
        self.at += (size + 31) // 32 * 32
        assert self.at <= self.end, (name, self.at, self.end)
        return t

    def pair(self, name, shape):
        return self.tile(name + "_hi", shape, F32R), self.tile(name + "_lo", shape, F32R)


def hybrid_block(
    nc, x, W_in, conv_w, conv_b, W_x, W_dt, b_dt, A_log, D, W_out,
    Wq, bq, Wk, bk, Wv, bv, Wo, bo, lut, gate_idx_T, up_idx_T, down_idx_T, out,
):
    TOK, DM = x.shape
    DI = conv_b.shape[0]
    NS = A_log.shape[1]
    R = W_dt.shape[0]
    HD = Wq.shape[1]
    DH = P
    NH = HD // DH
    INTER = gate_idx_T.shape[1]
    NLUT = lut.shape[0]
    NT = TOK // P
    KD = DM // P
    CT = DI // P
    NB = TOK // BANK
    FM = (INTER + P - 1) // P
    FREM = INTER - (FM - 1) * P
    NP = NH // 2
    SCALE = float(1.0 / np.sqrt(np.float32(DH)))
    assert R == P and NT == 8 and KD == 2 and CT == 4 and NB == 2 and NS == 16 and NLUT == 16
    MW = [min(P, INTER - m * P) for m in range(FM)]

    with ExitStack() as ctx:
        sem = lambda name: ctx.enter_context(nc.semaphore(name))
        psum = ctx.enter_context(nc.psum_tensor("psum", [P, 8, BANK], F32))

        base = (nc.sbuf_base + 31) // 32 * 32
        top = nc.sbuf_usable_end // 32 * 32
        keep = SbufPlan(nc, base, top)
        ident = keep.tile("ident", [P, P])
        ident_r = keep.tile("ident_r", [P, P], F32R)
        ident_b = keep.tile("ident_b", [P, P], BF16)
        causal = SbufPlan(nc, top - 4 * P, top).tile("causal", [P, P])
        causal_b = keep.tile("causal_b", [P, P], BF16)
        half_neg = keep.tile("half_neg", [P, NT])
        ones_col = keep.tile("ones_col", [P, 1])
        stats = keep.tile("stats", [P, NT, 6])
        mean_var = keep.tile("mean_var", [P, NT, 2])
        var_eps = keep.tile("var_eps", [P, NT])
        rstd = keep.tile("rstd", [P, NT])
        convw = keep.tile("convw", [P, CT, 3])
        convw_half = keep.tile("convw_half", [P, CT, 3])
        convb = keep.tile("convb", [P, CT])
        convb_half = keep.tile("convb_half", [P, CT])
        bdt = keep.tile("bdt", [P, CT])
        dskip = keep.tile("dskip", [P, CT])
        alog = keep.tile("alog", [P, CT, NS])
        aneg = keep.tile("aneg", [P, CT, NS])
        bq_t = keep.tile("bq_t", [P, NH])
        bk_t = keep.tile("bk_t", [P, NH])
        bv_t = keep.tile("bv_t", [P, NH])
        bo_row = keep.tile("bo_row", [P, DM])
        lut_row = keep.tile("lut_row", [P, NLUT])
        lut_step = keep.tile("lut_step", [P, NLUT // 2])
        res = keep.tile("res", [P, NT, DM])
        xn_at = keep.at
        xn = keep.tile("xn", [P, NT, DM])
        xnT = keep.pair("xnT", [P, KD, TOK])

        def cursor(at, end=top):
            return SbufPlan(nc, at, end)

        mp = cursor(keep.at)
        wx = mp.pair("wx", [P, CT, R + 2 * NS])
        wdt = mp.pair("wdt", [P, DI])
        wout = mp.pair("wout", [P, CT, DM])
        xc = mp.tile("xc", [P, CT, TOK])
        inner_hi_t = mp.tile("inner_hi", [P, CT, TOK], F32R)
        raws = mp.at
        inner = (inner_hi_t, mp.tile("inner_lo", [P, CT, TOK], F32R))
        rp = cursor(raws, mp.at)
        wx_raw = rp.tile("wx_raw", [P, CT, R + 2 * NS])
        wdt_raw = rp.tile("wdt_raw", [P, DI])
        wout_raw = rp.tile("wout_raw", [P, CT, DM])
        building = mp.at
        sz2 = mp.tile("sz2", [P, CT, TOK])
        dt = mp.tile("dt", [P, CT, TOK])
        dtu = mp.tile("dtu", [P, CT, TOK])
        bp = cursor(building, mp.at)
        idx_t = [bp.tile(f"idx{i}", [P, INTER], I32) for i in range(2)]
        bit0, bit1, bit2, bit3 = (bp.tile(f"bit{i}", [P, INTER], I32) for i in range(4))
        pick = [bp.tile(f"pick{i}", [P, INTER]) for i in range(NLUT // 2)]
        whi, wlo = bp.pair("built", [P, INTER])
        bct = mp.pair("bct", [2 * NS, TOK])
        shared = mp.at
        pre = cursor(shared)
        win_raw = pre.tile("win_raw", [P, KD, 2 * DI])
        win = pre.pair("win", [P, KD, 2 * DI])
        taps = [pre.tile(f"taps{i}", [P, TOK]) for i in range(2)]
        tanh_xz = [pre.tile(f"tanh_xz{i}", [P, TOK]) for i in range(2)]
        assert pre.at <= top - 4 * P
        dtin = win
        softp = taps
        sp = cursor(shared)
        b_row = [sp.tile(f"b_row{i}", [P, TOK]) for i in range(2)]
        c_row = [sp.tile(f"c_row{i}", [P, TOK]) for i in range(2)]
        decay = [sp.tile(f"decay{i}", [P, TOK]) for i in range(2)]
        drive = [sp.tile(f"drive{i}", [P, TOK]) for i in range(2)]
        state = [sp.tile(f"state{i}", [P, TOK]) for i in range(3)]

        late = top - 4 * (KD * 2 * INTER + FM * DM) * 2 - 256
        late = min(late, top - 4 * NH * TOK // 2 - 4 * KD * BANK - 64) // 32 * 32
        assert late >= shared
        fw = cursor(late)
        wgu = fw.pair("wgu", [P, KD, 2 * INTER])
        wdn = fw.pair("wdn", [P, FM, DM])
        fp = cursor(keep.at, late)
        hid = [fp.pair(f"hid{i}", [P, FM, BANK]) for i in range(2)]
        f_tanh = [fp.tile(f"f_tanh{i}", [P, BANK]) for i in range(2)]
        f_gate = [fp.tile(f"f_gate{i}", [P, BANK]) for i in range(2)]
        f_prod = [fp.tile(f"f_prod{i}", [P, BANK]) for i in range(2)]

        HALF = TOK // 2
        lp = cursor(late)
        qT = lp.tile("qT", [P, NH, HALF])
        wq_raw = lp.tile("wq_raw", [P, KD, BANK])
        ap_ = cursor(keep.at, late)
        kT = [ap_.pair(f"kT{i}", [P, TOK]) for i in range(2)]
        v2 = [ap_.pair(f"v2{i}", [P, NT, 2 * DH]) for i in range(2)]
        q = [ap_.pair(f"q{i}", [P, TOK]) for i in range(2)]
        w_raw = ap_.tile("w_raw", [P, KD, 2 * DH])
        wk = ap_.pair("wk", [P, KD, 2 * DH])
        wv = ap_.pair("wv", [P, KD, 2 * DH])
        wo = ap_.pair("wo", [P, 2, DM])
        probs = [ap_.tile(f"probs{i}", [P, TOK]) for i in range(2)]
        pT = ap_.pair("pT", [P, NT, SLAB])
        oT = [ap_.pair(f"oT{i}", [P, 2, TOK]) for i in range(2)]
        neg_max, row_sum, row_inv = (ap_.tile(n, [P, NH, NT]) for n in ("neg_max", "row_sum", "row_inv"))
        wqp = cursor(xn_at, xn_at + 4 * NT * DM)
        wq = wqp.pair("wq", [P, KD, BANK])

        wgu_dram = [nc.dram_tensor(f"wgu_dram{i}", [P, KD, 2 * INTER], F32, kind="Internal").ap() for i in range(2)]
        wdn_dram = [nc.dram_tensor(f"wdn_dram{i}", [P, FM, DM], F32, kind="Internal").ap() for i in range(2)]

        ld = {n: sem("ld_" + n) for n in (
            "x", "win", "small", "lut", "bias", "wx", "wdt", "wout", "idx0", "idx1",
            "wffn", "w", "wq")}
        consts_made = sem("consts_made")
        ones_made = sem("ones_made")
        consts_cast = sem("consts_cast")
        out_stored = sem("out_stored")
        spilled = sem("spilled")
        dve_own = sem("dve_own")
        act_own = sem("act_own")
        pool_own = sem("pool_own")
        ln_stats, ln_mv, ln_rstd, ln_xn, ln_turned, ln_hi, ln_lo = (
            sem(n) for n in ("ln_stats", "ln_mv", "ln_rstd", "ln_xn", "ln_turned", "ln_hi", "ln_lo"))
        win_hi, win_lo = sem("win_hi"), sem("win_lo")
        mw_hi, mw_lo = sem("mw_hi"), sem("mw_lo")
        bits_done, pick_filled, weight_picked, weight_hi, weight_lo = (
            sem(n) for n in ("bits_done", "pick_filled", "weight_picked", "weight_hi", "weight_lo"))
        small_done = sem("small_done")
        (xz_made, tap_mid, conv_done, tanh_done, gated, xc_hi, xc_lo, xd_made, xd_hi, xd_lo, dtp_made,
         softp_done, relu_done, dt_done, dtu_done, row_made, row_copied, decay_done, drive_done, scanned,
         weighed, y_added, y_read, inner_f, inner_hi, inner_lo, op_made, res1) = (
            sem(n) for n in (
                "xz_made", "tap_mid", "conv_done", "tanh_done", "gated", "xc_hi", "xc_lo", "xd_made", "xd_hi",
                "xd_lo", "dtp_made", "softp_done", "relu_done", "dt_done", "dtu_done", "row_made", "row_copied",
                "decay_done", "drive_done", "scanned", "weighed", "y_added", "y_read", "inner_f", "inner_hi",
                "inner_lo", "op_made", "res1"))
        gu_made, f_tanhed, f_gated, f_mult, hid_hi, hid_lo, dn_made, f_res = (
            sem(n) for n in ("gu_made", "f_tanhed", "f_gated", "f_mult", "hid_hi", "hid_lo", "dn_made", "f_res"))
        (wq_split, w_split, q_hi, q_split, unit_made, unit_hi, unit_done, scored, max_done, exp_done, inv_done,
         normed, turned, pT_hi, pT_lo, pv_made, oT_hi, oT_lo, bo_added) = (
            sem(n) for n in (
                "wq_split", "w_split", "q_hi", "q_split", "unit_made", "unit_hi", "unit_done", "scored",
                "max_done", "exp_done", "inv_done", "normed", "turned", "pT_hi", "pT_lo", "pv_made", "oT_hi",
                "oT_lo", "bo_added"))

        x_t = x.rearrange("(t p) c -> p t c", p=P)
        out_t = out.rearrange("(t p) c -> p t c", p=P)

        f32 = lambda t: t.bitcast(F32)

        def product(e, acc, pairs, first=True, last=True):
            n = len(pairs)
            for i, ((wh, wl), (mh, ml)) in enumerate(pairs):
                e.matmul(acc, wh, mh, start=first and i == 0, stop=False)
                e.matmul(acc, wh, ml, start=False, stop=False)
                mm = e.matmul(acc, wl, mh, start=False, stop=last and i == n - 1)
            return mm

        def cut(pair, *ix):
            return tuple(t[ix] for t in pair)

        def split_hi_pool(e, hi, src):
            return e.tensor_scalar(hi, src, 1.0, 0.0, ALU.mult, ALU.add)

        def split_lo(e, lo, src, hi):
            return e.tensor_tensor(lo, src, f32(hi), ALU.subtract)

        builds = []
        for kt in range(KD):
            for g, src in enumerate((gate_idx_T, up_idx_T)):
                builds.append((wgu_dram, (slice(None), kt, slice(g * INTER, (g + 1) * INTER)),
                               src[kt * P:(kt + 1) * P, :], P, INTER))
        for m in range(FM):
            builds.append((wdn_dram, (slice(0, MW[m]), m, slice(None)), down_idx_T[m * P:m * P + MW[m], :], MW[m], DM))
        NBUILD = len(builds)

        block = ctx.enter_context(nc.Block())

        def step_units(n):
            h, i = divmod(n, NT)
            r, st = h // 2, (h % 2) * NT + i
            units = []
            if r >= 1 and st < NT and st % 2:
                units.append(("O", r - 1, st // 2))
            if i in (0, 2) and h + 1 < NH:
                units.append(("K", h + 1, i // 2))
            if st >= NT and st % 2 and r + 1 < NP:
                units.append(("V", r + 1, (st - NT) // 2))
            if h == NH // 2 - 2 and i >= NT - 4:
                units += [("Q", 1, 4 * (i - (NT - 4)) + c) for c in range(4)]
            return units

        first_units = [("Q", 0, c) for c in range(NH)]
        first_units += [("K", 0, s) for s in range(NB)] + [("V", 0, t) for t in range(NT // 2)]
        last_units = [("O", NP - 1, t) for t in range(NT // 2)]
        all_units = list(first_units)
        units_at = {}
        for n in range(NH * NT):
            units_at[n] = step_units(n)
            all_units += units_at[n]
        all_units += last_units
        unit_no = {u: k for k, u in enumerate(all_units)}
        hi_no = {u: k for k, u in enumerate(u for u in all_units if u[0] in "KV")}
        wq_chunk = lambda u: u[1] * 4 + u[2] // 4

        def unit_bank(k):
            middle = len(first_units) <= k < len(all_units) - len(last_units)
            return 7 if middle else 4 + k % 4

        def bank_free(k):
            return max((j + 1 for j in range(k) if unit_bank(j) == unit_bank(k)), default=0)

        def groups(i):
            return [(b, min(b + 4, i + 1)) for b in range(0, i + 1, 4)]

        def turned_before(n):
            h, i = divmod(n, NT)
            return 12 * h + (i if i <= 4 else 4 + 2 * (i - 4))

        split_order = [("wk", 0), ("wv", 0)]
        for r in range(NP):
            if r + 1 < NP:
                split_order += [("wk", r + 1), ("wv", r + 1)]
            split_order.append(("wo", r))
        split_no = {k: 2 * n + 2 for n, k in enumerate(split_order)}

        def load_ffn_weights(e):
            for i in range(2):
                e.dma_start(f32(wgu[i][:]), wgu_dram[i]).then_inc(ld["wffn"], 16)
                e.dma_start(f32(wdn[i][:, 0:FM - 1]), wdn_dram[i][:, 0:FM - 1]).then_inc(ld["wffn"], 16)
                e.dma_start(f32(wdn[i][0:FREM, FM - 1]), wdn_dram[i][0:FREM, FM - 1]).then_inc(ld["wffn"], 16)

        def load_wq(e, k):
            if k >= 1:
                e.wait_ge(wq_split, 2 * k)
            e.dma_start(wq_raw[:], Wq[:, (k % 4) * BANK:(k % 4 + 1) * BANK].rearrange(
                "(k p) n -> p k n", p=P)).then_inc(ld["wq"], 16)

        def load_w(e, n):
            name, r = split_order[n]
            if n >= 1:
                e.wait_ge(w_split, 2 * n)
            cols = slice(r * 2 * DH, (r + 1) * 2 * DH)
            src = Wo[cols, :] if name == "wo" else (Wk if name == "wk" else Wv)[:, cols]
            e.dma_start(w_raw[:], src.rearrange("(k p) n -> p k n", p=P)).then_inc(ld["w"], 16)

        @block.sync
        def _(e):
            e.dma_start(res[:], x_t).then_inc(ld["x"], 16)
            e.dma_start(win_raw[:], W_in.rearrange("(k p) n -> p k n", p=P)).then_inc(ld["win"], 16)
            e.dma_start(convw[:], conv_w.rearrange("(c p) o k -> p c (o k)", p=P)).then_inc(ld["small"], 16)
            with nc.allow_non_contiguous_dma(reason="small vectors"):
                for t, v in ((convb, conv_b), (bdt, b_dt), (dskip, D)):
                    e.dma_start(t[:], v.rearrange("(c p) -> p c", p=P)).then_inc(ld["small"], 16)
                e.dma_start(alog[:], A_log.rearrange("(c p) s -> p c s", p=P)).then_inc(ld["small"], 16)
                e.dma_start(lut_row[:], lut.rearrange("(o n) -> o n", o=1).broadcast_to([P, NLUT])).then_inc(ld["lut"], 16)
                e.dma_start(wx_raw[:], W_x.rearrange("(c p) n -> p c n", p=P)).then_inc(ld["wx"], 16)
                e.dma_start(wdt_raw[:], W_dt).then_inc(ld["wdt"], 16)
                e.dma_start(wout_raw[:], W_out.rearrange("(c p) n -> p c n", p=P)).then_inc(ld["wout"], 16)
                for t, v in ((bq_t, bq), (bk_t, bk), (bv_t, bv)):
                    e.dma_start(t[:], v.rearrange("(c p) -> p c", p=P)).then_inc(ld["bias"], 16)
                e.dma_start(bo_row[:], bo.rearrange("(o n) -> o n", o=1).broadcast_to([P, DM])).then_inc(ld["bias"], 16)
            for b in range(NBUILD + 2):
                if b < NBUILD:
                    _, _, src, parts, cols = builds[b]
                    if b >= 2:
                        e.wait_ge(bits_done, 4 * (b - 1))
                    e.dma_start(idx_t[b % 2][0:parts, 0:cols], src).then_inc(ld[f"idx{b % 2}"], 16)
                if b >= 2:
                    dram, where, _, parts, cols = builds[b - 2]
                    e.wait_ge(weight_lo, b - 1)
                    for i, t in enumerate((whi, wlo)):
                        e.dma_start(dram[i][where], f32(t[0:parts, 0:cols])).then_inc(spilled, 16)
            e.wait_ge(spilled, 32 * NBUILD)
            e.wait_ge(y_added, 4 * NS)
            load_ffn_weights(e)
            e.wait_ge(f_res, NT)
            load_wq(e, 0)
            load_w(e, 0)
            for k in range(1, 4):
                load_wq(e, k)
                if k == 1:
                    load_w(e, 1)
            before_wq = 3 * 3 + 2
            for n in range(2, before_wq):
                load_w(e, n)
            load_wq(e, 4)
            load_w(e, before_wq)
            load_wq(e, 5)
            load_wq(e, 6)
            load_w(e, before_wq + 1)
            load_wq(e, 7)
            for n in range(before_wq + 2, len(split_order)):
                load_w(e, n)
            e.wait_ge(q_split, 4 * NH)
            load_ffn_weights(e)
            for i in range(NT):
                e.wait_ge(f_res, NT + i + 1)
                e.dma_start(out_t[:, i], res[:, i]).then_inc(out_stored, 16)
            e.wait_ge(out_stored, 16 * NT)

        def pe_layer_norm(e, L):
            e.wait_ge(consts_made, 2)
            for g in range(NT // 2):
                e.wait_ge(ln_xn, NT * L + 2 * g + 2)
                if g >= 2:
                    e.wait_ge(ln_lo, 4 * L + g - 1)
                for t in range(2):
                    for k in range(KD):
                        mm = e.transpose(psum[:, 6 + g % 2, (2 * t + k) * P:(2 * t + k + 1) * P],
                                         xn[:, 2 * g + t, k * P:(k + 1) * P], ident[:])
                mm.then_inc(ln_turned, 1)

        def pe_mamba(e):
            slot = lambda n: 2 * (n % 3)
            e.wait_ge(win_hi, 1)
            e.wait_ge(win_lo, 1)
            e.wait_ge(ln_lo, NT // 2)
            for m in range(2 * CT):
                if 3 <= m < 3 + CT:
                    e.wait_ge(conv_done, m - 2)
                if m >= 3 + CT:
                    e.wait_ge(gated, m - 2)
                for n in range(NB):
                    mm = product(e, psum[:, slot(m) + n], [
                        (cut(win, slice(None), k, slice(m * P, (m + 1) * P)),
                         cut(xnT, slice(None), k, slice(n * BANK, (n + 1) * BANK))) for k in range(KD)])
                mm.then_inc(xz_made, 1)
            e.wait_ge(mw_hi, 2)
            e.wait_ge(mw_lo, 2)
            for m, (a, b) in enumerate(((0, R), (R, R + 2 * NS))):
                if m == 0:
                    e.wait_ge(gated, 2 * CT - 2)
                    e.wait_ge(xc_lo, CT)
                else:
                    e.wait_ge(gated, 2 * CT - 1)
                for n in range(NB):
                    mm = product(e, psum[0:b - a, slot(2 * CT + m) + n], [
                        (cut(wx, slice(None), c, slice(a, b)),
                         cut(inner, slice(None), c, slice(n * BANK, (n + 1) * BANK))) for c in range(CT)])
                mm.then_inc(xd_made, 1)
            for c in range(CT):
                e.wait_ge(xd_lo, 1)
                if c == 0:
                    e.wait_ge(gated, 2 * CT)
                elif c <= 2:
                    e.wait_ge(xd_lo, c)
                else:
                    e.wait_ge(relu_done, 1)
                    e.wait_ge(softp_done, 1)
                for n in range(NB):
                    mm = product(e, psum[:, slot(2 * CT + 2 + c) + n], [
                        (cut(wdt, slice(None), slice(c * P, (c + 1) * P)),
                         dtin_cut(n))])
                mm.then_inc(dtp_made, 1)

            def rows(s):
                for w in range(2):
                    b = 2 * s + w
                    if b == 0:
                        e.wait_ge(relu_done, CT)
                        e.wait_ge(softp_done, CT)
                        e.wait_ge(xd_lo, 2)
                    if b >= 2:
                        e.wait_ge(row_copied, b - 1)
                    col = w * NS + s % NS
                    for n in range(NB):
                        for part in range(2):
                            mm = e.matmul(psum[:, 4 + 2 * (b % 2) + n],
                                          ident_r[0:2 * NS, col:col + 1].broadcast_to([2 * NS, P]),
                                          bct[part][:, n * BANK:(n + 1) * BANK],
                                          start=part == 0, stop=part == 1)
                    mm.then_inc(row_made, 1)

            e.wait_ge(consts_cast, 3)
            rows(0)
            for s in range(2 * NS):
                if s + 1 < 2 * NS:
                    rows(s + 1)
                for c in range(2):
                    j = 2 * s + c
                    e.wait_ge(weighed, j + 1)
                    if s == NS:
                        e.wait_ge(y_read, c + 1)
                    for n in range(NB):
                        mm = e.matmul(psum[:, 2 * c + n], ident[:], state[j % 3][:, n * BANK:(n + 1) * BANK],
                                      start=s % NS == 0, stop=s % NS == NS - 1)
                    mm.then_inc(y_added, 1)
            e.wait_ge(mw_hi, 3)
            e.wait_ge(mw_lo, 3)
            e.wait_ge(inner_lo, CT)
            for i in range(NT):
                if i >= 4:
                    e.wait_ge(res1, i - 3)
                mm = product(e, psum[:, 4 + i % 4, 0:DM], [
                    (cut(inner, slice(None), c, slice(i * P, (i + 1) * P)), cut(wout, slice(None), c, slice(None)))
                    for c in range(CT)])
                mm.then_inc(op_made, 1)

        def dtin_cut(n):
            return tuple(t[:, 0, n * BANK:(n + 1) * BANK] for t in dtin)

        def pe_ffn(e, f):
            Q = 2 * FM

            def gate_up(k):
                n, m = divmod(k, FM)
                if k >= 3:
                    e.wait_ge(f_mult, Q * f + k - 2)
                for g in range(2):
                    mm = product(e, psum[0:MW[m], 2 * (k % 3) + g], [
                        (cut(wgu, slice(None), kt, slice(g * INTER + m * P, g * INTER + m * P + MW[m])),
                         cut(xnT, slice(None), kt, slice(n * BANK, (n + 1) * BANK))) for kt in range(KD)])
                mm.then_inc(gu_made, 1)

            def down(i):
                n = i // 4
                e.wait_ge(hid_lo, Q * f + (n + 1) * FM)
                if i >= 2:
                    e.wait_ge(f_res, NT * f + i - 1)
                mm = product(e, psum[:, 6 + i % 2, 0:DM], [
                    (cut(hid[n], slice(0, MW[m]), m, slice((i % 4) * P, (i % 4 + 1) * P)),
                     cut(wdn, slice(0, MW[m]), m, slice(None))) for m in range(FM)])
                mm.then_inc(dn_made, 1)

            e.wait_ge(ld["wffn"], 96 * (f + 1))
            e.wait_ge(ln_lo, 4 * (2 * f + 2))
            for k in range(FM + 2):
                gate_up(k)
            for i in range(4):
                down(i)
            for k in range(FM + 2, Q):
                gate_up(k)
            for i in range(4, NT):
                down(i)

        def pe_attention(e):
            def unit(u):
                kind, a, b = u
                k = unit_no[u]
                acc = psum[:, unit_bank(k)]
                if bank_free(k):
                    e.wait_ge(unit_done, bank_free(k))
                if kind == "Q":
                    e.wait_ge(wq_split, 2 * (wq_chunk(u) + 1))
                    mm = product(e, acc, [
                        (cut(wq, slice(None), kt, slice((b % 4) * P, (b % 4 + 1) * P)),
                         cut(xnT, slice(None), kt, slice(a * HALF, (a + 1) * HALF))) for kt in range(KD)])
                elif kind == "K":
                    e.wait_ge(w_split, split_no[("wk", a // 2)])
                    mm = product(e, acc, [
                        (cut(wk, slice(None), kt, slice((a % 2) * P, (a % 2 + 1) * P)),
                         cut(xnT, slice(None), kt, slice(b * BANK, (b + 1) * BANK))) for kt in range(KD)])
                elif kind == "V":
                    e.wait_ge(w_split, split_no[("wv", a)])
                    for t in range(2):
                        mm = product(e, acc[:, t * SLAB:(t + 1) * SLAB], [
                            (cut(xnT, slice(None), kt, slice((2 * b + t) * P, (2 * b + t + 1) * P)),
                             cut(wv, slice(None), kt, slice(None))) for kt in range(KD)])
                else:
                    e.wait_ge(w_split, split_no[("wo", a)])
                    if b == 0:
                        e.wait_ge(oT_lo, 8 * (a + 1))
                    for t in range(2):
                        mm = product(e, acc[:, t * SLAB:(t + 1) * SLAB], [
                            (cut(oT[a % 2], slice(None), hh, slice((2 * b + t) * P, (2 * b + t + 1) * P)),
                             cut(wo, slice(None), hh, slice(None))) for hh in range(2)])
                mm.then_inc(unit_made, 1)

            def scores(n):
                h, i = divmod(n, NT)
                if n >= 2:
                    e.wait_ge(exp_done, n - 1)
                e.wait_ge(q_split, 4 * h + i // 2 + 1)
                if i == 0:
                    e.wait_ge(unit_done, unit_no[("K", h, NB - 1)] + 1)
                width = (i + 1) * P
                for b in range(0, width, BANK):
                    w = min(BANK, width - b)
                    acc = psum[:, 2 * (n % 2) + b // BANK]
                    diagonal = b + w == width
                    mm = product(e, acc[:, 0:w], [
                        (cut(q[h % 2], slice(None), slice(i * P, (i + 1) * P)),
                         cut(kT[h % 2], slice(None), slice(b, b + w)))], last=not diagonal)
                    if diagonal:
                        mm = e.matmul(acc[:, w - P:w], ident_b[:], causal_b[:], start=False, stop=True)
                mm.then_inc(scored, 1)

            def turn(n):
                h, i = divmod(n, NT)
                e.wait_ge(normed, n + 1)
                if n == 0:
                    e.wait_ge(unit_done, len(first_units))
                for g, (a, b) in enumerate(groups(i)):
                    t = turned_before(n) + g
                    if t >= 2:
                        e.wait_ge(pT_lo, t - 1)
                    for j in range(a, b):
                        mm = e.transpose(psum[:, 4 + t % 2, (j - a) * P:(j - a + 1) * P],
                                         probs[n % 2][:, j * P:(j + 1) * P], ident[:])
                    mm.then_inc(turned, 1)

            def values(n):
                h, i = divmod(n, NT)
                s = n // 2
                e.wait_ge(pT_lo, turned_before(n + 1))
                if i == 1:
                    e.wait_ge(unit_done, unit_no[("V", h // 2, NT // 2 - 1)] + 1)
                if s >= 1:
                    e.wait_ge(oT_lo, s)
                acc = psum[:, 6, 0:SLAB]
                vh = lambda j: cut(v2[h // 2 % 2], slice(None), j, slice((h % 2) * DH, (h % 2 + 1) * DH))
                product(e, acc, [(vh(j), cut(pT, slice(None), j, slice(None))) for j in range(i)], last=False)
                mm = product(e, acc[:, P:SLAB], [(vh(i), cut(pT, slice(None), i, slice(P, SLAB)))], first=False)
                mm.then_inc(pv_made, 1)

            e.wait_ge(ln_lo, 12)
            for u in first_units:
                unit(u)
            scores(0)
            scores(1)
            for n in range(NH * NT):
                turn(n)
                if n + 2 < NH * NT:
                    scores(n + 2)
                for u in units_at[n]:
                    unit(u)
                if n % 2:
                    values(n)
            for u in last_units:
                unit(u)

        @block.tensor
        def _(e):
            pe_layer_norm(e, 0)
            pe_mamba(e)
            pe_layer_norm(e, 1)
            pe_ffn(e, 0)
            pe_layer_norm(e, 2)
            pe_attention(e)
            pe_layer_norm(e, 3)
            pe_ffn(e, 1)

        def turn_views(g):
            src = psum[:, 6 + g % 2].rearrange("p (t k c) -> p t k c", t=2, k=KD)
            dst = [t[:, :, g * 2 * P:(g + 1) * 2 * P].rearrange("p k (t c) -> p t k c", t=2) for t in xnT]
            return src, dst

        def act_layer_norm(e, L):
            for g in range(NT // 2):
                e.wait_ge(ln_turned, 4 * L + g + 1)
                src, dst = turn_views(g)
                nc.scalar.activation(dst[0], src, ACT.Copy).then_inc(ln_hi, 1)

        def act_mamba(e):
            slot = lambda n: 2 * (n % 3)
            two = lambda n: psum[:, slot(n):slot(n) + 2].rearrange("p a b -> p (a b)")

            def tap(m):
                e.wait_ge(xz_made, m + 1)
                if m >= 2:
                    e.wait_ge(gated, m - 1)
                nc.scalar.activation(taps[m % 2][:], two(m), ACT.Identity, bias=convb_half[:, m:m + 1],
                                     scale=convw_half[:, m, 1:2]).then_inc(tap_mid, 1)

            def tanh(m):
                if m >= 2:
                    e.wait_ge(gated, m - 1)
                if m < CT:
                    e.wait_ge(conv_done, m + 1)
                    nc.scalar.activation(tanh_xz[m % 2][:], taps[m % 2][:], ACT.Tanh).then_inc(tanh_done, 1)
                else:
                    e.wait_ge(xz_made, m + 1)
                    nc.scalar.activation(tanh_xz[m % 2][:], two(m), ACT.Tanh, scale=0.5).then_inc(tanh_done, 1)

            def xc_high(m):
                e.wait_ge(gated, m + 1)
                nc.scalar.activation(inner[0][:, m], xc[:, m], ACT.Copy).then_inc(xc_hi, 1)

            e.wait_ge(small_done, 2)
            e.wait_ge(ones_made, 1)
            for m in range(CT):
                tap(m)
                if m >= 1:
                    tanh(m - 1)
                if m >= 2:
                    xc_high(m - 2)
            tanh(CT - 1)
            xc_high(CT - 2)
            for m in range(CT, 2 * CT):
                tanh(m)
                if m == CT:
                    xc_high(CT - 1)
            for m in range(2):
                e.wait_ge(xd_made, m + 1)
                if m == 0:
                    nc.scalar.activation(dtin[0][:, 0, 0:TOK], two(2 * CT), ACT.Copy).then_inc(xd_hi, 1)
                else:
                    nc.scalar.activation(bct[0][:], two(2 * CT + 1)[0:2 * NS], ACT.Copy).then_inc(xd_hi, 1)
            nc.scalar.preload_act_table_set("natural_log_exp_and_others")
            e.wait_ge(gated, 2 * CT)
            own = 0
            nc.scalar.activation(aneg[:], alog[:], ACT.Exp).then_inc(act_own, 1)
            own += 1
            for c in range(CT):
                e.wait_ge(dtp_made, c + 1)
                if c >= 2:
                    e.wait_ge(dt_done, c - 1)
                t = softp[c % 2]
                nc.scalar.activation(t[:], two(2 * CT + 2 + c), ACT.Abs, bias=bdt[:, c:c + 1]).then_inc(act_own, 1)
                own += 1
                e.wait_ge(act_own, own)
                nc.scalar.activation(t[:], t[:], ACT.Exp, scale=-1.0).then_inc(act_own, 1)
                own += 1
                e.wait_ge(act_own, own)
                nc.scalar.activation(t[:], t[:], ACT.Ln, bias=ones_col[:]).then_inc(softp_done, 1)

            def row(b):
                s, w = divmod(b, 2)
                e.wait_ge(row_made, b + 1)
                if s >= 2:
                    e.wait_ge(drive_done if w == 0 else weighed, 2 * (s - 1))
                dst = (b_row, c_row)[w][s % 2]
                nc.scalar.activation(dst[:], psum[:, 4 + 2 * w:6 + 2 * w].rearrange("p a b -> p (a b)"),
                                     ACT.Copy).then_inc(row_copied, 1)

            e.wait_ge(dt_done, CT)
            e.wait_ge(small_done, 3)
            e.wait_ge(xc_lo, CT)
            e.wait_ge(dtu_done, CT)
            row(0)
            row(1)
            for s in range(2 * NS):
                for c in range(2):
                    j, ct = 2 * s + c, 2 * (s // NS) + c
                    if j >= 2:
                        e.wait_ge(scanned, j - 1)
                    nc.scalar.activation(decay[j % 2][:], dt[:, ct], ACT.Exp,
                                         scale=aneg[:, ct, s % NS:s % NS + 1]).then_inc(decay_done, 1)
                if s + 1 < 2 * NS:
                    row(2 * s + 2)
                    row(2 * s + 3)
                if s in (NS + 1, 2 * NS - 1):
                    for c in range(2):
                        ct = 2 * (s // (NS + 2)) + c
                        e.wait_ge(inner_f, ct + 1)
                        nc.scalar.activation(inner[0][:, ct], dtu[:, ct], ACT.Copy).then_inc(inner_hi, 1)

        def act_ffn(e, f):
            Q = 2 * FM
            for k in range(Q):
                n, m = divmod(k, FM)
                w = MW[m]
                e.wait_ge(gu_made, Q * f + k + 1)
                if k >= 2:
                    e.wait_ge(f_gated, Q * f + k - 1)
                nc.scalar.activation(f_tanh[k % 2][0:w], psum[0:w, 2 * (k % 3)], ACT.Tanh,
                                     scale=0.5).then_inc(f_tanhed, 1)
                if k >= 1:
                    hid_high(e, f, k - 1)
            hid_high(e, f, Q - 1)

        def hid_high(e, f, k):
            n, m = divmod(k, FM)
            e.wait_ge(f_mult, 2 * FM * f + k + 1)
            nc.scalar.activation(hid[n][0][0:MW[m], m], f_prod[k % 2][0:MW[m]], ACT.Copy,
                                 scale=0.5).then_inc(hid_hi, 1)

        def unit_target(u, part):
            kind, a, b = u
            if kind == "K":
                return kT[a % 2][part][:, b * BANK:(b + 1) * BANK]
            return v2[a % 2][part][:, 2 * b:2 * b + 2].rearrange("p t c -> p (t c)")

        def act_attention(e):
            def unit(u):
                kind, a, b = u
                if kind not in "KV":
                    return
                k = unit_no[u]
                e.wait_ge(unit_made, k + 1)
                acc = psum[:, unit_bank(k)]
                if kind == "K":
                    nc.scalar.activation(unit_target(u, 0), acc, ACT.Identity,
                                         bias=bk_t[:, a:a + 1]).then_inc(unit_hi, 1)
                else:
                    nc.scalar.activation(unit_target(u, 0), acc, ACT.Copy).then_inc(unit_hi, 1)

            def exp(n):
                h, i = divmod(n, NT)
                e.wait_ge(max_done, n + 1)
                if n >= 2:
                    e.wait_ge(turned, turned_before(n - 1))
                nc.scalar.activation(probs[n % 2][:, 0:(i + 1) * P],
                                     psum[:, 2 * (n % 2):2 * (n % 2) + 2].rearrange("p a b -> p (a b)")[:, 0:(i + 1) * P],
                                     ACT.Exp, bias=neg_max[:, h, i:i + 1],
                                     accum_out=row_sum[:, h, i:i + 1]).then_inc(exp_done, 1)

            def turned_hi(n):
                h, i = divmod(n, NT)
                for g, (a, b) in enumerate(groups(i)):
                    t = turned_before(n) + g
                    e.wait_ge(turned, t + 1)
                    dst, src = turned_views(n, t, a, b)
                    nc.scalar.activation(dst[0], src, ACT.Copy).then_inc(pT_hi, 1)

            def value_hi(n):
                s = n // 2
                e.wait_ge(pv_made, s + 1)
                dst, src = value_views(s)
                nc.scalar.activation(dst[0], src, ACT.Identity,
                                     bias=bv_t[:, n // NT:n // NT + 1]).then_inc(oT_hi, 1)

            e.wait_ge(ld["bias"], 64)
            for u in first_units:
                unit(u)
            exp(0)
            exp(1)
            for n in range(NH * NT):
                turned_hi(n)
                if n + 2 < NH * NT:
                    exp(n + 2)
                for u in units_at[n]:
                    unit(u)
                if n % 2:
                    value_hi(n)

        def turned_views(n, t, a, b):
            c = (n % 2) * P
            dst = [p[:, a:b, c:c + P] for p in pT]
            src = psum[:, 4 + t % 2, 0:(b - a) * P].rearrange("p (j c) -> p j c", c=P)
            return dst, src

        def value_views(s):
            h, g = divmod(s, NT // 2)
            dst = [t[:, h % 2, g * SLAB:(g + 1) * SLAB] for t in oT[h // 2 % 2]]
            return dst, psum[:, 6, 0:SLAB]

        @block.scalar
        def _(e):
            e.wait_ge(ld["win"], 16)
            nc.scalar.activation(win[0][:], win_raw[:], ACT.Copy).then_inc(win_hi, 1)
            act_layer_norm(e, 0)
            e.wait_ge(ld["wx"], 16)
            nc.scalar.activation(wx[0][:], wx_raw[:], ACT.Copy).then_inc(mw_hi, 1)
            e.wait_ge(ld["wdt"], 16)
            nc.scalar.activation(wdt[0][:], wdt_raw[:], ACT.Copy).then_inc(mw_hi, 1)
            e.wait_ge(ld["wout"], 16)
            nc.scalar.activation(wout[0][:], wout_raw[:], ACT.Copy).then_inc(mw_hi, 1)
            act_mamba(e)
            act_layer_norm(e, 1)
            e.wait_ge(ld["wffn"], 96)
            act_ffn(e, 0)
            act_layer_norm(e, 2)
            act_attention(e)
            act_layer_norm(e, 3)
            act_ffn(e, 1)

        def dve_layer_norm(e, L, ready):
            for i in range(NT):
                s, v = ready(i)
                e.wait_ge(s, v)
                nc.vector.bn_stats(stats[:, i], res[:, i]).then_inc(ln_stats, 1)
                if i >= 1:
                    e.wait_ge(ln_stats, NT * L + i)
                    nc.vector.bn_aggr(mean_var[:, i - 1], stats[:, i - 1]).then_inc(ln_mv, 1)
            e.wait_ge(ln_stats, NT * (L + 1))
            nc.vector.bn_aggr(mean_var[:, NT - 1], stats[:, NT - 1]).then_inc(ln_mv, 1)
            e.wait_ge(ln_rstd, L + 1)
            for i in range(NT):
                nc.vector.tensor_scalar(xn[:, i], res[:, i], mean_var[:, i, 0:1], rstd[:, i:i + 1],
                                        ALU.subtract, ALU.mult).then_inc(ln_xn, 1)
            for g in range(NT // 2):
                e.wait_ge(ln_hi, 4 * L + g + 1)
                src, dst = turn_views(g)
                nc.vector.tensor_tensor(dst[1], src, f32(dst[0]), ALU.subtract).then_inc(ln_lo, 1)

        def dve_build(e, b):
            dram, where, src, parts, cols = builds[b]
            a = lambda t: t[0:parts, 0:cols]
            e.wait_ge(ld[f"idx{b % 2}"], 16 * (b // 2 + 1))
            if b >= 1:
                e.wait_ge(weight_picked, 7 * b)
                e.wait_ge(pick_filled, 8 * b)
            for k, t in enumerate((bit0, bit1, bit2, bit3)):
                nc.vector.tensor_single_scalar(a(t), a(idx_t[b % 2]), 1 << k, ALU.bitwise_and).then_inc(bits_done, 1)
            e.wait_ge(pick_filled, 8 * (b + 1))
            e.wait_ge(bits_done, 4 * (b + 1))
            for k in range(4):
                nc.vector.copy_predicated(a(pick[2 * k]), a(bit1), a(pick[2 * k + 1])).then_inc(weight_picked, 1)
            e.wait_ge(weight_picked, 7 * b + 4)
            for k in range(2):
                nc.vector.copy_predicated(a(pick[4 * k]), a(bit2), a(pick[4 * k + 2])).then_inc(weight_picked, 1)
            e.wait_ge(weight_picked, 7 * b + 6)
            nc.vector.copy_predicated(a(pick[0]), a(bit3), a(pick[4])).then_inc(weight_picked, 1)

        def dve_mamba(e):
            slot = lambda n: 2 * (n % 3)
            two = lambda n: psum[:, slot(n):slot(n) + 2].rearrange("p a b -> p (a b)")

            def conv(m):
                t = taps[m % 2]
                e.wait_ge(tap_mid, m + 1)
                nc.vector.scalar_tensor_tensor(out=t[:, 1:TOK], in0=two(m)[:, 0:TOK - 1], scalar=convw_half[:, m, 0:1],
                                               in1=t[:, 1:TOK], op0=ALU.mult, op1=ALU.add).then_inc(dve_own, 1)
                own[0] += 1
                e.wait_ge(dve_own, own[0])
                nc.vector.scalar_tensor_tensor(out=t[:, 0:TOK - 1], in0=two(m)[:, 1:TOK], scalar=convw_half[:, m, 2:3],
                                               in1=t[:, 0:TOK - 1], op0=ALU.mult, op1=ALU.add).then_inc(conv_done, 1)

            def gate(m):
                e.wait_ge(tanh_done, m + 1)
                src = taps[m % 2][:] if m < CT else two(m)
                dst = xc[:, m] if m < CT else sz2[:, m - CT]
                nc.vector.scalar_tensor_tensor(out=dst, in0=tanh_xz[m % 2][:], scalar=1.0, in1=src,
                                               op0=ALU.add, op1=ALU.mult).then_inc(gated, 1)

            for m in range(CT):
                conv(m)
                if m >= 1:
                    gate(m - 1)
            gate(CT - 1)
            e.wait_ge(spilled, 32 * NBUILD)
            for m in range(CT, 2 * CT):
                gate(m)
            for m in range(2):
                e.wait_ge(xd_hi, m + 1)
                if m == 0:
                    nc.vector.tensor_tensor(dtin[1][:, 0, 0:TOK], two(2 * CT), f32(dtin[0][:, 0, 0:TOK]),
                                            ALU.subtract).then_inc(xd_lo, 1)
                else:
                    nc.vector.tensor_tensor(bct[1][:], two(2 * CT + 1)[0:2 * NS], f32(bct[0][:]),
                                            ALU.subtract).then_inc(xd_lo, 1)
            for c in range(CT):
                e.wait_ge(dtp_made, c + 1)
                e.wait_ge(act_own, 2 * c + 2)
                nc.vector.tensor_scalar(dt[:, c], two(2 * CT + 2 + c), bdt[:, c:c + 1], 0.0,
                                        ALU.add, ALU.max).then_inc(relu_done, 1)
                e.wait_ge(softp_done, c + 1)
                e.wait_ge(relu_done, c + 1)
                nc.vector.tensor_tensor(dt[:, c], dt[:, c], softp[c % 2][:], ALU.add).then_inc(dt_done, 1)
            e.wait_ge(act_own, 1)
            nc.vector.tensor_scalar(aneg[:], aneg[:], -1.0, None, ALU.mult).then_inc(small_done, 1)

            def scan(j):
                e.wait_ge(decay_done, j + 1)
                e.wait_ge(drive_done, j + 1)
                if j >= 3:
                    e.wait_ge(y_added, j - 2)
                nc.vector.tensor_tensor_scan(state[j % 3][:], decay[j % 2][:], drive[j % 2][:], 0.0,
                                             ALU.mult, ALU.add).then_inc(scanned, 1)

            def weigh(j):
                e.wait_ge(scanned, j + 1)
                e.wait_ge(row_copied, 2 * (j // 2) + 2)
                nc.vector.tensor_tensor(state[j % 3][:], state[j % 3][:], c_row[j // 2 % 2][:],
                                        ALU.mult).then_inc(weighed, 1)

            def finish(c):
                e.wait_ge(y_added, 32 * (c // 2) + 31 + c % 2)
                y = psum[:, 2 * (c % 2):2 * (c % 2) + 2].rearrange("p a b -> p (a b)")
                e.wait_ge(drive_done, 32 * (c // 2 + 1))
                nc.vector.scalar_tensor_tensor(out=dtu[:, c], in0=xc[:, c], scalar=dskip[:, c:c + 1], in1=y,
                                               op0=ALU.mult, op1=ALU.add).then_inc(y_read, 1)
                e.wait_ge(y_read, c + 1)
                nc.vector.scalar_tensor_tensor(out=dtu[:, c], in0=dtu[:, c], scalar=0.5, in1=sz2[:, c],
                                               op0=ALU.mult, op1=ALU.mult).then_inc(inner_f, 1)

            for cp in range(2):
                for k in range(2 * NS):
                    scan(32 * cp + k)
                    if k >= 1:
                        weigh(32 * cp + k - 1)
                weigh(32 * cp + 2 * NS - 1)
                finish(2 * cp)
                finish(2 * cp + 1)
            for i in range(NT):
                e.wait_ge(op_made, i + 1)
                nc.vector.tensor_tensor(res[:, i], res[:, i], psum[:, 4 + i % 4, 0:DM], ALU.add).then_inc(res1, 1)

        own = [0]

        def dve_ffn(e, f):
            Q = 2 * FM

            def down(i):
                e.wait_ge(dn_made, NT * f + i + 1)
                nc.vector.tensor_tensor(res[:, i], res[:, i], psum[:, 6 + i % 2, 0:DM], ALU.add).then_inc(f_res, 1)

            for k in range(Q):
                n, m = divmod(k, FM)
                w = MW[m]
                e.wait_ge(f_tanhed, Q * f + k + 1)
                if k >= 2:
                    e.wait_ge(f_mult, Q * f + k - 1)
                nc.vector.scalar_tensor_tensor(out=f_gate[k % 2][0:w], in0=f_tanh[k % 2][0:w], scalar=1.0,
                                               in1=psum[0:w, 2 * (k % 3)], op0=ALU.add,
                                               op1=ALU.mult).then_inc(f_gated, 1)
                e.wait_ge(f_gated, Q * f + k + 1)
                if k >= 2:
                    e.wait_ge(hid_lo, Q * f + k - 1)
                nc.vector.tensor_tensor(f_prod[k % 2][0:w], f_gate[k % 2][0:w], psum[0:w, 2 * (k % 3) + 1],
                                        ALU.mult).then_inc(f_mult, 1)
                if k >= 1:
                    hid_low(e, f, k - 1)
                if k == FM + 1:
                    for i in range(4):
                        down(i)
            hid_low(e, f, Q - 1)
            for i in range(4, NT):
                down(i)

        def hid_low(e, f, k):
            n, m = divmod(k, FM)
            w = MW[m]
            e.wait_ge(hid_hi, 2 * FM * f + k + 1)
            nc.vector.scalar_tensor_tensor(out=hid[n][1][0:w, m], in0=f_prod[k % 2][0:w], scalar=0.5,
                                           in1=f32(hid[n][0][0:w, m]), op0=ALU.mult,
                                           op1=ALU.subtract).then_inc(hid_lo, 1)

        def dve_attention(e):
            def unit(u):
                kind, a, b = u
                k = unit_no[u]
                acc = psum[:, unit_bank(k)]
                if kind == "Q":
                    e.wait_ge(unit_made, k + 1)
                    if a == 1:
                        e.wait_ge(q_split, 4 * (NH // 2))
                    nc.vector.tensor_scalar(qT[:, b], acc, bq_t[:, b:b + 1], SCALE,
                                            ALU.add, ALU.mult).then_inc(unit_done, 1)
                elif kind == "O":
                    e.wait_ge(unit_made, k + 1)
                    if a == 0:
                        e.wait_ge(bo_added, NT)
                    else:
                        e.wait_ge(unit_done, unit_no[("O", a - 1, b)] + 1)
                    both = res[:, 2 * b:2 * b + 2].rearrange("p t c -> p (t c)")
                    nc.vector.tensor_tensor(both, both, acc, ALU.add).then_inc(unit_done, 1)
                else:
                    e.wait_ge(unit_hi, hi_no[u] + 1)
                    hi = f32(unit_target(u, 0))
                    if kind == "K":
                        nc.vector.scalar_tensor_tensor(out=unit_target(u, 1), in0=acc, scalar=bk_t[:, a:a + 1],
                                                       in1=hi, op0=ALU.add, op1=ALU.subtract).then_inc(unit_done, 1)
                    else:
                        nc.vector.tensor_tensor(unit_target(u, 1), acc, hi, ALU.subtract).then_inc(unit_done, 1)

            def row_max(n):
                h, i = divmod(n, NT)
                e.wait_ge(scored, n + 1)
                nc.vector.tensor_reduce(neg_max[:, h, i:i + 1],
                                        psum[:, 2 * (n % 2):2 * (n % 2) + 2].rearrange("p a b -> p (a b)")[:, 0:(i + 1) * P],
                                        AX_X, ALU.max, negate=True).then_inc(max_done, 1)

            def inverse(n):
                h, i = divmod(n, NT)
                e.wait_ge(exp_done, n + 1)
                nc.vector.reciprocal(row_inv[:, h, i:i + 1], row_sum[:, h, i:i + 1]).then_inc(inv_done, 1)

            def turned_lo(n):
                h, i = divmod(n, NT)
                for g, (a, b) in enumerate(groups(i)):
                    t = turned_before(n) + g
                    e.wait_ge(pT_hi, t + 1)
                    dst, src = turned_views(n, t, a, b)
                    nc.vector.tensor_tensor(dst[1], src, f32(dst[0]), ALU.subtract).then_inc(pT_lo, 1)

            def value_lo(n):
                s = n // 2
                e.wait_ge(oT_hi, s + 1)
                dst, src = value_views(s)
                nc.vector.scalar_tensor_tensor(out=dst[1], in0=src, scalar=bv_t[:, n // NT:n // NT + 1],
                                               in1=f32(dst[0]), op0=ALU.add, op1=ALU.subtract).then_inc(oT_lo, 1)

            e.wait_ge(ld["bias"], 64)
            for i in range(NT):
                nc.vector.tensor_tensor(res[:, i], res[:, i], bo_row[:], ALU.add).then_inc(bo_added, 1)
            for u in first_units:
                unit(u)
            for n in range(2):
                row_max(n)
            for n in range(2):
                inverse(n)
            for n in range(NH * NT):
                turned_lo(n)
                if n + 2 < NH * NT:
                    row_max(n + 2)
                for u in units_at[n]:
                    unit(u)
                if n + 2 < NH * NT:
                    inverse(n + 2)
                if n % 2:
                    value_lo(n)
            for u in last_units:
                unit(u)

        @block.vector
        def _(e):
            nc.vector.memset(ones_col[:], 1.0).then_inc(ones_made, 1)
            e.wait_ge(ld["lut"], 16)
            pairs = lut_row[:].rearrange("p (a b) -> p a b", b=2)
            nc.vector.tensor_tensor(lut_step[:], pairs[:, :, 1], pairs[:, :, 0], ALU.subtract).then_inc(small_done, 1)
            dve_layer_norm(e, 0, lambda i: (ld["x"], 16))
            e.wait_ge(ld["small"], 80)
            nc.vector.tensor_scalar(convw_half[:], convw[:], 0.5, None, ALU.mult).then_inc(dve_own, 1)
            own[0] += 1
            nc.vector.tensor_scalar(convb_half[:], convb[:], 0.5, None, ALU.mult).then_inc(small_done, 1)
            e.wait_ge(consts_made, 3)
            nc.vector.tensor_copy(ident_r[:], ident[:]).then_inc(consts_cast, 1)
            nc.vector.tensor_copy(ident_b[:], ident[:]).then_inc(consts_cast, 1)
            nc.vector.tensor_copy(causal_b[:], causal[:]).then_inc(consts_cast, 1)
            for b in range(NBUILD):
                dve_build(e, b)
            dve_mamba(e)
            dve_layer_norm(e, 1, lambda i: (res1, i + 1))
            dve_ffn(e, 0)
            dve_layer_norm(e, 2, lambda i: (f_res, i + 1))
            dve_attention(e)
            dve_layer_norm(e, 3, lambda i: (unit_done, unit_no[("O", NP - 1, i // 2)] + 1))
            dve_ffn(e, 1)

        def pool_layer_norm(e, L):
            e.wait_ge(consts_made, 3)
            e.wait_ge(ln_mv, NT * (L + 1))
            nc.gpsimd.tensor_scalar(var_eps[:], mean_var[:, :, 1], 1.0, EPS, ALU.mult, ALU.add).then_inc(pool_own, 1)
            pown[0] += 1
            e.wait_ge(pool_own, pown[0])
            nc.gpsimd.tensor_tensor(rstd[:], var_eps[:], half_neg[:], ALU.pow).then_inc(ln_rstd, 1)

        pown = [0]

        def pool_lo(e, lo, src, hi, s):
            split_lo(nc.gpsimd, lo, src, hi).then_inc(s, 1)

        def pool_attention(e):
            def split(name, r):
                pair = {"wk": wk, "wv": wv, "wo": wo}[name]
                e.wait_ge(ld["w"], 8 * split_no[(name, r)])
                if r >= 1:
                    last = {"wk": ("K", 2 * r - 1, NB - 1), "wv": ("V", r - 1, NT // 2 - 1),
                            "wo": ("O", r - 1, NT // 2 - 1)}[name]
                    e.wait_ge(unit_made, unit_no[last] + 1)
                split_hi_pool(nc.gpsimd, pair[0][:], w_raw[:]).then_inc(w_split, 1)
                e.wait_ge(w_split, split_no[(name, r)] - 1)
                split_lo(nc.gpsimd, pair[1][:], w_raw[:], pair[0][:]).then_inc(w_split, 1)

            def split_wq(k):
                e.wait_ge(ld["wq"], 16 * (k + 1))
                if k >= 1:
                    last = ("Q", (k - 1) // 4, 4 * ((k - 1) % 4) + 3)
                    e.wait_ge(unit_made, unit_no[last] + 1)
                split_hi_pool(nc.gpsimd, wq[0][:], wq_raw[:]).then_inc(wq_split, 1)
                e.wait_ge(wq_split, 2 * k + 1)
                split_lo(nc.gpsimd, wq[1][:], wq_raw[:], wq[0][:]).then_inc(wq_split, 1)

            def q_piece(h, pc):
                npc = TOK // SLAB
                if h >= 2:
                    e.wait_ge(scored, NT * (h - 1))
                tok = SLAB // NH
                t0 = (h % (NH // 2)) * (TOK // NH) + pc * tok
                c_last = unit_no[("Q", h // (NH // 2), NH - 1)]
                if pc == 0:
                    e.wait_ge(unit_done, c_last + 1)
                src = qT[:, :, t0:t0 + tok].rearrange("p c t -> p t c")
                hi, lo = (t[:, pc * SLAB:(pc + 1) * SLAB].rearrange("p (t c) -> p t c", c=NH) for t in q[h % 2])
                split_hi_pool(nc.gpsimd, hi, src).then_inc(q_hi, 1)
                e.wait_ge(q_hi, npc * h + pc + 1)
                split_lo(nc.gpsimd, lo, src, hi).then_inc(q_split, 1)

            def norm(n):
                h, i = divmod(n, NT)
                e.wait_ge(inv_done, n + 1)
                pr = probs[n % 2][:, 0:(i + 1) * P]
                nc.gpsimd.tensor_scalar(pr, pr, row_inv[:, h, i:i + 1], 0.0, ALU.mult, ALU.add).then_inc(normed, 1)

            e.wait_ge(ln_turned, 12)
            for k in range(4):
                split_wq(k)
                if k == 0:
                    split("wk", 0)
                    split("wv", 0)
            for pc in range(TOK // SLAB):
                q_piece(0, pc)
            norm(0)
            norm(1)
            for n in range(NH * NT):
                h, i = divmod(n, NT)
                r, st = h // 2, (h % 2) * NT + i
                if i < TOK // SLAB and h + 1 < NH:
                    q_piece(h + 1, i)
                if st == 5 and r + 1 < NP:
                    split("wk", r + 1)
                if st == 6 and r + 1 < NP:
                    split("wv", r + 1)
                if st == 10:
                    split("wo", r)
                if h == NH // 2 - 2 and i >= 3 and i < 7:
                    split_wq(4 + i - 3)
                if n + 2 < NH * NT:
                    norm(n + 2)

        @block.gpsimd
        def _(e):
            nc.gpsimd.memset(ident[:], 0.0).then_inc(pool_own, 1)
            nc.gpsimd.memset(causal[:], 0.0).then_inc(pool_own, 1)
            nc.gpsimd.memset(half_neg[:], -0.5).then_inc(consts_made, 1)
            e.wait_ge(pool_own, 2)
            pown[0] += 2
            nc.gpsimd.affine_select(out=ident[:], in_=ident[:], compare_op=ALU.not_equal, fill=1.0, base=0,
                                    pattern=[[-1, P]], channel_multiplier=1).then_inc(consts_made, 1)
            nc.gpsimd.affine_select(out=causal[:], in_=causal[:], compare_op=ALU.is_ge, fill=MASKED, base=0,
                                    pattern=[[-1, P]], channel_multiplier=1).then_inc(consts_made, 1)
            pool_layer_norm(e, 0)
            e.wait_ge(win_hi, 1)
            pool_lo(e, win[1][:], win_raw[:], win[0][:], win_lo)
            for k, (w, raw) in enumerate(((wx, wx_raw[:]), (wdt, wdt_raw[:]), (wout, wout_raw[:]))):
                e.wait_ge(mw_hi, k + 1)
                pool_lo(e, w[1][:], raw, w[0][:], mw_lo)
            e.wait_ge(small_done, 1)
            for b in range(NBUILD):
                dram, where, src, parts, cols = builds[b]
                a = lambda t: t[0:parts, 0:cols]
                e.wait_ge(bits_done, 4 * b + 1)
                if b >= 1:
                    e.wait_ge(weight_picked, 7 * b)
                    e.wait_ge(weight_lo, b)
                for k in range(8):
                    nc.gpsimd.tensor_scalar(a(pick[k]), a(bit0), lut_step[0:parts, k:k + 1],
                                            lut_row[0:parts, 2 * k:2 * k + 1], ALU.mult, ALU.add).then_inc(pick_filled, 1)
                e.wait_ge(weight_picked, 7 * (b + 1))
                if b >= 1:
                    e.wait_ge(spilled, 32 * b)
                split_hi_pool(nc.gpsimd, a(whi), a(pick[0])).then_inc(weight_hi, 1)
                e.wait_ge(weight_hi, b + 1)
                split_lo(nc.gpsimd, a(wlo), a(pick[0]), a(whi)).then_inc(weight_lo, 1)
            e.wait_ge(mw_lo, 3)
            for m in range(CT):
                e.wait_ge(xc_hi, m + 1)
                pool_lo(e, inner[1][:, m], xc[:, m], inner[0][:, m], xc_lo)
            e.wait_ge(spilled, 32 * NBUILD)
            for c in range(CT):
                e.wait_ge(dt_done, c + 1)
                nc.gpsimd.tensor_tensor(dtu[:, c], dt[:, c], xc[:, c], ALU.mult).then_inc(dtu_done, 1)
            e.wait_ge(dtu_done, CT)
            for s in range(2 * NS):
                e.wait_ge(row_copied, 2 * s + 1)
                for c in range(2):
                    j, ct = 2 * s + c, 2 * (s // NS) + c
                    if j >= 2:
                        e.wait_ge(scanned, j - 1)
                    nc.gpsimd.tensor_tensor(drive[j % 2][:], dtu[:, ct], b_row[s % 2][:], ALU.mult).then_inc(drive_done, 1)
                if s in (NS + 1, 2 * NS - 1):
                    for c in range(2):
                        ct = 2 * (s // (NS + 2)) + c
                        e.wait_ge(inner_hi, ct + 1)
                        pool_lo(e, inner[1][:, ct], dtu[:, ct], inner[0][:, ct], inner_lo)
            pool_layer_norm(e, 1)
            pool_layer_norm(e, 2)
            e.wait_ge(f_res, NT)
            pool_attention(e)
            pool_layer_norm(e, 3)


INPUTS = [
    "L0_attn_a_x", "L0_attn_a_W_in", "L0_attn_a_conv_w", "L0_attn_a_conv_b", "L0_attn_a_W_x", "L0_attn_a_W_dt",
    "L0_attn_a_b_dt", "L0_attn_a_A_log", "L0_attn_a_D", "L0_attn_a_W_out", "L0_attn_b_Wq", "L0_attn_b_bq",
    "L0_attn_b_Wk", "L0_attn_b_bk", "L0_attn_b_Wv", "L0_attn_b_bv", "L0_attn_b_Wo", "L0_attn_b_bo",
    "L0_ffn_lut", "L0_ffn_gate_idx", "L0_ffn_up_idx", "L0_ffn_down_idx",
]


def kernel(**inputs):
    import concourse.bacc as bacc
    from concourse.bass_utils import run_bass_kernel_spmd

    nc = bacc.Bacc("TRN2", target_bir_lowering=False, num_devices=1)
    arrays, args = {}, []
    for name in INPUTS:
        a = np.asarray(inputs[name])
        shape = a.shape
        if name == "L0_attn_a_x":
            a = a.reshape(shape[-2:])
        if name.endswith("_idx"):
            a = a.T
        a = np.ascontiguousarray(a)
        arrays["in_" + name] = a
        args.append(nc.dram_tensor("in_" + name, list(a.shape), mybir.dt.from_np(a.dtype), kind="ExternalInput").ap())
    x_shape = np.asarray(inputs["L0_attn_a_x"]).shape
    out = nc.dram_tensor("out_x", list(x_shape[-2:]), F32, kind="ExternalOutput").ap()
    hybrid_block(nc, *args, out)
    got = run_bass_kernel_spmd(nc, [arrays], core_ids=[0])
    return got.results[0]["out_x"].reshape(x_shape)
```

```python
from contextlib import ExitStack

import numpy as np

import concourse.bass as bass
from concourse import mybir

ALU = mybir.AluOpType
ACT = mybir.ActivationFunctionType
F32 = mybir.dt.float32
F32R = mybir.dt.float32r
BF16 = mybir.dt.bfloat16
I32 = mybir.dt.int32
AX_X = mybir.AxisListType.X

P = 128
BANK = 512
SLAB = 256
EPS = 1e-5
MASKED = -2e38


class SbufPlan:

    def __init__(self, nc, start, end):
        self.nc, self.at, self.end = nc, start, end

    def tile(self, name, shape, dtype=F32):
        size = {F32: 4, F32R: 4, I32: 4, BF16: 2}[dtype]
        for n in shape[1:]:
            size *= n
        t = self.nc.alloc_sbuf_tensor_at(name, list(shape), dtype, offset=self.at)
        self.at += (size + 31) // 32 * 32
        assert self.at <= self.end, (name, self.at, self.end)
        return t

    def pair(self, name, shape):
        return self.tile(name + "_hi", shape, F32R), self.tile(name + "_lo", shape, F32R)


def hybrid_block(
    nc, x, W_in, conv_w, conv_b, W_x, W_dt, b_dt, A_log, D, W_out,
    Wq, bq, Wk, bk, Wv, bv, Wo, bo, lut, gate_idx_T, up_idx_T, down_idx_T, out,
):
    TOK, DM = x.shape
    DI = conv_b.shape[0]
    NS = A_log.shape[1]
    R = W_dt.shape[0]
    HD = Wq.shape[1]
    DH = P
    NH = HD // DH
    INTER = gate_idx_T.shape[1]
    NLUT = lut.shape[0]
    NT = TOK // P
    KD = DM // P
    CT = DI // P
    NB = TOK // BANK
    FM = (INTER + P - 1) // P
    FREM = INTER - (FM - 1) * P
    NP = NH // 2
    SCALE = float(1.0 / np.sqrt(np.float32(DH)))
    assert R == P and NT == 8 and KD == 2 and CT == 4 and NB == 2 and NS == 16 and NLUT == 16
    MW = [min(P, INTER - m * P) for m in range(FM)]

    with ExitStack() as ctx:
        sem = lambda name: ctx.enter_context(nc.semaphore(name))
        psum = ctx.enter_context(nc.psum_tensor("psum", [P, 8, BANK], F32))

        base = (nc.sbuf_base + 31) // 32 * 32
        top = nc.sbuf_usable_end // 32 * 32
        keep = SbufPlan(nc, base, top)
        ident = keep.tile("ident", [P, P])
        ident_r = keep.tile("ident_r", [P, P], F32R)
        ident_b = keep.tile("ident_b", [P, P], BF16)
        causal = SbufPlan(nc, top - 4 * P, top).tile("causal", [P, P])
        causal_b = keep.tile("causal_b", [P, P], BF16)
        half_neg = keep.tile("half_neg", [P, NT])
        ones_col = keep.tile("ones_col", [P, 1])
        stats = keep.tile("stats", [P, NT, 6])
        mean_var = keep.tile("mean_var", [P, NT, 2])
        var_eps = keep.tile("var_eps", [P, NT])
        rstd = keep.tile("rstd", [P, NT])
        convw = keep.tile("convw", [P, CT, 3])
        convw_half = keep.tile("convw_half", [P, CT, 3])
        convb = keep.tile("convb", [P, CT])
        convb_half = keep.tile("convb_half", [P, CT])
        bdt = keep.tile("bdt", [P, CT])
        dskip = keep.tile("dskip", [P, CT])
        alog = keep.tile("alog", [P, CT, NS])
        aneg = keep.tile("aneg", [P, CT, NS])
        bq_t = keep.tile("bq_t", [P, NH])
        bk_t = keep.tile("bk_t", [P, NH])
        bv_t = keep.tile("bv_t", [P, NH])
        bo_row = keep.tile("bo_row", [P, DM])
        lut_row = keep.tile("lut_row", [P, NLUT])
        lut_step = keep.tile("lut_step", [P, NLUT // 2])
        res = keep.tile("res", [P, NT, DM])
        xn_at = keep.at
        xn = keep.tile("xn", [P, NT, DM])
        xnT_at = keep.at
        xnT = keep.pair("xnT", [P, KD, TOK])

        def cursor(at, end=top):
            return SbufPlan(nc, at, end)

        mp = cursor(keep.at)
        wx = mp.pair("wx", [P, CT, R + 2 * NS])
        wdt = mp.pair("wdt", [P, DI])
        wout = mp.pair("wout", [P, CT, DM])
        xc = mp.tile("xc", [P, CT, TOK])
        inner_hi_t = mp.tile("inner_hi", [P, CT, TOK], F32R)
        raws = mp.at
        inner = (inner_hi_t, mp.tile("inner_lo", [P, CT, TOK], F32R))
        rp = cursor(raws, mp.at)
        wx_raw = rp.tile("wx_raw", [P, CT, R + 2 * NS])
        wdt_raw = rp.tile("wdt_raw", [P, DI])
        wout_raw = rp.tile("wout_raw", [P, CT, DM])
        building = mp.at
        sz2 = mp.tile("sz2", [P, CT, TOK])
        dt = mp.tile("dt", [P, CT, TOK])
        dtu = mp.tile("dtu", [P, CT, TOK])
        bp = cursor(building, mp.at)
        BW = INTER // 2
        idx_t = [bp.tile(f"idx{i}", [P, BW], I32) for i in range(2)]
        bits = [[bp.tile(f"bit{k}_{i}", [P, BW], I32) for k in range(4)] for i in range(2)]
        pick = [[bp.tile(f"pick{k}_{i}", [P, BW]) for k in range(NLUT // 2)] for i in range(2)]
        built = [bp.pair(f"built{i}", [P, BW]) for i in range(2)]
        bct = mp.pair("bct", [2 * NS, TOK])
        shared = mp.at
        pre = cursor(shared)
        win_raw = pre.tile("win_raw", [P, KD, 2 * DI])
        win = pre.pair("win", [P, KD, 2 * DI])
        taps = [pre.tile(f"taps{i}", [P, TOK]) for i in range(2)]
        tanh_xz = [pre.tile(f"tanh_xz{i}", [P, TOK]) for i in range(2)]
        assert pre.at <= top - 4 * P
        dtin = win
        softp = taps
        sp = cursor(shared)
        xn_rows = [xn[:, i * NT // 2:(i + 1) * NT // 2].rearrange("p t c -> p (t c)") for i in range(2)]
        tp = cursor(xnT_at, keep.at)
        xnT_rows = [tp.tile(f"xnT_row{i}", [P, TOK])[:] for i in range(2 * KD)]
        b_row = [sp.tile(f"b_row{i}", [P, TOK])[:] for i in range(2)] + [xn_rows[0]]
        c_row = [sp.tile(f"c_row{i}", [P, TOK])[:] for i in range(2)] + [xn_rows[1]]
        decay = [sp.tile(f"decay{i}", [P, TOK])[:] for i in range(2)] + [xnT_rows[0]]
        drive = [sp.tile(f"drive{i}", [P, TOK])[:] for i in range(2)] + [xnT_rows[1]]
        state = [sp.tile(f"state{i}", [P, TOK])[:] for i in range(3)] + [xnT_rows[2]]

        late = (top - 4 * (KD * 2 * INTER + FM * DM) * 2 - 64) // 32 * 32
        assert late >= shared
        fw = cursor(late)
        wgu = fw.pair("wgu", [P, KD, 2 * INTER])
        wdn = fw.pair("wdn", [P, FM, DM])
        fp = cursor(keep.at, late)
        hid = [fp.pair(f"hid{i}", [P, FM, BANK]) for i in range(2)]
        f_tanh = [fp.tile(f"f_tanh{i}", [P, BANK]) for i in range(2)]
        f_gate = [fp.tile(f"f_gate{i}", [P, BANK]) for i in range(2)]
        f_prod = [fp.tile(f"f_prod{i}", [P, BANK]) for i in range(2)]

        HALF = TOK // 2
        HTOK = TOK // NH
        HH = HALF // HTOK
        ap_ = cursor(keep.at, late)
        kT = [ap_.pair(f"kT{i}", [P, TOK]) for i in range(2)]
        v2 = [ap_.pair(f"v2{i}", [P, NT, 2 * DH]) for i in range(2)]
        probs = [ap_.tile(f"probs{i}", [P, TOK]) for i in range(2)]
        neg_max, row_sum, row_inv = (ap_.tile(n, [P, NH, NT]) for n in ("neg_max", "row_sum", "row_inv"))
        ap_.at = max(ap_.at, fp.at)
        w_raw = ap_.tile("w_raw", [P, KD, 2 * DH])
        wk = ap_.pair("wk", [P, KD, 2 * DH])
        wv = ap_.pair("wv", [P, KD, 2 * DH])
        wo = ap_.pair("wo", [P, 2, DM])
        first = ap_.at
        q = [ap_.pair(f"q{i}", [P, TOK]) for i in range(2)]
        pT = ap_.pair("pT", [P, NT, SLAB])
        qstage0 = cursor(first, ap_.at).tile("qstage0", [P, HH, NH, HTOK])
        first = ap_.at
        oT = [ap_.pair(f"oT{i}", [P, 2, TOK]) for i in range(2)]
        wqp = cursor(first, ap_.at)
        wq_raw = wqp.tile("wq_raw", [P, KD, BANK])
        wq = [wqp.pair(f"wq{i}", [P, KD, BANK]) for i in range(2)]
        qstage = [qstage0, cursor(late).tile("qstage1", [P, HH, NH, HTOK])]
        q_raw = [xn[:, i * NT // 2:(i + 1) * NT // 2].rearrange("p t c -> p (t c)").rearrange(
            "p (c t) -> p c t", c=NH) for i in range(2)]

        wgu_dram = [nc.dram_tensor(f"wgu_dram{i}", [P, KD, 2 * INTER], F32, kind="Internal").ap() for i in range(2)]
        wdn_dram = [nc.dram_tensor(f"wdn_dram{i}", [P, FM, DM], F32, kind="Internal").ap() for i in range(2)]

        q_dram = nc.dram_tensor("q_dram", [NH, P, NH * HTOK], F32, kind="Internal").ap()

        ld = {n: sem("ld_" + n) for n in (
            "x", "win", "small", "lut", "bias", "wx", "wdt", "wout", "idx0", "idx1",
            "wffn", "w", "wq", "q0", "q1")}
        q_stored = sem("q_stored")
        consts_made = sem("consts_made")
        ones_made = sem("ones_made")
        consts_cast = sem("consts_cast")
        out_stored = sem("out_stored")
        spilled = [sem(f"spilled{i}") for i in range(2)]
        dve_own = sem("dve_own")
        act_own = sem("act_own")
        pool_own = sem("pool_own")
        ln_stats, ln_mv, ln_rstd, ln_xn, ln_turned, ln_hi, ln_lo = (
            sem(n) for n in ("ln_stats", "ln_mv", "ln_rstd", "ln_xn", "ln_turned", "ln_hi", "ln_lo"))
        win_hi, win_lo = sem("win_hi"), sem("win_lo")
        mw_hi, mw_lo = sem("mw_hi"), sem("mw_lo")
        bits_done, act_picks, pool_picks, weight_picked, weight_hi, weight_lo = (
            sem(n) for n in ("bits_done", "act_picks", "pool_picks", "weight_picked", "weight_hi", "weight_lo"))
        small_done = sem("small_done")
        (xz_made, tap_mid, conv_done, tanh_done, gated, xc_hi, xc_lo, xd_made, xd_hi, xd_lo, dtp_made,
         softp_done, relu_done, dt_done, dtu_done, row_made, row_copied, decay_done, drive_done, scanned,
         weighed, y_added, y_read, inner_f, inner_hi, inner_lo, op_made, res1) = (
            sem(n) for n in (
                "xz_made", "tap_mid", "conv_done", "tanh_done", "gated", "xc_hi", "xc_lo", "xd_made", "xd_hi",
                "xd_lo", "dtp_made", "softp_done", "relu_done", "dt_done", "dtu_done", "row_made", "row_copied",
                "decay_done", "drive_done", "scanned", "weighed", "y_added", "y_read", "inner_f", "inner_hi",
                "inner_lo", "op_made", "res1"))
        gu_made, f_tanhed, f_gated, f_mult, hid_hi, hid_lo, dn_made, f_res = (
            sem(n) for n in ("gu_made", "f_tanhed", "f_gated", "f_mult", "hid_hi", "hid_lo", "dn_made", "f_res"))
        (wq_split, w_split, q_hi, q_split, unit_made, unit_hi, unit_done, scored, max_done, exp_done, inv_done,
         normed, turned, pT_hi, pT_lo, pv_made, oT_hi, oT_lo, bo_added) = (
            sem(n) for n in (
                "wq_split", "w_split", "q_hi", "q_split", "unit_made", "unit_hi", "unit_done", "scored",
                "max_done", "exp_done", "inv_done", "normed", "turned", "pT_hi", "pT_lo", "pv_made", "oT_hi",
                "oT_lo", "bo_added"))

        x_t = x.rearrange("(t p) c -> p t c", p=P)
        out_t = out.rearrange("(t p) c -> p t c", p=P)

        f32 = lambda t: t.bitcast(F32)

        def product(e, acc, pairs, first=True, last=True):
            n = len(pairs)
            for i, ((wh, wl), (mh, ml)) in enumerate(pairs):
                e.matmul(acc, wh, mh, start=first and i == 0, stop=False)
                e.matmul(acc, wh, ml, start=False, stop=False)
                mm = e.matmul(acc, wl, mh, start=False, stop=last and i == n - 1)
            return mm

        def cut(pair, *ix):
            return tuple(t[ix] for t in pair)

        def split_hi_pool(e, hi, src):
            return e.tensor_scalar(hi, src, 1.0, 0.0, ALU.mult, ALU.add)

        def split_lo(e, lo, src, hi):
            return e.tensor_tensor(lo, src, f32(hi), ALU.subtract)

        builds = []
        for kt in range(KD):
            for g, src in enumerate((gate_idx_T, up_idx_T)):
                for c in range(0, INTER, BW):
                    builds.append((wgu_dram, (slice(None), kt, slice(g * INTER + c, g * INTER + c + BW)),
                                   src[kt * P:(kt + 1) * P, c:c + BW], P, BW))
        for m in range(FM):
            builds.append((wdn_dram, (slice(0, MW[m]), m, slice(None)), down_idx_T[m * P:m * P + MW[m], :], MW[m], DM))
        NBUILD = len(builds)
        PICKS = NLUT // 2
        ACT_PICKS = 3

        block = ctx.enter_context(nc.Block())

        def all_spilled(e):
            for i in range(2):
                e.wait_ge(spilled[i], 32 * ((NBUILD + 1 - i) // 2))

        def step_units(n):
            h, i = divmod(n, NT)
            r, st = h // 2, (h % 2) * NT + i
            units = []
            if i in (0, 1) and h + 1 < NH:
                units.append(("K", h + 1, i))
            for t in {2: (0,), 4: (1,), 6: (2, 3)}.get(i, ()):
                if st < NT and r >= 1:
                    units.append(("O", r - 1, t))
                if st >= NT and r + 1 < NP:
                    units.append(("V", r + 1, t))
            return units

        first_units = [("Q", a, c) for a in range(2) for c in range(NH)]
        first_units += [("K", 0, s) for s in range(NB)] + [("V", 0, t) for t in range(NT // 2)]
        last_units = [("O", NP - 1, t) for t in range(NT // 2)]
        all_units = list(first_units)
        units_at = {}
        for n in range(NH * NT):
            units_at[n] = step_units(n)
            all_units += units_at[n]
        all_units += last_units
        unit_no = {u: k for k, u in enumerate(all_units)}
        hi_no = {u: k for k, u in enumerate(u for u in all_units if u[0] in "KV")}
        wq_chunk = lambda u: u[1] * 4 + u[2] // 4

        def unit_bank(k):
            if k < 2 * NH:
                return k % 6
            middle = len(first_units) <= k < len(all_units) - len(last_units)
            return 7 if middle else 4 + k % 4

        def bank_free(k):
            return max((j + 1 for j in range(k) if unit_bank(j) == unit_bank(k)), default=0)

        def groups(i):
            return [(b, min(b + 4, i + 1)) for b in range(0, i + 1, 4)]

        def turned_before(n):
            h, i = divmod(n, NT)
            return 12 * h + (i if i <= 4 else 4 + 2 * (i - 4))

        split_order = [("wk", 0), ("wv", 0)] + [(w, r + (w != "wo")) for r in range(NP) for w in ("wk", "wv", "wo")
                                                if r + (w != "wo") < NP]
        split_no = {k: 2 * n + 2 for n, k in enumerate(split_order)}

        def load_ffn_weights(e):
            for i in range(2):
                e.dma_start(f32(wgu[i][:]), wgu_dram[i]).then_inc(ld["wffn"], 16)
                e.dma_start(f32(wdn[i][:, 0:FM - 1]), wdn_dram[i][:, 0:FM - 1]).then_inc(ld["wffn"], 16)
                e.dma_start(f32(wdn[i][0:FREM, FM - 1]), wdn_dram[i][0:FREM, FM - 1]).then_inc(ld["wffn"], 16)

        def load_wq(e, k):
            if k >= 1:
                e.wait_ge(wq_split, 2 * k)
            e.dma_start(wq_raw[:], Wq[:, (k % 4) * BANK:(k % 4 + 1) * BANK].rearrange(
                "(k p) n -> p k n", p=P)).then_inc(ld["wq"], 16)

        def store_q(e, half):
            e.wait_ge(unit_done, unit_no[("Q", half, NH - 1)] + 1)
            e.dma_start(q_dram.rearrange("h p n -> p h n")[:, half * HH:(half + 1) * HH],
                        qstage[half][:].rearrange("p h c t -> p h (c t)")).then_inc(q_stored, 16)

        def load_q(e, h):
            e.wait_ge(q_stored, 16 * (h // HH + 1))
            if h >= 2:
                e.wait_ge(q_split, 4 * (h - 1))
            e.dma_start(q_raw[h % 2].rearrange("p c t -> p (c t)"), q_dram[h]).then_inc(ld[f"q{h % 2}"], 16)

        def load_w(e, n):
            name, r = split_order[n]
            if n >= 1:
                e.wait_ge(w_split, 2 * n)
            cols = slice(r * 2 * DH, (r + 1) * 2 * DH)
            src = Wo[cols, :] if name == "wo" else (Wk if name == "wk" else Wv)[:, cols]
            e.dma_start(w_raw[:], src.rearrange("(k p) n -> p k n", p=P)).then_inc(ld["w"], 16)

        @block.sync
        def _(e):
            e.dma_start(res[:], x_t).then_inc(ld["x"], 16)
            e.dma_start(win_raw[:], W_in.rearrange("(k p) n -> p k n", p=P)).then_inc(ld["win"], 16)
            e.dma_start(convw[:], conv_w.rearrange("(c p) o k -> p c (o k)", p=P)).then_inc(ld["small"], 16)
            with nc.allow_non_contiguous_dma(reason="small vectors"):
                for t, v in ((convb, conv_b), (bdt, b_dt), (dskip, D)):
                    e.dma_start(t[:], v.rearrange("(c p) -> p c", p=P)).then_inc(ld["small"], 16)
                e.dma_start(alog[:], A_log.rearrange("(c p) s -> p c s", p=P)).then_inc(ld["small"], 16)
                e.dma_start(lut_row[:], lut.rearrange("(o n) -> o n", o=1).broadcast_to([P, NLUT])).then_inc(ld["lut"], 16)
                e.dma_start(wx_raw[:], W_x.rearrange("(c p) n -> p c n", p=P)).then_inc(ld["wx"], 16)
                e.dma_start(wdt_raw[:], W_dt).then_inc(ld["wdt"], 16)
                e.dma_start(wout_raw[:], W_out.rearrange("(c p) n -> p c n", p=P)).then_inc(ld["wout"], 16)
                for t, v in ((bq_t, bq), (bk_t, bk), (bv_t, bv)):
                    e.dma_start(t[:], v.rearrange("(c p) -> p c", p=P)).then_inc(ld["bias"], 16)
                e.dma_start(bo_row[:], bo.rearrange("(o n) -> o n", o=1).broadcast_to([P, DM])).then_inc(ld["bias"], 16)
            for b in range(NBUILD + 2):
                if b < NBUILD:
                    _, _, src, parts, cols = builds[b]
                    if b >= 2:
                        e.wait_ge(bits_done, 4 * (b - 1))
                    e.dma_start(idx_t[b % 2][0:parts, 0:cols], src).then_inc(ld[f"idx{b % 2}"], 16)
                if b >= 2:
                    dram, where, _, parts, cols = builds[b - 2]
                    e.wait_ge(weight_lo, b - 1)
                    for i, t in enumerate(built[b % 2]):
                        e.dma_start(dram[i][where], f32(t[0:parts, 0:cols])).then_inc(spilled[b % 2], 16)
            all_spilled(e)
            e.wait_ge(y_added, 4 * NS)
            load_ffn_weights(e)
            e.wait_ge(op_made, NT)
            load_wq(e, 0)
            load_w(e, 0)
            load_wq(e, 1)
            load_w(e, 1)
            for k in range(2, 8):
                load_wq(e, k)
                if k == 6:
                    store_q(e, 0)
            load_w(e, 2)
            load_q(e, 0)
            load_q(e, 1)
            store_q(e, 1)
            load_q(e, 2)
            for n in range(3, len(split_order)):
                load_w(e, n)
                if n % 3 == 0 and 2 * (n // 3) + 1 < NH:
                    load_q(e, 2 * (n // 3) + 1)
                if n % 3 == 2 and 2 * (n // 3) + 2 < NH:
                    load_q(e, 2 * (n // 3) + 2)
            e.wait_ge(q_stored, 32)
            load_ffn_weights(e)
            for i in range(NT):
                e.wait_ge(f_res, NT + i + 1)
                e.dma_start(out_t[:, i], res[:, i]).then_inc(out_stored, 16)
            e.wait_ge(out_stored, 16 * NT)

        def pe_layer_norm(e, L):
            e.wait_ge(consts_made, 2)
            for g in range(NT // 2):
                e.wait_ge(ln_xn, NT * L + 2 * g + 2)
                if g >= 2:
                    e.wait_ge(ln_lo, 4 * L + g - 1)
                for t in range(2):
                    for k in range(KD):
                        mm = e.transpose(psum[:, 6 + g % 2, (2 * t + k) * P:(2 * t + k + 1) * P],
                                         xn[:, 2 * g + t, k * P:(k + 1) * P], ident[:])
                mm.then_inc(ln_turned, 1)

        def pe_mamba(e):
            slot = lambda n: 2 * (n % 3)
            e.wait_ge(win_hi, 1)
            e.wait_ge(win_lo, 1)
            for m in range(2 * CT):
                if 3 <= m < 3 + CT:
                    e.wait_ge(conv_done, m - 2)
                if m >= 3 + CT:
                    e.wait_ge(gated, m - 2)
                for n in range(NB):
                    if m == 0:
                        e.wait_ge(ln_lo, 2 * n + 2)
                    mm = product(e, psum[:, slot(m) + n], [
                        (cut(win, slice(None), k, slice(m * P, (m + 1) * P)),
                         cut(xnT, slice(None), k, slice(n * BANK, (n + 1) * BANK))) for k in range(KD)])
                mm.then_inc(xz_made, 1)
            e.wait_ge(mw_hi, 2)
            e.wait_ge(mw_lo, 2)
            for m, (a, b) in enumerate(((0, R), (R, R + 2 * NS))):
                if m == 0:
                    e.wait_ge(gated, 2 * CT - 2)
                    e.wait_ge(xc_lo, CT)
                else:
                    e.wait_ge(gated, 2 * CT - 1)
                for n in range(NB):
                    mm = product(e, psum[0:b - a, slot(2 * CT + m) + n], [
                        (cut(wx, slice(None), c, slice(a, b)),
                         cut(inner, slice(None), c, slice(n * BANK, (n + 1) * BANK))) for c in range(CT)])
                mm.then_inc(xd_made, 1)
            for c in range(CT):
                e.wait_ge(xd_lo, 1)
                if c == 0:
                    e.wait_ge(gated, 2 * CT)
                elif c <= 2:
                    e.wait_ge(xd_lo, c)
                else:
                    e.wait_ge(relu_done, 1)
                    e.wait_ge(softp_done, 1)
                for n in range(NB):
                    mm = product(e, psum[:, slot(2 * CT + 2 + c) + n], [
                        (cut(wdt, slice(None), slice(c * P, (c + 1) * P)),
                         dtin_cut(n))])
                mm.then_inc(dtp_made, 1)

            def row(b):
                s, w = divmod(b, 2)
                if b == 0:
                    e.wait_ge(relu_done, CT)
                    e.wait_ge(softp_done, CT)
                    e.wait_ge(xd_lo, 2)
                if b >= 2:
                    e.wait_ge(row_copied, b - 1)
                col = w * NS + s % NS
                for n in range(NB):
                    for part in range(2):
                        mm = e.matmul(psum[:, 4 + 2 * w + n],
                                      ident_r[0:2 * NS, col:col + 1].broadcast_to([2 * NS, P]),
                                      bct[part][:, n * BANK:(n + 1) * BANK],
                                      start=part == 0, stop=part == 1)
                mm.then_inc(row_made, 1)

            e.wait_ge(consts_cast, 3)
            for b in range(6):
                row(b)
            for j in range(4 * NS):
                s, c = divmod(j, 2)
                e.wait_ge(weighed, j + 1)
                if s == NS:
                    e.wait_ge(y_read, c + 1)
                for n in range(NB):
                    mm = e.matmul(psum[:, 2 * c + n], ident[:], state[j % 4][:, n * BANK:(n + 1) * BANK],
                                  start=s % NS == 0, stop=s % NS == NS - 1)
                mm.then_inc(y_added, 1)
                if j + 6 < 4 * NS:
                    row(j + 6)
            e.wait_ge(mw_hi, 3)
            e.wait_ge(mw_lo, 3)
            e.wait_ge(inner_lo, CT)
            for i in range(NT):
                if i >= 4:
                    e.wait_ge(res1, i - 3)
                mm = product(e, psum[:, 4 + i % 4, 0:DM], [
                    (cut(inner, slice(None), c, slice(i * P, (i + 1) * P)), cut(wout, slice(None), c, slice(None)))
                    for c in range(CT)])
                mm.then_inc(op_made, 1)

        def dtin_cut(n):
            return tuple(t[:, 0, n * BANK:(n + 1) * BANK] for t in dtin)

        def pe_ffn(e, f):
            Q = 2 * FM

            def gate_up(k):
                n, m = divmod(k, FM)
                if k >= 3:
                    e.wait_ge(f_mult, Q * f + k - 2)
                if m == 0:
                    e.wait_ge(ln_lo, 4 * (2 * f + 1) + 2 * n + 2)
                for g in range(2):
                    mm = product(e, psum[0:MW[m], 2 * (k % 3) + g], [
                        (cut(wgu, slice(None), kt, slice(g * INTER + m * P, g * INTER + m * P + MW[m])),
                         cut(xnT, slice(None), kt, slice(n * BANK, (n + 1) * BANK))) for kt in range(KD)])
                mm.then_inc(gu_made, 1)

            def down(i):
                n = i // 4
                e.wait_ge(hid_lo, Q * f + (n + 1) * FM)
                if i >= 2:
                    e.wait_ge(f_res, NT * f + i - 1)
                mm = product(e, psum[:, 6 + i % 2, 0:DM], [
                    (cut(hid[n], slice(0, MW[m]), m, slice((i % 4) * P, (i % 4 + 1) * P)),
                     cut(wdn, slice(0, MW[m]), m, slice(None))) for m in range(FM)])
                mm.then_inc(dn_made, 1)

            e.wait_ge(ld["wffn"], 96 * (f + 1))
            for k in range(FM + 2):
                gate_up(k)
            for i in range(4):
                down(i)
            for k in range(FM + 2, Q):
                gate_up(k)
            for i in range(4, NT):
                down(i)

        def pe_attention(e):
            def unit(u):
                kind, a, b = u
                k = unit_no[u]
                acc = psum[:, unit_bank(k)]
                if bank_free(k):
                    e.wait_ge(unit_done, bank_free(k))
                if kind in "QKV":
                    e.wait_ge(ln_lo, 8 + (2 * a + 2 if kind == "Q" else 4))
                if kind == "Q":
                    e.wait_ge(wq_split, 2 * (wq_chunk(u) + 1))
                    mm = product(e, acc, [
                        (cut(wq[wq_chunk(u) % 2], slice(None), kt, slice((b % 4) * P, (b % 4 + 1) * P)),
                         cut(xnT, slice(None), kt, slice(a * HALF, (a + 1) * HALF))) for kt in range(KD)])
                elif kind == "K":
                    e.wait_ge(w_split, split_no[("wk", a // 2)])
                    mm = product(e, acc, [
                        (cut(wk, slice(None), kt, slice((a % 2) * P, (a % 2 + 1) * P)),
                         cut(xnT, slice(None), kt, slice(b * BANK, (b + 1) * BANK))) for kt in range(KD)])
                elif kind == "V":
                    e.wait_ge(w_split, split_no[("wv", a)])
                    for t in range(2):
                        mm = product(e, acc[:, t * SLAB:(t + 1) * SLAB], [
                            (cut(xnT, slice(None), kt, slice((2 * b + t) * P, (2 * b + t + 1) * P)),
                             cut(wv, slice(None), kt, slice(None))) for kt in range(KD)])
                else:
                    e.wait_ge(w_split, split_no[("wo", a)])
                    if b == 0:
                        e.wait_ge(oT_lo, 8 * (a + 1))
                    for t in range(2):
                        mm = product(e, acc[:, t * SLAB:(t + 1) * SLAB], [
                            (cut(oT[a % 2], slice(None), hh, slice((2 * b + t) * P, (2 * b + t + 1) * P)),
                             cut(wo, slice(None), hh, slice(None))) for hh in range(2)])
                mm.then_inc(unit_made, 1)

            def scores(n):
                h, i = divmod(n, NT)
                if n >= 2:
                    e.wait_ge(exp_done, n - 1)
                e.wait_ge(q_split, 4 * h + i // 2 + 1)
                if i == 0:
                    e.wait_ge(unit_done, unit_no[("K", h, NB - 1)] + 1)
                width = (i + 1) * P
                for b in range(0, width, BANK):
                    w = min(BANK, width - b)
                    acc = psum[:, 2 * (n % 2) + b // BANK]
                    diagonal = b + w == width
                    mm = product(e, acc[:, 0:w], [
                        (cut(q[h % 2], slice(None), slice(i * P, (i + 1) * P)),
                         cut(kT[h % 2], slice(None), slice(b, b + w)))], last=not diagonal)
                    if diagonal:
                        mm = e.matmul(acc[:, w - P:w], ident_b[:], causal_b[:], start=False, stop=True)
                mm.then_inc(scored, 1)

            def turn(n):
                h, i = divmod(n, NT)
                e.wait_ge(normed, n + 1)
                if n == 0:
                    e.wait_ge(unit_done, len(first_units))
                for g, (a, b) in enumerate(groups(i)):
                    t = turned_before(n) + g
                    if t >= 2:
                        e.wait_ge(pT_lo, t - 1)
                    for j in range(a, b):
                        mm = e.transpose(psum[:, 4 + t % 2, (j - a) * P:(j - a + 1) * P],
                                         probs[n % 2][:, j * P:(j + 1) * P], ident[:])
                    mm.then_inc(turned, 1)

            def values(n):
                h, i = divmod(n, NT)
                s = n // 2
                e.wait_ge(pT_lo, turned_before(n + 1))
                if i == 1:
                    e.wait_ge(unit_done, unit_no[("V", h // 2, NT // 2 - 1)] + 1)
                if s >= 1:
                    e.wait_ge(oT_lo, s)
                acc = psum[:, 6, 0:SLAB]
                vh = lambda j: cut(v2[h // 2 % 2], slice(None), j, slice((h % 2) * DH, (h % 2 + 1) * DH))
                product(e, acc, [(vh(j), cut(pT, slice(None), j, slice(None))) for j in range(i)], last=False)
                mm = product(e, acc[:, P:SLAB], [(vh(i), cut(pT, slice(None), i, slice(P, SLAB)))], first=False)
                mm.then_inc(pv_made, 1)

            for u in first_units:
                unit(u)
            scores(0)
            scores(1)
            for n in range(NH * NT):
                turn(n)
                if n + 2 < NH * NT:
                    scores(n + 2)
                for u in units_at[n]:
                    unit(u)
                if n % 2:
                    values(n)
            for u in last_units:
                unit(u)

        @block.tensor
        def _(e):
            pe_layer_norm(e, 0)
            pe_mamba(e)
            pe_layer_norm(e, 1)
            pe_ffn(e, 0)
            pe_layer_norm(e, 2)
            pe_attention(e)
            pe_layer_norm(e, 3)
            pe_ffn(e, 1)

        def turn_views(g):
            src = psum[:, 6 + g % 2].rearrange("p (t k c) -> p t k c", t=2, k=KD)
            dst = [t[:, :, g * 2 * P:(g + 1) * 2 * P].rearrange("p k (t c) -> p t k c", t=2) for t in xnT]
            return src, dst

        def act_layer_norm(e, L):
            for g in range(NT // 2):
                e.wait_ge(ln_turned, 4 * L + g + 1)
                src, dst = turn_views(g)
                nc.scalar.activation(dst[0], src, ACT.Copy).then_inc(ln_hi, 1)

        def act_mamba(e):
            slot = lambda n: 2 * (n % 3)
            two = lambda n: psum[:, slot(n):slot(n) + 2].rearrange("p a b -> p (a b)")

            def tap(m):
                e.wait_ge(xz_made, m + 1)
                if m >= 2:
                    e.wait_ge(gated, m - 1)
                nc.scalar.activation(taps[m % 2][:], two(m), ACT.Identity, bias=convb_half[:, m:m + 1],
                                     scale=convw_half[:, m, 1:2]).then_inc(tap_mid, 1)

            def tanh(m):
                if m >= 2:
                    e.wait_ge(gated, m - 1)
                if m < CT:
                    e.wait_ge(conv_done, m + 1)
                    nc.scalar.activation(tanh_xz[m % 2][:], taps[m % 2][:], ACT.Tanh).then_inc(tanh_done, 1)
                else:
                    e.wait_ge(xz_made, m + 1)
                    nc.scalar.activation(tanh_xz[m % 2][:], two(m), ACT.Tanh, scale=0.5).then_inc(tanh_done, 1)

            def xc_high(m):
                e.wait_ge(gated, m + 1)
                nc.scalar.activation(inner[0][:, m], xc[:, m], ACT.Copy).then_inc(xc_hi, 1)

            e.wait_ge(small_done, 2)
            e.wait_ge(ones_made, 1)
            todo = list(range(NBUILD))
            act_build(e, todo.pop(0))
            for m in range(CT):
                tap(m)
                if m >= 1:
                    tanh(m - 1)
                if m >= 2:
                    xc_high(m - 2)
                act_build(e, todo.pop(0))
            tanh(CT - 1)
            xc_high(CT - 2)
            for n, b in enumerate(todo):
                act_build(e, b)
                if n == 0:
                    xc_high(CT - 1)
            weight_high(e, NBUILD - 1)
            for m in range(CT, 2 * CT):
                tanh(m)
            for m in range(2):
                e.wait_ge(xd_made, m + 1)
                if m == 0:
                    nc.scalar.activation(dtin[0][:, 0, 0:TOK], two(2 * CT), ACT.Copy).then_inc(xd_hi, 1)
                else:
                    nc.scalar.activation(bct[0][:], two(2 * CT + 1)[0:2 * NS], ACT.Copy).then_inc(xd_hi, 1)
            nc.scalar.preload_act_table_set("natural_log_exp_and_others")
            e.wait_ge(gated, 2 * CT)
            own = 0
            nc.scalar.activation(aneg[:], alog[:], ACT.Exp).then_inc(act_own, 1)
            own += 1
            for c in range(CT):
                e.wait_ge(dtp_made, c + 1)
                if c >= 2:
                    e.wait_ge(dt_done, c - 1)
                t = softp[c % 2]
                nc.scalar.activation(t[:], two(2 * CT + 2 + c), ACT.Abs, bias=bdt[:, c:c + 1]).then_inc(act_own, 1)
                own += 1
                e.wait_ge(act_own, own)
                nc.scalar.activation(t[:], t[:], ACT.Exp, scale=-1.0).then_inc(act_own, 1)
                own += 1
                e.wait_ge(act_own, own)
                nc.scalar.activation(t[:], t[:], ACT.Ln, bias=ones_col[:]).then_inc(softp_done, 1)

            def row(b):
                s, w = divmod(b, 2)
                e.wait_ge(row_made, b + 1)
                if s >= 3:
                    e.wait_ge(drive_done if w == 0 else weighed, 2 * (s - 2))
                dst = (b_row, c_row)[w][s % 3]
                nc.scalar.activation(dst, psum[:, 4 + 2 * w:6 + 2 * w].rearrange("p a b -> p (a b)"),
                                     ACT.Copy).then_inc(row_copied, 1)

            e.wait_ge(dt_done, CT)
            e.wait_ge(small_done, 3)
            e.wait_ge(xc_lo, CT)
            e.wait_ge(dtu_done, CT)
            def decay_of(j):
                s, c = divmod(j, 2)
                ct = 2 * (s // NS) + c
                if j >= 3:
                    e.wait_ge(scanned, j - 2)
                nc.scalar.activation(decay[j % 3], dt[:, ct], ACT.Exp,
                                     scale=aneg[:, ct, s % NS:s % NS + 1]).then_inc(decay_done, 1)

            for b in range(4):
                row(b)
            decay_of(0)
            decay_of(1)
            for j in range(4 * NS):
                if j + 4 < 4 * NS:
                    row(j + 4)
                if j + 2 < 4 * NS:
                    decay_of(j + 2)
                if j in (2 * NS + 5, 4 * NS - 1):
                    for c in range(2):
                        ct = 2 * (j // (2 * NS + 6)) + c
                        e.wait_ge(inner_f, ct + 1)
                        nc.scalar.activation(inner[0][:, ct], dtu[:, ct], ACT.Copy).then_inc(inner_hi, 1)

        def act_build(e, b):
            _, _, _, parts, cols = builds[b]
            a = lambda t: t[0:parts, 0:cols]
            e.wait_ge(bits_done, 4 * b + 1)
            if b >= 2:
                e.wait_ge(weight_picked, 7 * (b - 1))
                e.wait_ge(weight_lo, b - 1)
            for k in range(ACT_PICKS):
                nc.scalar.activation(a(pick[b % 2][k]), a(bits[b % 2][0]), ACT.Identity,
                                     bias=lut_row[0:parts, 2 * k:2 * k + 1],
                                     scale=lut_step[0:parts, k:k + 1]).then_inc(act_picks, 1)
            if b >= 1:
                weight_high(e, b - 1)

        def weight_high(e, b):
            _, _, _, parts, cols = builds[b]
            e.wait_ge(weight_picked, 7 * (b + 1))
            if b >= 2:
                e.wait_ge(spilled[b % 2], 32 * (b // 2))
            nc.scalar.activation(built[b % 2][0][0:parts, 0:cols], pick[b % 2][0][0:parts, 0:cols],
                                 ACT.Copy).then_inc(weight_hi, 1)

        def act_ffn(e, f):
            Q = 2 * FM
            for k in range(Q):
                n, m = divmod(k, FM)
                w = MW[m]
                e.wait_ge(gu_made, Q * f + k + 1)
                if k >= 2:
                    e.wait_ge(f_gated, Q * f + k - 1)
                nc.scalar.activation(f_tanh[k % 2][0:w], psum[0:w, 2 * (k % 3)], ACT.Tanh,
                                     scale=0.5).then_inc(f_tanhed, 1)
                if k >= 1:
                    hid_high(e, f, k - 1)
            hid_high(e, f, Q - 1)

        def hid_high(e, f, k):
            n, m = divmod(k, FM)
            e.wait_ge(f_mult, 2 * FM * f + k + 1)
            nc.scalar.activation(hid[n][0][0:MW[m], m], f_prod[k % 2][0:MW[m]], ACT.Copy,
                                 scale=0.5).then_inc(hid_hi, 1)

        def unit_target(u, part):
            kind, a, b = u
            if kind == "K":
                return kT[a % 2][part][:, b * BANK:(b + 1) * BANK]
            return v2[a % 2][part][:, 2 * b:2 * b + 2].rearrange("p t c -> p (t c)")

        def act_attention(e):
            def unit(u):
                kind, a, b = u
                if kind not in "KV":
                    return
                k = unit_no[u]
                e.wait_ge(unit_made, k + 1)
                acc = psum[:, unit_bank(k)]
                if kind == "K":
                    nc.scalar.activation(unit_target(u, 0), acc, ACT.Identity,
                                         bias=bk_t[:, a:a + 1]).then_inc(unit_hi, 1)
                else:
                    nc.scalar.activation(unit_target(u, 0), acc, ACT.Copy).then_inc(unit_hi, 1)

            def exp(n):
                h, i = divmod(n, NT)
                e.wait_ge(max_done, n + 1)
                if n >= 2:
                    e.wait_ge(turned, turned_before(n - 1))
                nc.scalar.activation(probs[n % 2][:, 0:(i + 1) * P],
                                     psum[:, 2 * (n % 2):2 * (n % 2) + 2].rearrange("p a b -> p (a b)")[:, 0:(i + 1) * P],
                                     ACT.Exp, bias=neg_max[:, h, i:i + 1],
                                     accum_out=row_sum[:, h, i:i + 1]).then_inc(exp_done, 1)

            def turned_hi(n):
                h, i = divmod(n, NT)
                for g, (a, b) in enumerate(groups(i)):
                    t = turned_before(n) + g
                    e.wait_ge(turned, t + 1)
                    dst, src = turned_views(n, t, a, b)
                    nc.scalar.activation(dst[0], src, ACT.Copy).then_inc(pT_hi, 1)

            def value_hi(n):
                s = n // 2
                e.wait_ge(pv_made, s + 1)
                dst, src = value_views(s)
                nc.scalar.activation(dst[0], src, ACT.Identity,
                                     bias=bv_t[:, n // NT:n // NT + 1]).then_inc(oT_hi, 1)

            e.wait_ge(ld["bias"], 64)
            for u in first_units:
                unit(u)
            exp(0)
            exp(1)
            for n in range(NH * NT):
                turned_hi(n)
                if n + 2 < NH * NT:
                    exp(n + 2)
                for u in units_at[n]:
                    unit(u)
                if n % 2:
                    value_hi(n)

        def turned_views(n, t, a, b):
            c = (n % 2) * P
            dst = [p[:, a:b, c:c + P] for p in pT]
            src = psum[:, 4 + t % 2, 0:(b - a) * P].rearrange("p (j c) -> p j c", c=P)
            return dst, src

        def value_views(s):
            h, g = divmod(s, NT // 2)
            dst = [t[:, h % 2, g * SLAB:(g + 1) * SLAB] for t in oT[h // 2 % 2]]
            return dst, psum[:, 6, 0:SLAB]

        @block.scalar
        def _(e):
            e.wait_ge(ld["win"], 16)
            nc.scalar.activation(win[0][:], win_raw[:], ACT.Copy).then_inc(win_hi, 1)
            act_layer_norm(e, 0)
            e.wait_ge(ld["wx"], 16)
            nc.scalar.activation(wx[0][:], wx_raw[:], ACT.Copy).then_inc(mw_hi, 1)
            e.wait_ge(ld["wdt"], 16)
            nc.scalar.activation(wdt[0][:], wdt_raw[:], ACT.Copy).then_inc(mw_hi, 1)
            e.wait_ge(ld["wout"], 16)
            nc.scalar.activation(wout[0][:], wout_raw[:], ACT.Copy).then_inc(mw_hi, 1)
            act_mamba(e)
            act_layer_norm(e, 1)
            e.wait_ge(ld["wffn"], 96)
            act_ffn(e, 0)
            act_layer_norm(e, 2)
            act_attention(e)
            act_layer_norm(e, 3)
            act_ffn(e, 1)

        def dve_layer_norm(e, L, ready):
            for g in range(NT // 2 + 2):
                if g < NT // 2:
                    for i in (2 * g, 2 * g + 1):
                        e.wait_ge(*ready(i))
                        nc.vector.bn_stats(stats[:, i], res[:, i]).then_inc(ln_stats, 1)
                    for i in (2 * g, 2 * g + 1):
                        e.wait_ge(ln_stats, NT * L + i + 1)
                        nc.vector.bn_aggr(mean_var[:, i], stats[:, i]).then_inc(ln_mv, 1)
                if 1 <= g <= NT // 2:
                    e.wait_ge(ln_rstd, 4 * L + g)
                    for i in (2 * g - 2, 2 * g - 1):
                        nc.vector.tensor_scalar(xn[:, i], res[:, i], mean_var[:, i, 0:1], rstd[:, i:i + 1],
                                                ALU.subtract, ALU.mult).then_inc(ln_xn, 1)
                if g >= 2:
                    turned_low(e, L, g - 2)

        def turned_low(e, L, g):
            e.wait_ge(ln_hi, 4 * L + g + 1)
            src, dst = turn_views(g)
            nc.vector.tensor_tensor(dst[1], src, f32(dst[0]), ALU.subtract).then_inc(ln_lo, 1)

        def dve_bits(e, b):
            dram, where, src, parts, cols = builds[b]
            a = lambda t: t[0:parts, 0:cols]
            e.wait_ge(ld[f"idx{b % 2}"], 16 * (b // 2 + 1))
            if b >= 2:
                e.wait_ge(weight_picked, 7 * (b - 1))
                e.wait_ge(act_picks, ACT_PICKS * (b - 1))
                e.wait_ge(pool_picks, (PICKS - ACT_PICKS) * (b - 1))
            for k, t in enumerate(bits[b % 2]):
                nc.vector.tensor_single_scalar(a(t), a(idx_t[b % 2]), 1 << k, ALU.bitwise_and).then_inc(bits_done, 1)

        def dve_build(e, b):
            if b + 1 < NBUILD:
                dve_bits(e, b + 1)
            dram, where, src, parts, cols = builds[b]
            a = lambda t: t[0:parts, 0:cols]
            pk, bt = pick[b % 2], bits[b % 2]
            e.wait_ge(act_picks, ACT_PICKS * (b + 1))
            e.wait_ge(pool_picks, (PICKS - ACT_PICKS) * (b + 1))
            e.wait_ge(bits_done, 4 * (b + 1))
            n = 0
            for level, step in ((1, 1), (2, 2), (3, 4)):
                if n:
                    e.wait_ge(weight_picked, 7 * b + n)
                for k in range(0, PICKS, 2 * step):
                    nc.vector.copy_predicated(a(pk[k]), a(bt[level]), a(pk[k + step])).then_inc(weight_picked, 1)
                    n += 1

        def dve_mamba(e):
            slot = lambda n: 2 * (n % 3)
            two = lambda n: psum[:, slot(n):slot(n) + 2].rearrange("p a b -> p (a b)")

            def conv(m):
                t = taps[m % 2]
                e.wait_ge(tap_mid, m + 1)
                nc.vector.scalar_tensor_tensor(out=t[:, 1:TOK], in0=two(m)[:, 0:TOK - 1], scalar=convw_half[:, m, 0:1],
                                               in1=t[:, 1:TOK], op0=ALU.mult, op1=ALU.add).then_inc(dve_own, 1)
                own[0] += 1
                e.wait_ge(dve_own, own[0])
                nc.vector.scalar_tensor_tensor(out=t[:, 0:TOK - 1], in0=two(m)[:, 1:TOK], scalar=convw_half[:, m, 2:3],
                                               in1=t[:, 0:TOK - 1], op0=ALU.mult, op1=ALU.add).then_inc(conv_done, 1)

            def gate(m):
                e.wait_ge(tanh_done, m + 1)
                src = taps[m % 2][:] if m < CT else two(m)
                dst = xc[:, m] if m < CT else sz2[:, m - CT]
                nc.vector.scalar_tensor_tensor(out=dst, in0=tanh_xz[m % 2][:], scalar=1.0, in1=src,
                                               op0=ALU.add, op1=ALU.mult).then_inc(gated, 1)

            dve_bits(e, 0)
            todo = list(range(NBUILD))
            for m in range(CT):
                conv(m)
                if m >= 1:
                    gate(m - 1)
                dve_build(e, todo.pop(0))
            gate(CT - 1)
            for b in todo:
                dve_build(e, b)
            all_spilled(e)
            for m in range(CT, 2 * CT):
                gate(m)
            for m in range(2):
                e.wait_ge(xd_hi, m + 1)
                if m == 0:
                    nc.vector.tensor_tensor(dtin[1][:, 0, 0:TOK], two(2 * CT), f32(dtin[0][:, 0, 0:TOK]),
                                            ALU.subtract).then_inc(xd_lo, 1)
                else:
                    nc.vector.tensor_tensor(bct[1][:], two(2 * CT + 1)[0:2 * NS], f32(bct[0][:]),
                                            ALU.subtract).then_inc(xd_lo, 1)
            for c in range(CT):
                e.wait_ge(dtp_made, c + 1)
                e.wait_ge(act_own, 2 * c + 2)
                nc.vector.tensor_scalar(dt[:, c], two(2 * CT + 2 + c), bdt[:, c:c + 1], 0.0,
                                        ALU.add, ALU.max).then_inc(relu_done, 1)
                e.wait_ge(softp_done, c + 1)
                e.wait_ge(relu_done, c + 1)
                nc.vector.tensor_tensor(dt[:, c], dt[:, c], softp[c % 2][:], ALU.add).then_inc(dt_done, 1)
            e.wait_ge(act_own, 1)
            nc.vector.tensor_scalar(aneg[:], aneg[:], -1.0, None, ALU.mult).then_inc(small_done, 1)

            def scan(j):
                e.wait_ge(decay_done, j + 1)
                e.wait_ge(drive_done, j + 1)
                if j >= 4:
                    e.wait_ge(y_added, j - 3)
                nc.vector.tensor_tensor_scan(state[j % 4], decay[j % 3], drive[j % 3], 0.0,
                                             ALU.mult, ALU.add).then_inc(scanned, 1)

            def weigh(j):
                e.wait_ge(scanned, j + 1)
                e.wait_ge(row_copied, 2 * (j // 2) + 2)
                nc.vector.tensor_tensor(state[j % 4], state[j % 4], c_row[j // 2 % 3],
                                        ALU.mult).then_inc(weighed, 1)

            def finish(c):
                e.wait_ge(y_added, 32 * (c // 2) + 31 + c % 2)
                y = psum[:, 2 * (c % 2):2 * (c % 2) + 2].rearrange("p a b -> p (a b)")
                e.wait_ge(drive_done, 32 * (c // 2 + 1))
                nc.vector.scalar_tensor_tensor(out=dtu[:, c], in0=xc[:, c], scalar=dskip[:, c:c + 1], in1=y,
                                               op0=ALU.mult, op1=ALU.add).then_inc(y_read, 1)
                e.wait_ge(y_read, c + 1)
                nc.vector.scalar_tensor_tensor(out=dtu[:, c], in0=dtu[:, c], scalar=0.5, in1=sz2[:, c],
                                               op0=ALU.mult, op1=ALU.mult).then_inc(inner_f, 1)

            for j in range(4 * NS + 1):
                if j < 4 * NS:
                    scan(j)
                if j >= 1:
                    weigh(j - 1)
                if j in (2 * NS + 1, 4 * NS):
                    finish(2 * (j // (2 * NS + 2)))
                    finish(2 * (j // (2 * NS + 2)) + 1)
            for i in range(NT):
                e.wait_ge(op_made, i + 1)
                nc.vector.tensor_tensor(res[:, i], res[:, i], psum[:, 4 + i % 4, 0:DM], ALU.add).then_inc(res1, 1)

        own = [0]

        def dve_ffn(e, f):
            Q = 2 * FM

            def down(i):
                e.wait_ge(dn_made, NT * f + i + 1)
                nc.vector.tensor_tensor(res[:, i], res[:, i], psum[:, 6 + i % 2, 0:DM], ALU.add).then_inc(f_res, 1)

            for k in range(Q):
                n, m = divmod(k, FM)
                w = MW[m]
                e.wait_ge(f_tanhed, Q * f + k + 1)
                if k >= 2:
                    e.wait_ge(f_mult, Q * f + k - 1)
                nc.vector.scalar_tensor_tensor(out=f_gate[k % 2][0:w], in0=f_tanh[k % 2][0:w], scalar=1.0,
                                               in1=psum[0:w, 2 * (k % 3)], op0=ALU.add,
                                               op1=ALU.mult).then_inc(f_gated, 1)
                e.wait_ge(f_gated, Q * f + k + 1)
                if k >= 2:
                    e.wait_ge(hid_lo, Q * f + k - 1)
                nc.vector.tensor_tensor(f_prod[k % 2][0:w], f_gate[k % 2][0:w], psum[0:w, 2 * (k % 3) + 1],
                                        ALU.mult).then_inc(f_mult, 1)
                if k >= 1:
                    hid_low(e, f, k - 1)
                if k == FM + 1:
                    for i in range(4):
                        down(i)
            hid_low(e, f, Q - 1)
            for i in range(4, NT):
                down(i)

        def hid_low(e, f, k):
            n, m = divmod(k, FM)
            w = MW[m]
            e.wait_ge(hid_hi, 2 * FM * f + k + 1)
            nc.vector.scalar_tensor_tensor(out=hid[n][1][0:w, m], in0=f_prod[k % 2][0:w], scalar=0.5,
                                           in1=f32(hid[n][0][0:w, m]), op0=ALU.mult,
                                           op1=ALU.subtract).then_inc(hid_lo, 1)

        def dve_attention(e):
            def unit(u):
                kind, a, b = u
                k = unit_no[u]
                acc = psum[:, unit_bank(k)]
                if kind == "Q":
                    e.wait_ge(unit_made, k + 1)
                    nc.vector.tensor_scalar(qstage[a][:, :, b], acc.rearrange("p (h t) -> p h t", t=HTOK), bq_t[:, b:b + 1], SCALE,
                                            ALU.add, ALU.mult).then_inc(unit_done, 1)
                elif kind == "O":
                    e.wait_ge(unit_made, k + 1)
                    if a == 0:
                        e.wait_ge(bo_added, NT)
                    else:
                        e.wait_ge(unit_done, unit_no[("O", a - 1, b)] + 1)
                    both = res[:, 2 * b:2 * b + 2].rearrange("p t c -> p (t c)")
                    nc.vector.tensor_tensor(both, both, acc, ALU.add).then_inc(unit_done, 1)
                else:
                    e.wait_ge(unit_hi, hi_no[u] + 1)
                    hi = f32(unit_target(u, 0))
                    if kind == "K":
                        nc.vector.scalar_tensor_tensor(out=unit_target(u, 1), in0=acc, scalar=bk_t[:, a:a + 1],
                                                       in1=hi, op0=ALU.add, op1=ALU.subtract).then_inc(unit_done, 1)
                    else:
                        nc.vector.tensor_tensor(unit_target(u, 1), acc, hi, ALU.subtract).then_inc(unit_done, 1)

            def row_max(n):
                h, i = divmod(n, NT)
                e.wait_ge(scored, n + 1)
                nc.vector.tensor_reduce(neg_max[:, h, i:i + 1],
                                        psum[:, 2 * (n % 2):2 * (n % 2) + 2].rearrange("p a b -> p (a b)")[:, 0:(i + 1) * P],
                                        AX_X, ALU.max, negate=True).then_inc(max_done, 1)

            def inverse(n):
                h, i = divmod(n, NT)
                e.wait_ge(exp_done, n + 1)
                nc.vector.reciprocal(row_inv[:, h, i:i + 1], row_sum[:, h, i:i + 1]).then_inc(inv_done, 1)

            def turned_lo(n):
                h, i = divmod(n, NT)
                for g, (a, b) in enumerate(groups(i)):
                    t = turned_before(n) + g
                    e.wait_ge(pT_hi, t + 1)
                    dst, src = turned_views(n, t, a, b)
                    nc.vector.tensor_tensor(dst[1], src, f32(dst[0]), ALU.subtract).then_inc(pT_lo, 1)

            def value_lo(n):
                s = n // 2
                e.wait_ge(oT_hi, s + 1)
                dst, src = value_views(s)
                nc.vector.scalar_tensor_tensor(out=dst[1], in0=src, scalar=bv_t[:, n // NT:n // NT + 1],
                                               in1=f32(dst[0]), op0=ALU.add, op1=ALU.subtract).then_inc(oT_lo, 1)

            e.wait_ge(ld["bias"], 64)
            for u in first_units:
                unit(u)
            for i in range(NT):
                nc.vector.tensor_tensor(res[:, i], res[:, i], bo_row[:], ALU.add).then_inc(bo_added, 1)
            for n in range(2):
                row_max(n)
            for n in range(2):
                inverse(n)
            for n in range(NH * NT):
                turned_lo(n)
                if n + 2 < NH * NT:
                    row_max(n + 2)
                for u in units_at[n]:
                    unit(u)
                if n + 2 < NH * NT:
                    inverse(n + 2)
                if n % 2:
                    value_lo(n)
            for u in last_units:
                unit(u)

        @block.vector
        def _(e):
            nc.vector.memset(ones_col[:], 1.0).then_inc(ones_made, 1)
            e.wait_ge(ld["lut"], 16)
            pairs = lut_row[:].rearrange("p (a b) -> p a b", b=2)
            nc.vector.tensor_tensor(lut_step[:], pairs[:, :, 1], pairs[:, :, 0], ALU.subtract).then_inc(small_done, 1)
            dve_layer_norm(e, 0, lambda i: (ld["x"], 16))
            e.wait_ge(ld["small"], 80)
            nc.vector.tensor_scalar(convw_half[:], convw[:], 0.5, None, ALU.mult).then_inc(dve_own, 1)
            own[0] += 1
            nc.vector.tensor_scalar(convb_half[:], convb[:], 0.5, None, ALU.mult).then_inc(small_done, 1)
            e.wait_ge(consts_made, 3)
            nc.vector.tensor_copy(ident_r[:], ident[:]).then_inc(consts_cast, 1)
            nc.vector.tensor_copy(ident_b[:], ident[:]).then_inc(consts_cast, 1)
            nc.vector.tensor_copy(causal_b[:], causal[:]).then_inc(consts_cast, 1)
            dve_mamba(e)
            dve_layer_norm(e, 1, lambda i: (res1, i + 1))
            dve_ffn(e, 0)
            dve_layer_norm(e, 2, lambda i: (f_res, i + 1))
            dve_attention(e)
            dve_layer_norm(e, 3, lambda i: (unit_done, unit_no[("O", NP - 1, i // 2)] + 1))
            dve_ffn(e, 1)

        def pool_layer_norm(e, L):
            e.wait_ge(consts_made, 3)
            for g in range(NT // 2):
                two = slice(2 * g, 2 * g + 2)
                e.wait_ge(ln_mv, NT * L + 2 * g + 2)
                nc.gpsimd.tensor_scalar(var_eps[:, two], mean_var[:, two, 1], 1.0, EPS,
                                        ALU.mult, ALU.add).then_inc(pool_own, 1)
                pown[0] += 1
                e.wait_ge(pool_own, pown[0])
                nc.gpsimd.tensor_tensor(rstd[:, two], var_eps[:, two], half_neg[:, two], ALU.pow).then_inc(ln_rstd, 1)

        pown = [0]

        def pool_lo(e, lo, src, hi, s):
            split_lo(nc.gpsimd, lo, src, hi).then_inc(s, 1)

        def pool_attention(e):
            def split(name, r):
                pair = {"wk": wk, "wv": wv, "wo": wo}[name]
                e.wait_ge(ld["w"], 8 * split_no[(name, r)])
                if r >= 1:
                    last = {"wk": ("K", 2 * r - 1, NB - 1), "wv": ("V", r - 1, NT // 2 - 1),
                            "wo": ("O", r - 1, NT // 2 - 1)}[name]
                    e.wait_ge(unit_made, unit_no[last] + 1)
                split_hi_pool(nc.gpsimd, pair[0][:], w_raw[:]).then_inc(w_split, 1)
                e.wait_ge(w_split, split_no[(name, r)] - 1)
                split_lo(nc.gpsimd, pair[1][:], w_raw[:], pair[0][:]).then_inc(w_split, 1)

            def split_wq(k):
                e.wait_ge(ld["wq"], 16 * (k + 1))
                if k >= 2:
                    e.wait_ge(unit_made, unit_no[("Q", (k - 2) // 4, 4 * ((k - 2) % 4) + 3)] + 1)
                split_hi_pool(nc.gpsimd, wq[k % 2][0][:], wq_raw[:]).then_inc(wq_split, 1)
                e.wait_ge(wq_split, 2 * k + 1)
                split_lo(nc.gpsimd, wq[k % 2][1][:], wq_raw[:], wq[k % 2][0][:]).then_inc(wq_split, 1)

            def q_piece(h, pc):
                npc = TOK // SLAB
                if h >= 2:
                    e.wait_ge(scored, NT * (h - 1))
                tok = SLAB // NH
                if pc == 0:
                    e.wait_ge(ld[f"q{h % 2}"], 16 * (h // 2 + 1))
                src = q_raw[h % 2][:, :, pc * tok:(pc + 1) * tok].rearrange("p c t -> p t c")
                hi, lo = (t[:, pc * SLAB:(pc + 1) * SLAB].rearrange("p (t c) -> p t c", c=NH) for t in q[h % 2])
                split_hi_pool(nc.gpsimd, hi, src).then_inc(q_hi, 1)
                e.wait_ge(q_hi, npc * h + pc + 1)
                split_lo(nc.gpsimd, lo, src, hi).then_inc(q_split, 1)

            def norm(n):
                h, i = divmod(n, NT)
                e.wait_ge(inv_done, n + 1)
                pr = probs[n % 2][:, 0:(i + 1) * P]
                nc.gpsimd.tensor_scalar(pr, pr, row_inv[:, h, i:i + 1], 0.0, ALU.mult, ALU.add).then_inc(normed, 1)

            split_wq(0)
            split("wk", 0)
            split_wq(1)
            split("wv", 0)
            pool_layer_norm(e, 2)
            for k in range(2, 8):
                split_wq(k)
            for pc in range(TOK // SLAB):
                q_piece(0, pc)
            norm(0)
            norm(1)
            for n in range(NH * NT):
                h, i = divmod(n, NT)
                r, st = h // 2, (h % 2) * NT + i
                if n + 2 < NH * NT:
                    norm(n + 2)
                if i < TOK // SLAB and h + 1 < NH:
                    q_piece(h + 1, i)
                if st == 4 and r + 1 < NP:
                    split("wk", r + 1)
                if st == 6 and r + 1 < NP:
                    split("wv", r + 1)
                if st == 12:
                    split("wo", r)

        @block.gpsimd
        def _(e):
            nc.gpsimd.memset(ident[:], 0.0).then_inc(pool_own, 1)
            nc.gpsimd.memset(causal[:], 0.0).then_inc(pool_own, 1)
            nc.gpsimd.memset(half_neg[:], -0.5).then_inc(consts_made, 1)
            e.wait_ge(pool_own, 2)
            pown[0] += 2
            nc.gpsimd.affine_select(out=ident[:], in_=ident[:], compare_op=ALU.not_equal, fill=1.0, base=0,
                                    pattern=[[-1, P]], channel_multiplier=1).then_inc(consts_made, 1)
            nc.gpsimd.affine_select(out=causal[:], in_=causal[:], compare_op=ALU.is_ge, fill=MASKED, base=0,
                                    pattern=[[-1, P]], channel_multiplier=1).then_inc(consts_made, 1)
            pool_layer_norm(e, 0)
            e.wait_ge(win_hi, 1)
            pool_lo(e, win[1][:], win_raw[:], win[0][:], win_lo)
            for k, (w, raw) in enumerate(((wx, wx_raw[:]), (wdt, wdt_raw[:]), (wout, wout_raw[:]))):
                e.wait_ge(mw_hi, k + 1)
                pool_lo(e, w[1][:], raw, w[0][:], mw_lo)
            e.wait_ge(small_done, 1)
            for b in range(NBUILD + 1):
                if b < NBUILD:
                    _, _, _, parts, cols = builds[b]
                    a = lambda t: t[0:parts, 0:cols]
                    e.wait_ge(bits_done, 4 * b + 1)
                    if b >= 2:
                        e.wait_ge(weight_picked, 7 * (b - 1))
                        e.wait_ge(weight_lo, b - 1)
                    for k in range(ACT_PICKS, PICKS):
                        nc.gpsimd.tensor_scalar(a(pick[b % 2][k]), a(bits[b % 2][0]), lut_step[0:parts, k:k + 1],
                                                lut_row[0:parts, 2 * k:2 * k + 1], ALU.mult,
                                                ALU.add).then_inc(pool_picks, 1)
                if b >= 1:
                    _, _, _, parts, cols = builds[b - 1]
                    a = lambda t: t[0:parts, 0:cols]
                    e.wait_ge(weight_hi, b)
                    src = built[(b - 1) % 2]
                    pool_lo(e, a(src[1]), a(pick[(b - 1) % 2][0]), a(src[0]), weight_lo)
                if 3 <= b < 3 + CT:
                    if b == 3:
                        e.wait_ge(mw_lo, 3)
                    e.wait_ge(xc_hi, b - 2)
                    pool_lo(e, inner[1][:, b - 3], xc[:, b - 3], inner[0][:, b - 3], xc_lo)
            all_spilled(e)
            for c in range(CT):
                e.wait_ge(dt_done, c + 1)
                nc.gpsimd.tensor_tensor(dtu[:, c], dt[:, c], xc[:, c], ALU.mult).then_inc(dtu_done, 1)
            e.wait_ge(dtu_done, CT)
            for s in range(2 * NS):
                e.wait_ge(row_copied, 2 * s + 1)
                for c in range(2):
                    j, ct = 2 * s + c, 2 * (s // NS) + c
                    if j >= 3:
                        e.wait_ge(scanned, j - 2)
                    nc.gpsimd.tensor_tensor(drive[j % 3], dtu[:, ct], b_row[s % 3], ALU.mult).then_inc(drive_done, 1)
                if s in (NS + 3, 2 * NS - 1):
                    for c in range(2):
                        ct = 2 * (s // (NS + 4)) + c
                        e.wait_ge(inner_hi, ct + 1)
                        pool_lo(e, inner[1][:, ct], dtu[:, ct], inner[0][:, ct], inner_lo)
            pool_layer_norm(e, 1)
            pool_attention(e)
            pool_layer_norm(e, 3)


INPUTS = [
    "L0_attn_a_x", "L0_attn_a_W_in", "L0_attn_a_conv_w", "L0_attn_a_conv_b", "L0_attn_a_W_x", "L0_attn_a_W_dt",
    "L0_attn_a_b_dt", "L0_attn_a_A_log", "L0_attn_a_D", "L0_attn_a_W_out", "L0_attn_b_Wq", "L0_attn_b_bq",
    "L0_attn_b_Wk", "L0_attn_b_bk", "L0_attn_b_Wv", "L0_attn_b_bv", "L0_attn_b_Wo", "L0_attn_b_bo",
    "L0_ffn_lut", "L0_ffn_gate_idx", "L0_ffn_up_idx", "L0_ffn_down_idx",
]


def kernel(**inputs):
    import concourse.bacc as bacc
    from concourse.bass_utils import run_bass_kernel_spmd

    nc = bacc.Bacc("TRN2", target_bir_lowering=False, num_devices=1)
    arrays, args = {}, []
    for name in INPUTS:
        a = np.asarray(inputs[name])
        shape = a.shape
        if name == "L0_attn_a_x":
            a = a.reshape(shape[-2:])
        if name.endswith("_idx"):
            a = a.T
        a = np.ascontiguousarray(a)
        arrays["in_" + name] = a
        args.append(nc.dram_tensor("in_" + name, list(a.shape), mybir.dt.from_np(a.dtype), kind="ExternalInput").ap())
    x_shape = np.asarray(inputs["L0_attn_a_x"]).shape
    out = nc.dram_tensor("out_x", list(x_shape[-2:]), F32, kind="ExternalOutput").ap()
    hybrid_block(nc, *args, out)
    got = run_bass_kernel_spmd(nc, [arrays], core_ids=[0])
    return got.results[0]["out_x"].reshape(x_shape)
```

```python
from contextlib import ExitStack

import numpy as np

import concourse.bass as bass
from concourse import mybir

ALU = mybir.AluOpType
ACT = mybir.ActivationFunctionType
F32 = mybir.dt.float32
F32R = mybir.dt.float32r
BF16 = mybir.dt.bfloat16
I32 = mybir.dt.int32
AX_X = mybir.AxisListType.X

P = 128
BANK = 512
SLAB = 256
EPS = 1e-5
MASKED = -2e38


class SbufPlan:

    def __init__(self, nc, start, end):
        self.nc, self.at, self.end = nc, start, end

    def tile(self, name, shape, dtype=F32):
        size = {F32: 4, F32R: 4, I32: 4, BF16: 2}[dtype]
        for n in shape[1:]:
            size *= n
        t = self.nc.alloc_sbuf_tensor_at(name, list(shape), dtype, offset=self.at)
        self.at += (size + 31) // 32 * 32
        assert self.at <= self.end, (name, self.at, self.end)
        return t

    def pair(self, name, shape):
        return self.tile(name + "_hi", shape, F32R), self.tile(name + "_lo", shape, F32R)


def hybrid_block(
    nc, x, W_in, conv_w, conv_b, W_x, W_dt, b_dt, A_log, D, W_out,
    Wq, bq, Wk, bk, Wv, bv, Wo, bo, lut, gate_idx_T, up_idx_T, down_idx_T, out,
):
    TOK, DM = x.shape
    DI = conv_b.shape[0]
    NS = A_log.shape[1]
    R = W_dt.shape[0]
    HD = Wq.shape[1]
    DH = P
    NH = HD // DH
    INTER = gate_idx_T.shape[1]
    NLUT = lut.shape[0]
    NT = TOK // P
    KD = DM // P
    CT = DI // P
    NB = TOK // BANK
    FM = (INTER + P - 1) // P
    FREM = INTER - (FM - 1) * P
    NP = NH // 2
    SCALE = float(1.0 / np.sqrt(np.float32(DH)))
    assert R == P and NT == 8 and KD == 2 and CT == 4 and NB == 2 and NS == 16 and NLUT == 16
    MW = [min(P, INTER - m * P) for m in range(FM)]

    with ExitStack() as ctx:
        sem = lambda name: ctx.enter_context(nc.semaphore(name))
        psum = ctx.enter_context(nc.psum_tensor("psum", [P, 8, BANK], F32))

        base = (nc.sbuf_base + 31) // 32 * 32
        top = nc.sbuf_usable_end // 32 * 32
        keep = SbufPlan(nc, base, top)
        ident = keep.tile("ident", [P, P])
        ident_r = keep.tile("ident_r", [P, P], F32R)
        ident_b = keep.tile("ident_b", [P, P], BF16)
        causal = SbufPlan(nc, top - 4 * P, top).tile("causal", [P, P])
        causal_b = keep.tile("causal_b", [P, P], BF16)
        half_neg = keep.tile("half_neg", [P, NT])
        ones_col = keep.tile("ones_col", [P, 1])
        stats = keep.tile("stats", [P, NT, 6])
        mean_var = keep.tile("mean_var", [P, NT, 2])
        var_eps = keep.tile("var_eps", [P, NT])
        rstd = keep.tile("rstd", [P, NT])
        convw = keep.tile("convw", [P, CT, 3])
        convw_half = keep.tile("convw_half", [P, CT, 3])
        convb = keep.tile("convb", [P, CT])
        convb_half = keep.tile("convb_half", [P, CT])
        bdt = keep.tile("bdt", [P, CT])
        dskip = keep.tile("dskip", [P, CT])
        alog = keep.tile("alog", [P, CT, NS])
        aneg = keep.tile("aneg", [P, CT, NS])
        carry = keep.tile("carry", [P, CT, NS])
        bq_t = keep.tile("bq_t", [P, NH])
        bk_t = keep.tile("bk_t", [P, NH])
        bv_t = keep.tile("bv_t", [P, NH])
        bo_row = keep.tile("bo_row", [P, DM])
        lut_row = keep.tile("lut_row", [P, NLUT])
        lut_step = keep.tile("lut_step", [P, NLUT // 2])
        res = keep.tile("res", [P, NT, DM])
        xn_at = keep.at
        xn = keep.tile("xn", [P, NT, DM])
        xnT_at = keep.at
        xnT = keep.pair("xnT", [P, KD, TOK])

        def cursor(at, end=top):
            return SbufPlan(nc, at, end)

        mp = cursor(keep.at)
        wx = mp.pair("wx", [P, CT, R + 2 * NS])
        wdt = mp.pair("wdt", [P, DI])
        wout = mp.pair("wout", [P, CT, DM])
        xc = mp.tile("xc", [P, CT, TOK])
        inner_hi_t = mp.tile("inner_hi", [P, CT, TOK], F32R)
        raws = mp.at
        inner = (inner_hi_t, mp.tile("inner_lo", [P, CT, TOK], F32R))
        rp = cursor(raws, mp.at)
        wx_raw = rp.tile("wx_raw", [P, CT, R + 2 * NS])
        wdt_raw = rp.tile("wdt_raw", [P, DI])
        wout_raw = rp.tile("wout_raw", [P, CT, DM])
        building = mp.at
        dtu = mp.tile("dtu", [P, CT, TOK])
        rings_at = mp.at
        mp.at += 8 * 4 * TOK
        rings_end = mp.at
        bp = cursor(building, mp.at)
        BW = INTER // 2
        idx_t = [bp.tile(f"idx{i}", [P, BW], I32) for i in range(2)]
        bits = [[bp.tile(f"bit{k}_{i}", [P, BW], I32) for k in range(4)] for i in range(2)]
        picked = [bp.tile(f"picked{i}", [P, BW]) for i in range(3)]
        picks = [[bp.tile(f"pick{k}_{i}", [P, BW]) for k in range(1, NLUT // 2)] for i in range(2)]
        pick = lambda b: [picked[b % 3]] + picks[b % 2]
        built = [bp.pair(f"built{i}", [P, BW]) for i in range(3)]
        bct = mp.pair("bct", [2 * NS, TOK])
        shared = mp.at
        pre = cursor(shared)
        win_raw = pre.tile("win_raw", [P, KD, 2 * DI])
        win = pre.pair("win", [P, KD, 2 * DI])
        taps = [pre.tile(f"taps{i}", [P, TOK]) for i in range(2)]
        tanh_xz = [pre.tile(f"tanh_xz{i}", [P, TOK]) for i in range(2)]
        sz2 = cursor(shared).tile("sz2", [P, CT, TOK])
        assert pre.at <= top - 4 * P
        dtin = cursor(xn_at).pair("dtin", [P, 1, TOK])
        softp = taps
        HALF = TOK // 2
        dt = cursor(xnT_at, keep.at).tile("dt", [P, CT, TOK])
        sp = cursor(rings_at, rings_end)
        b_row = [sp.tile(f"b_row{i}", [P, HALF])[:] for i in range(3)]
        c_row = [sp.tile(f"c_row{i}", [P, HALF])[:] for i in range(3)]
        decay = [sp.tile(f"decay{i}", [P, HALF])[:] for i in range(3)]
        drive = [sp.tile(f"drive{i}", [P, HALF])[:] for i in range(3)]
        state = [sp.tile(f"state{i}", [P, HALF])[:] for i in range(3)]
        weighted = [sp.tile("weighted0", [P, HALF])[:]]
        sp = cursor(xn_at + 4 * TOK, xnT_at)
        weighted += [sp.tile(f"weighted{i}", [P, HALF])[:] for i in (1, 2)]

        late = (top - 4 * (KD * 2 * INTER + FM * DM) * 2 - 64) // 32 * 32
        assert late >= shared
        fw = cursor(late)
        wgu = fw.pair("wgu", [P, KD, 2 * INTER])
        wdn = fw.pair("wdn", [P, FM, DM])
        fp = cursor(rings_at, late)
        f_tanh = [fp.tile(f"f_tanh{i}", [P, BANK]) for i in range(2)]
        f_gate = f_tanh
        f_prod = [fp.tile(f"f_prod{i}", [P, BANK]) for i in range(2)]
        hid = [fp.pair(f"hid{i}", [P, FM, BANK]) for i in range(2)]

        HTOK = TOK // NH
        HH = HALF // HTOK
        ap_ = cursor(keep.at, late)
        w_raw = ap_.tile("w_raw", [P, KD, 2 * DH])
        wk = ap_.pair("wk", [P, KD, 2 * DH])
        wv = ap_.pair("wv", [P, KD, 2 * DH])
        wo = ap_.pair("wo", [P, 2, DM])
        first = ap_.at
        oT = [ap_.pair(f"oT{i}", [P, 2, TOK]) for i in range(2)]
        wqp = cursor(first, ap_.at)
        wq_raw = [wqp.tile(f"wq_raw{i}", [P, KD, BANK]) for i in range(2)]
        wq = [wqp.pair(f"wq{i}", [P, KD, BANK]) for i in range(3)]
        assert ap_.at <= rings_at
        neg_max, row_sum, row_inv = (ap_.tile(n, [P, NH, NT]) for n in ("neg_max", "row_sum", "row_inv"))
        first = ap_.at
        q = [ap_.pair(f"q{i}", [P, TOK]) for i in range(2)]
        pT = [ap_.pair("pT0", [P, NT, SLAB])]
        qstage0 = cursor(first, ap_.at).tile("qstage0", [P, HH, NH, HTOK])
        kT = [ap_.pair(f"kT{i}", [P, TOK]) for i in range(2)]
        v2 = [ap_.pair(f"v2{i}", [P, NT, 2 * DH]) for i in range(2)]
        probs = [ap_.tile(f"probs{i}", [P, TOK]) for i in range(2)]
        qstage = [qstage0, cursor(late).tile("qstage1", [P, HH, NH, HTOK])]
        pT.append(cursor(top - 2 * 4 * NT * SLAB).pair("pT1", [P, NT, SLAB]))
        q_raw = [xn[:, i * NT // 2:(i + 1) * NT // 2].rearrange("p t c -> p (t c)").rearrange(
            "p (c t) -> p c t", c=NH) for i in range(2)]

        wgu_dram = [nc.dram_tensor(f"wgu_dram{i}", [P, KD, 2 * INTER], F32, kind="Internal").ap() for i in range(2)]
        wdn_dram = [nc.dram_tensor(f"wdn_dram{i}", [P, FM, DM], F32, kind="Internal").ap() for i in range(2)]

        q_dram = nc.dram_tensor("q_dram", [NH, P, NH * HTOK], F32, kind="Internal").ap()

        ld = {n: sem("ld_" + n) for n in (
            "x", "win", "small", "scan", "lut", "bias", "wx", "wdt", "wout", "idx0", "idx1",
            "wgu", "wdn", "w", "wq0", "wq1", "q0", "q1")}
        carried = sem("carried")
        q_start_stored, q_half_stored, q_end_stored = (
            sem(n) for n in ("q_start_stored", "q_half_stored", "q_end_stored"))
        wq_hi = sem("wq_hi")
        consts_made = sem("consts_made")
        ones_made = sem("ones_made")
        consts_cast = sem("consts_cast")
        out_stored = sem("out_stored")
        spilled = [sem(f"spilled{i}") for i in range(3)]
        dve_own = sem("dve_own")
        act_own = sem("act_own")
        pool_own = sem("pool_own")
        ln_stats, ln_mv, ln_rstd, ln_xn, ln_turned, ln_hi, ln_lo = (
            sem(n) for n in ("ln_stats", "ln_mv", "ln_rstd", "ln_xn", "ln_turned", "ln_hi", "ln_lo"))
        win_hi, win_x_lo, win_z_lo = sem("win_hi"), sem("win_x_lo"), sem("win_z_lo")
        mw_hi, mw_lo = sem("mw_hi"), sem("mw_lo")
        bits_done, act_picks, pool_picks, weight_picked, weight_hi, weight_lo = (
            sem(n) for n in ("bits_done", "act_picks", "pool_picks", "weight_picked", "weight_hi", "weight_lo"))
        small_done = sem("small_done")
        (xz_made, tap_mid, conv_done, tanh_done, gated, xc_hi, xc_lo, xd_made, xd_hi, xd_lo, dtp_made,
         softp_done, relu_done, dt_done, dtu_done, row_made, row_copied, decay_done, drive_done, scanned,
         weighed, y_added, y_read, inner_f, inner_hi, inner_a_lo, inner_b_lo, op_made, res1) = (
            sem(n) for n in (
                "xz_made", "tap_mid", "conv_done", "tanh_done", "gated", "xc_hi", "xc_lo", "xd_made", "xd_hi",
                "xd_lo", "dtp_made", "softp_done", "relu_done", "dt_done", "dtu_done", "row_made", "row_copied",
                "decay_done", "drive_done", "scanned", "weighed", "y_added", "y_read", "inner_f", "inner_hi",
                "inner_a_lo", "inner_b_lo", "op_made", "res1"))
        gu_made, f_tanhed, f_gated, f_mult, hid_hi, hid_lo, dn_made, f_res = (
            sem(n) for n in ("gu_made", "f_tanhed", "f_gated", "f_mult", "hid_hi", "hid_lo", "dn_made", "f_res"))
        (wq_split, w_split, q_hi, q_split, unit_made, unit_hi, unit_done, scored, max_done, exp_done, inv_done,
         normed, turned, pT_hi, pT_lo, pv_made, oT_hi, oT_lo, bo_added) = (
            sem(n) for n in (
                "wq_split", "w_split", "q_hi", "q_split", "unit_made", "unit_hi", "unit_done", "scored",
                "max_done", "exp_done", "inv_done", "normed", "turned", "pT_hi", "pT_lo", "pv_made", "oT_hi",
                "oT_lo", "bo_added"))

        x_t = x.rearrange("(t p) c -> p t c", p=P)
        out_t = out.rearrange("(t p) c -> p t c", p=P)

        f32 = lambda t: t.bitcast(F32)

        def product(e, acc, pairs, first=True, last=True):
            n = len(pairs)
            for i, ((wh, wl), (mh, ml)) in enumerate(pairs):
                e.matmul(acc, wh, mh, start=first and i == 0, stop=False)
                e.matmul(acc, wh, ml, start=False, stop=False)
                mm = e.matmul(acc, wl, mh, start=False, stop=last and i == n - 1)
            return mm

        def cut(pair, *ix):
            return tuple(t[ix] for t in pair)

        def split_hi_pool(e, hi, src):
            return e.tensor_scalar(hi, src, 1.0, 0.0, ALU.mult, ALU.add)

        def split_lo(e, lo, src, hi):
            return e.tensor_tensor(lo, src, f32(hi), ALU.subtract)

        builds = []
        for kt in range(KD):
            for g, src in enumerate((gate_idx_T, up_idx_T)):
                for c in range(0, INTER, BW):
                    builds.append((wgu_dram, (slice(None), kt, slice(g * INTER + c, g * INTER + c + BW)),
                                   src[kt * P:(kt + 1) * P, c:c + BW], P, BW))
        for m in range(FM):
            builds.append((wdn_dram, (slice(0, MW[m]), m, slice(None)), down_idx_T[m * P:m * P + MW[m], :], MW[m], DM))
        NBUILD = len(builds)
        PICKS = NLUT // 2
        act_share = [4 if build[3:] == (P, BW) else 2 for build in builds]
        act_upto = lambda b: sum(act_share[:b + 1])
        pool_upto = lambda b: PICKS * (b + 1) - act_upto(b)

        block = ctx.enter_context(nc.Block())

        def all_spilled(e):
            for i in range(3):
                e.wait_ge(spilled[i], 32 * ((NBUILD + 2 - i) // 3))

        def step_units(n):
            h, i = divmod(n, NT)
            r, st = h // 2, (h % 2) * NT + i
            units = []
            if i in (0, 2) and h + 1 < NH:
                units.append(("K", h + 1, i // 2))
            for t in {1: (0,), 3: (1,), 5: (2,), 7: (3,)}.get(i, ()):
                if st < NT and r >= 1:
                    units.append(("O", r - 1, t))
                if st >= NT and r + 1 < NP:
                    units.append(("V", r + 1, t))
            return units

        first_units = [("Q", a, c) for a in range(2) for c in range(NH)]
        first_units += [("K", 0, s) for s in range(NB)] + [("V", 0, t) for t in range(NT // 2)]
        last_units = [("O", NP - 1, t) for t in range(NT // 2)]
        all_units = list(first_units)
        units_at = {}
        for n in range(NH * NT):
            units_at[n] = step_units(n)
            all_units += units_at[n]
        all_units += last_units
        unit_no = {u: k for k, u in enumerate(all_units)}
        hi_no = {u: k for k, u in enumerate(u for u in all_units if u[0] in "KV")}
        wq_chunk = lambda u: u[1] * 4 + u[2] // 4

        loop_jobs = []
        for n in range(NH * NT):
            loop_jobs += units_at[n]
            if n % 2 == 0 and n:
                loop_jobs.append(n // 2 - 1)
        loop_jobs.append(NH * NT // 2 - 1)
        job_no = {job: m for m, job in enumerate(loop_jobs)}
        job_bank = lambda job: 6 + job_no[job] % 2

        def wait_job_bank(e, job):
            before = loop_jobs[job_no[job] - 2] if job_no[job] >= 2 else first_units[-1]
            if isinstance(before, int):
                e.wait_ge(oT_lo, before + 1)
            else:
                e.wait_ge(unit_done, unit_no[before] + 1)

        def unit_bank(k):
            u = all_units[k]
            if u in job_no:
                return job_bank(u)
            if k < 2 * NH:
                return k % 6
            if k < len(first_units):
                return 4 + k % 4
            return last_units.index(u)

        def wait_unit_bank(e, k):
            if all_units[k] in job_no:
                wait_job_bank(e, all_units[k])
            elif k < len(first_units):
                free = max((j + 1 for j in range(k) if unit_bank(j) == unit_bank(k)), default=0)
                if free:
                    e.wait_ge(unit_done, free)

        def groups(i):
            return [(b, min(b + 4, i + 1)) for b in range(0, i + 1, 4)]

        def turned_before(n):
            h, i = divmod(n, NT)
            return 12 * h + (i if i <= 4 else 4 + 2 * (i - 4))

        split_order = [("wk", 0), ("wv", 0)] + [(w, r + (w != "wo")) for r in range(NP) for w in ("wk", "wv", "wo")
                                                if r + (w != "wo") < NP]
        split_no = {k: 2 * n + 2 for n, k in enumerate(split_order)}

        def load_ffn_weights(e, f):
            for i in range(2):
                if f == 1 and i == 1:
                    e.wait_ge(pv_made, NH * NT // 2)
                e.dma_start(f32(wgu[i][:]), wgu_dram[i]).then_inc(ld["wgu"], 16)
            for i in range(2):
                e.dma_start(f32(wdn[i][:, 0:FM - 1]), wdn_dram[i][:, 0:FM - 1]).then_inc(ld["wdn"], 16)
                e.dma_start(f32(wdn[i][0:FREM, FM - 1]), wdn_dram[i][0:FREM, FM - 1]).then_inc(ld["wdn"], 16)

        def load_wq(e, k):
            if k >= 2:
                e.wait_ge(wq_split, k - 1)
            e.dma_start(wq_raw[k % 2][:], Wq[:, (k % 4) * BANK:(k % 4 + 1) * BANK].rearrange(
                "(k p) n -> p k n", p=P)).then_inc(ld[f"wq{k % 2}"], 16)

        def store_q(e, half, a, b, signal):
            e.wait_ge(unit_done, unit_no[("Q", half, NH - 1)] + 1)
            e.dma_start(q_dram.rearrange("h p n -> p h n")[:, half * HH + a:half * HH + b],
                        qstage[half][:, a:b].rearrange("p h c t -> p h (c t)")).then_inc(signal, 16)

        def load_q(e, h):
            if h < 2:
                e.wait_ge(q_start_stored, 16)
            else:
                e.wait_ge(q_half_stored if h < HH else q_end_stored, 16)
                e.wait_ge(q_split, 4 * (h - 1))
            e.dma_start(q_raw[h % 2].rearrange("p c t -> p (c t)"), q_dram[h]).then_inc(ld[f"q{h % 2}"], 16)

        def load_w(e, n):
            name, r = split_order[n]
            if n >= 1:
                e.wait_ge(w_split, 2 * n)
            cols = slice(r * 2 * DH, (r + 1) * 2 * DH)
            src = Wo[cols, :] if name == "wo" else (Wk if name == "wk" else Wv)[:, cols]
            e.dma_start(w_raw[:], src.rearrange("(k p) n -> p k n", p=P)).then_inc(ld["w"], 16)

        def load_indices(e, b):
            _, _, src, parts, cols = builds[b]
            e.dma_start(idx_t[b % 2][0:parts, 0:cols], src).then_inc(ld[f"idx{b % 2}"], 16)

        @block.sync
        def _(e):
            e.dma_start(res[:], x_t).then_inc(ld["x"], 16)
            e.dma_start(win_raw[:], W_in.rearrange("(k p) n -> p k n", p=P)).then_inc(ld["win"], 16)
            with nc.allow_non_contiguous_dma(reason="small vectors"):
                e.dma_start(lut_row[:], lut.rearrange("(o n) -> o n", o=1).broadcast_to([P, NLUT])).then_inc(ld["lut"], 16)
                load_indices(e, 0)
                e.dma_start(convw[:], conv_w.rearrange("(c p) o k -> p c (o k)", p=P)).then_inc(ld["small"], 16)
                e.dma_start(convb[:], conv_b.rearrange("(c p) -> p c", p=P)).then_inc(ld["small"], 16)
                load_indices(e, 1)
                e.dma_start(wx_raw[:], W_x.rearrange("(c p) n -> p c n", p=P)).then_inc(ld["wx"], 16)
                e.dma_start(wdt_raw[:], W_dt).then_inc(ld["wdt"], 16)
                e.dma_start(wout_raw[:], W_out.rearrange("(c p) n -> p c n", p=P)).then_inc(ld["wout"], 16)
                for t, v in ((bdt, b_dt), (dskip, D)):
                    e.dma_start(t[:], v.rearrange("(c p) -> p c", p=P)).then_inc(ld["scan"], 16)
                e.dma_start(alog[:], A_log.rearrange("(c p) s -> p c s", p=P)).then_inc(ld["scan"], 16)
                for t, v in ((bq_t, bq), (bk_t, bk), (bv_t, bv)):
                    e.dma_start(t[:], v.rearrange("(c p) -> p c", p=P)).then_inc(ld["bias"], 16)
                e.dma_start(bo_row[:], bo.rearrange("(o n) -> o n", o=1).broadcast_to([P, DM])).then_inc(ld["bias"], 16)
            for b in range(2, NBUILD + 3):
                if b < NBUILD:
                    e.wait_ge(bits_done, 4 * (b - 1))
                    load_indices(e, b)
                if b >= 3:
                    dram, where, _, parts, cols = builds[b - 3]
                    e.wait_ge(weight_lo, b - 2)
                    for i, t in enumerate(built[b % 3]):
                        e.dma_start(dram[i][where], f32(t[0:parts, 0:cols])).then_inc(spilled[b % 3], 16)
            all_spilled(e)
            e.wait_ge(dt_done, CT)
            load_ffn_weights(e, 0)
            e.wait_ge(op_made, NT)
            load_wq(e, 0)
            load_w(e, 0)
            load_wq(e, 1)
            load_w(e, 1)
            for k in range(2, 2 * NH // 4):
                load_wq(e, k)
            store_q(e, 0, 0, 2, q_start_stored)
            load_q(e, 0)
            load_q(e, 1)
            store_q(e, 0, 2, HH, q_half_stored)
            load_w(e, 2)
            store_q(e, 1, 0, HH, q_end_stored)
            load_q(e, 2)
            for n in range(3, len(split_order)):
                load_w(e, n)
                if n % 3 == 0 and 2 * (n // 3) + 1 < NH:
                    load_q(e, 2 * (n // 3) + 1)
                if n % 3 == 2 and 2 * (n // 3) + 2 < NH:
                    load_q(e, 2 * (n // 3) + 2)
            e.wait_ge(q_end_stored, 16)
            load_ffn_weights(e, 1)
            for i in range(NT):
                e.wait_ge(f_res, NT + i + 1)
                e.dma_start(out_t[:, i], res[:, i]).then_inc(out_stored, 16)
            e.wait_ge(out_stored, 16 * NT)

        def turn_normed(e, L, g):
            e.wait_ge(ln_xn, NT * L + 2 * g + 2)
            if g >= 2:
                e.wait_ge(ln_lo, 4 * L + g - 1)
            for t in range(2):
                for k in range(KD):
                    mm = e.transpose(psum[:, 6 + g % 2, (2 * t + k) * P:(2 * t + k + 1) * P],
                                     xn[:, 2 * g + t, k * P:(k + 1) * P], ident[:])
            mm.then_inc(ln_turned, 1)

        def pe_mamba(e):
            slot = lambda n: 2 * (n % 3)
            for m in range(2 * CT):
                if m in (0, CT):
                    e.wait_ge(win_hi, 1 + m // CT)
                    e.wait_ge(win_z_lo if m else win_x_lo, 1)
                if 3 <= m < 3 + CT:
                    e.wait_ge(conv_done, m - 2)
                if m >= 3 + CT:
                    e.wait_ge(gated, m - 2)
                for n in range(NB):
                    if m == 0:
                        e.wait_ge(ln_lo, 2 * n + 2)
                    mm = product(e, psum[:, slot(m) + n], [
                        (cut(win, slice(None), k, slice(m * P, (m + 1) * P)),
                         cut(xnT, slice(None), k, slice(n * BANK, (n + 1) * BANK))) for k in range(KD)])
                mm.then_inc(xz_made, 1)
            e.wait_ge(mw_hi, 2)
            e.wait_ge(mw_lo, 2)
            for m, (a, b) in enumerate(((0, R), (R, R + 2 * NS))):
                if m == 0:
                    e.wait_ge(gated, 2 * CT - 2)
                    e.wait_ge(xc_lo, CT)
                else:
                    e.wait_ge(gated, 2 * CT - 1)
                for n in range(NB):
                    mm = product(e, psum[0:b - a, slot(2 * CT + m) + n], [
                        (cut(wx, slice(None), c, slice(a, b)),
                         cut(inner, slice(None), c, slice(n * BANK, (n + 1) * BANK))) for c in range(CT)])
                mm.then_inc(xd_made, 1)
            for c in range(CT):
                e.wait_ge(xd_lo, 1)
                if c == 0:
                    e.wait_ge(gated, 2 * CT)
                elif c <= 2:
                    e.wait_ge(xd_lo, c)
                else:
                    e.wait_ge(relu_done, 1)
                    e.wait_ge(softp_done, 1)
                for n in range(NB):
                    mm = product(e, psum[:, slot(2 * CT + 2 + c) + n], [
                        (cut(wdt, slice(None), slice(c * P, (c + 1) * P)),
                         dtin_cut(n))])
                mm.then_inc(dtp_made, 1)

            def row(b):
                s, w = divmod(b, 2)
                half = s // NS
                if b == 0:
                    e.wait_ge(relu_done, CT)
                    e.wait_ge(softp_done, CT)
                    e.wait_ge(xd_lo, 2)
                if b >= 2:
                    e.wait_ge(row_copied, b - 1)
                col = w * NS + s % NS
                for part in range(2):
                    mm = e.matmul(psum[:, 4 + w], ident_r[0:2 * NS, col:col + 1].broadcast_to([2 * NS, P]),
                                  bct[part][:, half * HALF:(half + 1) * HALF], start=part == 0, stop=part == 1)
                mm.then_inc(row_made, 1)

            e.wait_ge(consts_cast, 3)
            for b in range(6):
                row(b)
            for j in range(2 * CT * NS):
                s, c = divmod(j, CT)
                e.wait_ge(weighed, j + 1)
                if s == NS:
                    e.wait_ge(y_read, c + 1)
                e.matmul(psum[:, c], ident[:], weighted[j % 3], start=s % NS == 0,
                         stop=s % NS == NS - 1).then_inc(y_added, 1)
                if c % 2 and s + 3 < 2 * NS:
                    row(2 * s + 6 + c // 2)
                if c == CT - 1 and NS + 4 <= s < NS + 8:
                    way_out(e, s - NS - 4)
                if c == CT - 1 and s == NS + 10:
                    turn_normed(e, 1, 0)
                    turn_normed(e, 1, 1)

        def way_out(e, i):
            if i == 0:
                e.wait_ge(mw_hi, 3)
                e.wait_ge(mw_lo, 3)
                e.wait_ge(inner_a_lo, CT)
            if i == 4:
                e.wait_ge(inner_a_lo, CT + 2)
                e.wait_ge(inner_b_lo, 2)
            if i in (4, 5):
                e.wait_ge(ln_lo, 4 + i - 3)
            elif i >= 2:
                e.wait_ge(res1, i - 1)
            mm = product(e, psum[:, 6 + i % 2, 0:DM], [
                (cut(inner, slice(None), c, slice(i * P, (i + 1) * P)), cut(wout, slice(None), c, slice(None)))
                for c in range(CT)])
            mm.then_inc(op_made, 1)

        def dtin_cut(n):
            return tuple(t[:, 0, n * BANK:(n + 1) * BANK] for t in dtin)

        def f_slot(k):
            return 2 * ((k + 2) % 3)

        def pe_ffn(e, f):
            Q = 2 * FM

            def gate_up(k):
                n, m = divmod(k, FM)
                if k >= 3:
                    e.wait_ge(f_mult, Q * f + k - 2)
                if m == 0:
                    e.wait_ge(ln_lo, 4 * (2 * f + 1) + 2 * n + 2)
                for g in range(2):
                    mm = product(e, psum[0:MW[m], f_slot(k) + g], [
                        (cut(wgu, slice(None), kt, slice(g * INTER + m * P, g * INTER + m * P + MW[m])),
                         cut(xnT, slice(None), kt, slice(n * BANK, (n + 1) * BANK))) for kt in range(KD)])
                mm.then_inc(gu_made, 1)

            def down(i):
                n = i // 4
                e.wait_ge(hid_lo, Q * f + (n + 1) * FM)
                if i >= 2:
                    e.wait_ge(f_res, NT * f + i - 1)
                mm = product(e, psum[:, 6 + i % 2, 0:DM], [
                    (cut(hid[n], slice(0, MW[m]), m, slice((i % 4) * P, (i % 4 + 1) * P)),
                     cut(wdn, slice(0, MW[m]), m, slice(None))) for m in range(FM)])
                mm.then_inc(dn_made, 1)

            e.wait_ge(ld["wgu"], 32 * (f + 1))
            for k in range(FM + 2):
                if f == 0 and k == 0:
                    e.wait_ge(row_copied, 4 * NS)
                if f == 0 and k in (1, 2):
                    e.wait_ge(y_read, CT + 2 * k)
                gate_up(k)
                if f == 0 and k == 2:
                    for i in range(4, NT):
                        way_out(e, i)
                if f == 0 and k == 3:
                    turn_normed(e, 1, 2)
                    turn_normed(e, 1, 3)
            e.wait_ge(ld["wdn"], 64 * (f + 1))
            for i in range(4):
                down(i)
            for k in range(FM + 2, Q):
                gate_up(k)
                if f == 0 and k == Q - 1:
                    turn_normed(e, 2, 0)
                    turn_normed(e, 2, 1)
            for i in range(4, NT):
                if f == 0 and i < 6:
                    e.wait_ge(ln_lo, 8 + i - 3)
                down(i)

        def pe_attention(e):
            def unit(u):
                kind, a, b = u
                k = unit_no[u]
                acc = psum[:, unit_bank(k)]
                wait_unit_bank(e, k)
                if kind in "QKV":
                    e.wait_ge(ln_lo, 8 + (2 * a + 2 if kind == "Q" else 4))
                if kind == "Q":
                    e.wait_ge(wq_split, wq_chunk(u) + 1)
                    mm = product(e, acc, [
                        (cut(wq[wq_chunk(u) % 3], slice(None), kt, slice((b % 4) * P, (b % 4 + 1) * P)),
                         cut(xnT, slice(None), kt, slice(a * HALF, (a + 1) * HALF))) for kt in range(KD)])
                elif kind == "K":
                    e.wait_ge(w_split, split_no[("wk", a // 2)])
                    mm = product(e, acc, [
                        (cut(wk, slice(None), kt, slice((a % 2) * P, (a % 2 + 1) * P)),
                         cut(xnT, slice(None), kt, slice(b * BANK, (b + 1) * BANK))) for kt in range(KD)])
                elif kind == "V":
                    e.wait_ge(w_split, split_no[("wv", a)])
                    for t in range(2):
                        mm = product(e, acc[:, t * SLAB:(t + 1) * SLAB], [
                            (cut(xnT, slice(None), kt, slice((2 * b + t) * P, (2 * b + t + 1) * P)),
                             cut(wv, slice(None), kt, slice(None))) for kt in range(KD)])
                else:
                    e.wait_ge(w_split, split_no[("wo", a)])
                    if b == 0:
                        e.wait_ge(oT_lo, 8 * (a + 1))
                    for t in range(2):
                        mm = product(e, acc[:, t * SLAB:(t + 1) * SLAB], [
                            (cut(oT[a % 2], slice(None), hh, slice((2 * b + t) * P, (2 * b + t + 1) * P)),
                             cut(wo, slice(None), hh, slice(None))) for hh in range(2)])
                mm.then_inc(unit_made, 1)

            def scores(n):
                h, i = divmod(n, NT)
                if n >= 2:
                    e.wait_ge(exp_done, n - 1)
                e.wait_ge(q_split, 4 * h + i // 2 + 1)
                if i == 0:
                    e.wait_ge(unit_done, unit_no[("K", h, NB - 1)] + 1)
                width = (i + 1) * P
                for b in range(0, width, BANK):
                    w = min(BANK, width - b)
                    acc = psum[:, 2 * (n % 2) + b // BANK]
                    diagonal = b + w == width
                    mm = product(e, acc[:, 0:w], [
                        (cut(q[h % 2], slice(None), slice(i * P, (i + 1) * P)),
                         cut(kT[h % 2], slice(None), slice(b, b + w)))], last=not diagonal)
                    if diagonal:
                        mm = e.matmul(acc[:, w - P:w], ident_b[:], causal_b[:], start=False, stop=True)
                mm.then_inc(scored, 1)

            def turn(n):
                h, i = divmod(n, NT)
                e.wait_ge(normed, n + 1)
                if n == 0:
                    e.wait_ge(unit_done, len(first_units))
                for g, (a, b) in enumerate(groups(i)):
                    t = turned_before(n) + g
                    if t >= 2:
                        e.wait_ge(pT_lo, t - 1)
                    for j in range(a, b):
                        mm = e.transpose(psum[:, 4 + t % 2, (j - a) * P:(j - a + 1) * P],
                                         probs[n % 2][:, j * P:(j + 1) * P], ident[:])
                    mm.then_inc(turned, 1)

            def values(n):
                h, i = divmod(n, NT)
                s = n // 2
                e.wait_ge(pT_lo, turned_before(n + 1))
                if i == 1:
                    e.wait_ge(unit_done, unit_no[("V", h // 2, NT // 2 - 1)] + 1)
                wait_job_bank(e, s)
                acc = psum[:, job_bank(s), 0:SLAB]
                pT_pair = pT[s % 2]
                vh = lambda j: cut(v2[h // 2 % 2], slice(None), j, slice((h % 2) * DH, (h % 2 + 1) * DH))
                product(e, acc, [(vh(j), cut(pT_pair, slice(None), j, slice(None))) for j in range(i)], last=False)
                mm = product(e, acc[:, P:SLAB], [(vh(i), cut(pT_pair, slice(None), i, slice(P, SLAB)))], first=False)
                mm.then_inc(pv_made, 1)

            for k, u in enumerate(first_units):
                unit(u)
                if k in (1, 3):
                    turn_normed(e, 2, 2 + k // 2)
            scores(0)
            scores(1)
            for n in range(NH * NT):
                if n + 2 < NH * NT:
                    scores(n + 2)
                turn(n)
                for u in units_at[n]:
                    unit(u)
                if n % 2 == 0 and n:
                    values(n - 1)
            values(NH * NT - 1)
            for t, u in enumerate(last_units):
                unit(u)
                if t >= 2:
                    turn_normed(e, 3, t - 2)
            turn_normed(e, 3, 2)
            turn_normed(e, 3, 3)

        @block.tensor
        def _(e):
            e.wait_ge(consts_made, 2)
            for g in range(NT // 2):
                turn_normed(e, 0, g)
            pe_mamba(e)
            pe_ffn(e, 0)
            pe_attention(e)
            pe_ffn(e, 1)

        def turn_views(g):
            src = psum[:, 6 + g % 2].rearrange("p (t k c) -> p t k c", t=2, k=KD)
            dst = [t[:, :, g * 2 * P:(g + 1) * 2 * P].rearrange("p k (t c) -> p t k c", t=2) for t in xnT]
            return src, dst

        def turned_high(e, L, g):
            e.wait_ge(ln_turned, 4 * L + g + 1)
            src, dst = turn_views(g)
            nc.scalar.activation(dst[0], src, ACT.Copy).then_inc(ln_hi, 1)

        def act_layer_norm(e, L):
            for g in range(NT // 2):
                turned_high(e, L, g)

        def act_mamba(e):
            slot = lambda n: 2 * (n % 3)
            two = lambda n: psum[:, slot(n):slot(n) + 2].rearrange("p a b -> p (a b)")

            def tap(m):
                e.wait_ge(xz_made, m + 1)
                if m >= 2:
                    e.wait_ge(gated, m - 1)
                nc.scalar.activation(taps[m % 2][:], two(m), ACT.Identity, bias=convb_half[:, m:m + 1],
                                     scale=convw_half[:, m, 1:2]).then_inc(tap_mid, 1)

            def tanh(m):
                if m >= 2:
                    e.wait_ge(gated, m - 1)
                if m < CT:
                    e.wait_ge(conv_done, m + 1)
                    nc.scalar.activation(tanh_xz[m % 2][:], taps[m % 2][:], ACT.Tanh).then_inc(tanh_done, 1)
                else:
                    e.wait_ge(xz_made, m + 1)
                    nc.scalar.activation(tanh_xz[m % 2][:], two(m), ACT.Tanh, scale=0.5).then_inc(tanh_done, 1)

            def xc_high(m):
                e.wait_ge(gated, m + 1)
                nc.scalar.activation(inner[0][:, m], xc[:, m], ACT.Copy).then_inc(xc_hi, 1)

            def x_dbl_high(m):
                e.wait_ge(xd_made, m + 1)
                if m == 0:
                    nc.scalar.activation(dtin[0][:, 0, 0:TOK], two(2 * CT), ACT.Copy).then_inc(xd_hi, 1)
                else:
                    nc.scalar.activation(bct[0][:], two(2 * CT + 1)[0:2 * NS], ACT.Copy).then_inc(xd_hi, 1)

            def softplus_part(c):
                if c == 0:
                    e.wait_ge(ld["scan"], 48)
                    e.wait_ge(gated, 2 * CT)
                e.wait_ge(dtp_made, c + 1)
                if c >= 2:
                    e.wait_ge(dt_done, c - 1)
                t = softp[c % 2]
                nc.scalar.activation(t[:], two(2 * CT + 2 + c), ACT.Abs, bias=bdt[:, c:c + 1]).then_inc(act_own, 1)
                e.wait_ge(act_own, 2 * c + 1)
                nc.scalar.activation(t[:], t[:], ACT.Exp, scale=-1.0).then_inc(act_own, 1)
                e.wait_ge(act_own, 2 * c + 2)
                nc.scalar.activation(t[:], t[:], ACT.Ln, bias=ones_col[:]).then_inc(softp_done, 1)

            e.wait_ge(small_done, 2)
            e.wait_ge(ones_made, 1)
            for b in range(NBUILD):
                act_build(e, b)
                if b < CT:
                    tap(b)
                if 1 <= b < CT + 1:
                    tanh(b - 1)
                if 2 <= b < CT + 2:
                    xc_high(b - 2)
                for m in {CT + 1: (4,), CT + 2: (5,), CT + 3: (6, 7)}.get(b, ()):
                    tanh(m)
                if b == 2 * CT:
                    x_dbl_high(0)
                if b == 2 * CT + 1:
                    x_dbl_high(1)
                    nc.scalar.preload_act_table_set("natural_log_exp_and_others")
                if NBUILD - CT - 1 <= b < NBUILD - 1:
                    softplus_part(b - NBUILD + CT + 1)
            weight_high(e, NBUILD - 1)
            e.wait_ge(ld["scan"], 48)
            nc.scalar.activation(aneg[:], alog[:], ACT.Exp).then_inc(act_own, 1)

            def row(b):
                s, w = divmod(b, 2)
                e.wait_ge(row_made, b + 1)
                if s >= 3:
                    e.wait_ge(drive_done if w == 0 else weighed, CT * (s - 2))
                nc.scalar.activation((b_row, c_row)[w][s % 3], psum[:, 4 + w], ACT.Copy).then_inc(row_copied, 1)

            def decay_of(j):
                s, c = divmod(j, CT)
                half = s // NS
                if j >= 3:
                    e.wait_ge(scanned, j - 2)
                nc.scalar.activation(decay[j % 3], dt[:, c, half * HALF:(half + 1) * HALF], ACT.Exp,
                                     scale=aneg[:, c, s % NS:s % NS + 1]).then_inc(decay_done, 1)

            def carry_state(j):
                s, c = divmod(j, CT)
                e.wait_ge(scanned, j + 1)
                nc.scalar.activation(carry[:, c, s:s + 1], state[j % 3][:, HALF - 1:HALF],
                                     ACT.Copy).then_inc(carried, 1)

            e.wait_ge(dtu_done, 1)
            for b in range(4):
                row(b)
            e.wait_ge(small_done, 3)
            decay_of(0)
            decay_of(1)
            for j in range(2 * CT * NS):
                s, c = divmod(j, CT)
                if c % 2 and s + 2 < 2 * NS:
                    row(2 * s + 4 + c // 2)
                if 1 <= j <= CT * NS:
                    carry_state(j - 1)
                if j + 2 < 2 * CT * NS:
                    decay_of(j + 2)
                if s in (NS + 2, NS + 3) and c % 2:
                    inner_high(e, 2 * (s - NS - 2) + c // 2, 0)
                if s == NS + 11 and c == 0:
                    turned_high(e, 1, 0)
                    turned_high(e, 1, 1)
            for c in range(CT):
                inner_high(e, c, 1)

        def inner_high(e, c, half):
            e.wait_ge(inner_f, CT * half + c + 1)
            cols = slice(half * HALF, (half + 1) * HALF)
            nc.scalar.activation(inner[0][:, c, cols], dtu[:, c, cols], ACT.Copy).then_inc(inner_hi, 1)

        def act_build(e, b):
            _, _, _, parts, cols = builds[b]
            a = lambda t: t[0:parts, 0:cols]
            e.wait_ge(bits_done, 4 * b + 1)
            if b >= 2:
                e.wait_ge(weight_picked, 7 * (b - 1))
            if b >= 3:
                e.wait_ge(weight_lo, b - 2)
            for k in range(act_share[b]):
                nc.scalar.activation(a(pick(b)[k]), a(bits[b % 2][0]), ACT.Identity,
                                     bias=lut_row[0:parts, 2 * k:2 * k + 1],
                                     scale=lut_step[0:parts, k:k + 1]).then_inc(act_picks, 1)
            if b >= 1:
                weight_high(e, b - 1)

        def weight_high(e, b):
            _, _, _, parts, cols = builds[b]
            e.wait_ge(weight_picked, 7 * (b + 1))
            if b >= 3:
                e.wait_ge(spilled[b % 3], 32 * (b // 3))
            nc.scalar.activation(built[b % 3][0][0:parts, 0:cols], picked[b % 3][0:parts, 0:cols],
                                 ACT.Copy).then_inc(weight_hi, 1)

        def act_ffn(e, f):
            Q = 2 * FM
            for k in range(Q):
                n, m = divmod(k, FM)
                w = MW[m]
                e.wait_ge(gu_made, Q * f + k + 1)
                if k >= 2:
                    e.wait_ge(f_mult, Q * f + k - 1)
                nc.scalar.activation(f_tanh[k % 2][0:w], psum[0:w, f_slot(k)], ACT.Tanh,
                                     scale=0.5).then_inc(f_tanhed, 1)
                if k >= 1:
                    hid_high(e, f, k - 1)
                if f == 0 and k == 3:
                    turned_high(e, 1, 2)
                    turned_high(e, 1, 3)
                if f == 0 and k == Q - 1:
                    turned_high(e, 2, 0)
                    turned_high(e, 2, 1)
            hid_high(e, f, Q - 1)

        def hid_high(e, f, k):
            n, m = divmod(k, FM)
            e.wait_ge(f_mult, 2 * FM * f + k + 1)
            nc.scalar.activation(hid[n][0][0:MW[m], m], f_prod[k % 2][0:MW[m]], ACT.Copy,
                                 scale=0.5).then_inc(hid_hi, 1)

        def unit_target(u, part):
            kind, a, b = u
            if kind == "K":
                return kT[a % 2][part][:, b * BANK:(b + 1) * BANK]
            return v2[a % 2][part][:, 2 * b:2 * b + 2].rearrange("p t c -> p (t c)")

        def act_attention(e):
            def unit(u):
                kind, a, b = u
                if kind not in "KV":
                    return
                k = unit_no[u]
                e.wait_ge(unit_made, k + 1)
                acc = psum[:, unit_bank(k)]
                if kind == "K":
                    nc.scalar.activation(unit_target(u, 0), acc, ACT.Identity,
                                         bias=bk_t[:, a:a + 1]).then_inc(unit_hi, 1)
                else:
                    nc.scalar.activation(unit_target(u, 0), acc, ACT.Copy).then_inc(unit_hi, 1)

            def exp(n):
                h, i = divmod(n, NT)
                e.wait_ge(max_done, n + 1)
                if n >= 2:
                    e.wait_ge(turned, turned_before(n - 1))
                nc.scalar.activation(probs[n % 2][:, 0:(i + 1) * P],
                                     psum[:, 2 * (n % 2):2 * (n % 2) + 2].rearrange("p a b -> p (a b)")[:, 0:(i + 1) * P],
                                     ACT.Exp, bias=neg_max[:, h, i:i + 1],
                                     accum_out=row_sum[:, h, i:i + 1]).then_inc(exp_done, 1)

            def turned_hi(n):
                h, i = divmod(n, NT)
                if n >= 4:
                    e.wait_ge(pv_made, n // 2 - 1)
                for g, (a, b) in enumerate(groups(i)):
                    t = turned_before(n) + g
                    e.wait_ge(turned, t + 1)
                    dst, src = turned_views(n, t, a, b)
                    nc.scalar.activation(dst[0], src, ACT.Copy).then_inc(pT_hi, 1)

            def value_hi(n):
                s = n // 2
                e.wait_ge(pv_made, s + 1)
                dst, src = value_views(s)
                nc.scalar.activation(dst[0], src, ACT.Identity,
                                     bias=bv_t[:, n // NT:n // NT + 1]).then_inc(oT_hi, 1)

            turned_high(e, 2, 2)
            turned_high(e, 2, 3)
            for k in range(3, 2 * NH // 4):
                e.wait_ge(ld[f"wq{k % 2}"], 16 * (k // 2 + 1))
                e.wait_ge(wq_split, k)
                e.wait_ge(unit_made, unit_no[("Q", (k - 3) // 4, 4 * ((k - 3) % 4) + 3)] + 1)
                nc.scalar.activation(wq[k % 3][0][:], wq_raw[k % 2][:], ACT.Copy).then_inc(wq_hi, 1)
            e.wait_ge(ld["bias"], 64)
            for u in first_units:
                unit(u)
            exp(0)
            exp(1)
            for n in range(NH * NT):
                if n in (0, 2):
                    e.wait_ge(q_half_stored if n == 0 else q_end_stored, 16)
                turned_hi(n)
                if n + 2 < NH * NT:
                    exp(n + 2)
                for u in units_at[n]:
                    unit(u)
                if n % 2 == 0 and n:
                    value_hi(n - 1)
            value_hi(NH * NT - 1)

        def turned_views(n, t, a, b):
            c = (n % 2) * P
            dst = [p[:, a:b, c:c + P] for p in pT[n // 2 % 2]]
            src = psum[:, 4 + t % 2, 0:(b - a) * P].rearrange("p (j c) -> p j c", c=P)
            return dst, src

        def value_views(s):
            h, g = divmod(s, NT // 2)
            dst = [t[:, h % 2, g * SLAB:(g + 1) * SLAB] for t in oT[h // 2 % 2]]
            return dst, psum[:, job_bank(s), 0:SLAB]

        @block.scalar
        def _(e):
            e.wait_ge(ld["win"], 16)
            for cols in (slice(0, DI), slice(DI, 2 * DI)):
                nc.scalar.activation(win[0][:, :, cols], win_raw[:, :, cols], ACT.Copy).then_inc(win_hi, 1)
            act_layer_norm(e, 0)
            e.wait_ge(ld["wx"], 16)
            nc.scalar.activation(wx[0][:], wx_raw[:], ACT.Copy).then_inc(mw_hi, 1)
            e.wait_ge(ld["wdt"], 16)
            nc.scalar.activation(wdt[0][:], wdt_raw[:], ACT.Copy).then_inc(mw_hi, 1)
            e.wait_ge(ld["wout"], 16)
            nc.scalar.activation(wout[0][:], wout_raw[:], ACT.Copy).then_inc(mw_hi, 1)
            act_mamba(e)
            nc.scalar.preload_act_table_set("exp_and_others")
            act_ffn(e, 0)
            act_attention(e)
            act_layer_norm(e, 3)
            act_ffn(e, 1)

        def ln_statistics(e, L, g, ready):
            for i in (2 * g, 2 * g + 1):
                e.wait_ge(*ready(i))
                nc.vector.bn_stats(stats[:, i], res[:, i]).then_inc(ln_stats, 1)
            for i in (2 * g, 2 * g + 1):
                e.wait_ge(ln_stats, NT * L + i + 1)
                nc.vector.bn_aggr(mean_var[:, i], stats[:, i]).then_inc(ln_mv, 1)

        def ln_normalise(e, L, g):
            e.wait_ge(ln_rstd, 4 * L + g + 1)
            for i in (2 * g, 2 * g + 1):
                nc.vector.tensor_scalar(xn[:, i], res[:, i], mean_var[:, i, 0:1], rstd[:, i:i + 1],
                                        ALU.subtract, ALU.mult).then_inc(ln_xn, 1)

        def dve_layer_norm(e, L, ready, residual=lambda i: None):
            for g in range(NT // 2 + 2):
                if g < NT // 2:
                    residual(2 * g)
                    residual(2 * g + 1)
                    ln_statistics(e, L, g, ready)
                if 1 <= g <= NT // 2:
                    ln_normalise(e, L, g - 1)
                if g >= 2:
                    turned_low(e, L, g - 2)

        def turned_low(e, L, g):
            e.wait_ge(ln_hi, 4 * L + g + 1)
            src, dst = turn_views(g)
            nc.vector.tensor_tensor(dst[1], src, f32(dst[0]), ALU.subtract).then_inc(ln_lo, 1)

        def dve_bits(e, b):
            dram, where, src, parts, cols = builds[b]
            a = lambda t: t[0:parts, 0:cols]
            e.wait_ge(ld[f"idx{b % 2}"], 16 * (b // 2 + 1))
            if b >= 2:
                e.wait_ge(weight_picked, 7 * (b - 1))
                e.wait_ge(act_picks, act_upto(b - 2))
                e.wait_ge(pool_picks, pool_upto(b - 2))
            for k, t in enumerate(bits[b % 2]):
                nc.vector.tensor_single_scalar(a(t), a(idx_t[b % 2]), 1 << k, ALU.bitwise_and).then_inc(bits_done, 1)

        def dve_build(e, b):
            if b + 1 < NBUILD:
                dve_bits(e, b + 1)
            dram, where, src, parts, cols = builds[b]
            a = lambda t: t[0:parts, 0:cols]
            pk, bt = pick(b), bits[b % 2]
            e.wait_ge(act_picks, act_upto(b))
            e.wait_ge(pool_picks, pool_upto(b))
            e.wait_ge(bits_done, 4 * (b + 1))
            n = 0
            for level, step in ((1, 1), (2, 2), (3, 4)):
                if n:
                    e.wait_ge(weight_picked, 7 * b + n)
                for k in range(0, PICKS, 2 * step):
                    nc.vector.copy_predicated(a(pk[k]), a(bt[level]), a(pk[k + step])).then_inc(weight_picked, 1)
                    n += 1

        def dve_mamba(e):
            slot = lambda n: 2 * (n % 3)
            two = lambda n: psum[:, slot(n):slot(n) + 2].rearrange("p a b -> p (a b)")

            def conv(m):
                t = taps[m % 2]
                e.wait_ge(tap_mid, m + 1)
                nc.vector.scalar_tensor_tensor(out=t[:, 1:TOK], in0=two(m)[:, 0:TOK - 1], scalar=convw_half[:, m, 0:1],
                                               in1=t[:, 1:TOK], op0=ALU.mult, op1=ALU.add).then_inc(dve_own, 1)
                own[0] += 1
                e.wait_ge(dve_own, own[0])
                nc.vector.scalar_tensor_tensor(out=t[:, 0:TOK - 1], in0=two(m)[:, 1:TOK], scalar=convw_half[:, m, 2:3],
                                               in1=t[:, 0:TOK - 1], op0=ALU.mult, op1=ALU.add).then_inc(conv_done, 1)

            def gate(m):
                e.wait_ge(tanh_done, m + 1)
                if m >= CT + 2:
                    e.wait_ge(xz_made, 2 * CT)
                src = taps[m % 2][:] if m < CT else two(m)
                dst = xc[:, m] if m < CT else sz2[:, m - CT]
                nc.vector.scalar_tensor_tensor(out=dst, in0=tanh_xz[m % 2][:], scalar=1.0, in1=src,
                                               op0=ALU.add, op1=ALU.mult).then_inc(gated, 1)

            def x_dbl_low(m):
                e.wait_ge(xd_hi, m + 1)
                if m == 0:
                    nc.vector.tensor_tensor(dtin[1][:, 0, 0:TOK], two(2 * CT), f32(dtin[0][:, 0, 0:TOK]),
                                            ALU.subtract).then_inc(xd_lo, 1)
                else:
                    nc.vector.tensor_tensor(bct[1][:], two(2 * CT + 1)[0:2 * NS], f32(bct[0][:]),
                                            ALU.subtract).then_inc(xd_lo, 1)

            def relu_part(c):
                e.wait_ge(dtp_made, c + 1)
                e.wait_ge(act_own, 2 * c + 1)
                nc.vector.tensor_scalar(dt[:, c], two(2 * CT + 2 + c), bdt[:, c:c + 1], 0.0,
                                        ALU.add, ALU.max).then_inc(relu_done, 1)

            def add_parts(c):
                e.wait_ge(softp_done, c + 1)
                e.wait_ge(relu_done, c + 1)
                nc.vector.tensor_tensor(dt[:, c], dt[:, c], softp[c % 2][:], ALU.add).then_inc(dt_done, 1)

            for b in range(NBUILD):
                dve_build(e, b)
                if b < CT:
                    conv(b)
                if 1 <= b < CT + 1:
                    gate(b - 1)
                for m in {CT + 1: (4,), CT + 2: (5,), CT + 3: (6, 7)}.get(b, ()):
                    gate(m)
                if b == 2 * CT:
                    x_dbl_low(0)
                if b == 2 * CT + 1:
                    x_dbl_low(1)
                    e.wait_ge(ld["scan"], 48)
                if NBUILD - CT - 1 <= b < NBUILD - 1:
                    relu_part(b - NBUILD + CT + 1)
                if b >= NBUILD - CT:
                    add_parts(b - NBUILD + CT)
            e.wait_ge(act_own, 2 * CT + 1)
            nc.vector.tensor_scalar(aneg[:], aneg[:], -1.0, None, ALU.mult).then_inc(small_done, 1)

            def scan(j):
                s, c = divmod(j, CT)
                e.wait_ge(decay_done, j + 1)
                e.wait_ge(drive_done, j + 1)
                if j >= 3:
                    e.wait_ge(weighed, j - 2)
                if 3 <= j < CT * NS + 3:
                    e.wait_ge(carried, j - 2)
                start = 0.0
                if s >= NS:
                    e.wait_ge(carried, j - CT * NS + 1)
                    start = carry[:, c, s - NS:s - NS + 1]
                nc.vector.tensor_tensor_scan(state[j % 3], decay[j % 3], drive[j % 3], start,
                                             ALU.mult, ALU.add).then_inc(scanned, 1)

            def weigh(j):
                e.wait_ge(scanned, j + 1)
                e.wait_ge(row_copied, 2 * (j // CT) + 2)
                if j >= 3:
                    e.wait_ge(y_added, j - 2)
                nc.vector.tensor_tensor(weighted[j % 3], state[j % 3], c_row[j // CT % 3],
                                        ALU.mult).then_inc(weighed, 1)

            def dt_times_x(c, half):
                cols = slice(half * HALF, (half + 1) * HALF)
                e.wait_ge(dt_done, c + 1)
                nc.vector.tensor_tensor(dtu[:, c, cols], dt[:, c, cols], xc[:, c, cols], ALU.mult).then_inc(dtu_done, 1)

            def skip(c, half):
                cols = slice(half * HALF, (half + 1) * HALF)
                steps = CT * NS * (half + 1) - CT + c + 1
                e.wait_ge(drive_done, steps)
                e.wait_ge(y_added, steps)
                nc.vector.scalar_tensor_tensor(out=dtu[:, c, cols], in0=xc[:, c, cols], scalar=dskip[:, c:c + 1],
                                               in1=psum[:, c], op0=ALU.mult, op1=ALU.add).then_inc(y_read, 1)

            def silu_gate(c, half):
                cols = slice(half * HALF, (half + 1) * HALF)
                e.wait_ge(y_read, CT * half + c + 1)
                nc.vector.scalar_tensor_tensor(out=dtu[:, c, cols], in0=dtu[:, c, cols], scalar=0.5,
                                               in1=sz2[:, c, cols], op0=ALU.mult, op1=ALU.mult).then_inc(inner_f, 1)

            e.wait_ge(weight_lo, NBUILD)
            for c in range(CT):
                dt_times_x(c, 0)
            steps = 2 * CT * NS
            for j in range(steps + 1):
                s, c = divmod(j, CT)
                if j < steps:
                    scan(j)
                if j >= 1:
                    weigh(j - 1)
                if s == 2:
                    dt_times_x(c, 1)
                if CT * NS + 1 <= j <= CT * NS + CT:
                    skip(j - CT * NS - 1, 0)
                if s in (NS + 2, NS + 3) and c % 2 == 0:
                    silu_gate(2 * (s - NS - 2) + c // 2, 0)
                if c == 0 and NS + 6 <= s < NS + 10:
                    add_out(e, s - NS - 6)
                if c == 2 and s in (NS + 7, NS + 9):
                    ln_statistics(e, 1, (s - NS - 7) // 2, lambda i: (res1, i + 1))
                if c == 0 and s == NS + 10:
                    ln_normalise(e, 1, 0)
                    ln_normalise(e, 1, 1)
                if c == 2 and s in (NS + 11, NS + 12):
                    turned_low(e, 1, s - NS - 11)
            for c in range(CT):
                skip(c, 1)
                silu_gate(c, 1)
            for c in (2, 3):
                e.wait_ge(inner_hi, CT + c + 1)
                split_lo(nc.vector, inner[1][:, c, HALF:TOK], dtu[:, c, HALF:TOK],
                         inner[0][:, c, HALF:TOK]).then_inc(inner_b_lo, 1)

        def add_out(e, i):
            e.wait_ge(op_made, i + 1)
            nc.vector.tensor_tensor(res[:, i], res[:, i], psum[:, 6 + i % 2, 0:DM], ALU.add).then_inc(res1, 1)

        own = [0]

        def dve_ffn(e, f):
            Q = 2 * FM

            def down(i):
                e.wait_ge(dn_made, NT * f + i + 1)
                nc.vector.tensor_tensor(res[:, i], res[:, i], psum[:, 6 + i % 2, 0:DM], ALU.add).then_inc(f_res, 1)

            for k in range(Q):
                n, m = divmod(k, FM)
                w = MW[m]
                e.wait_ge(f_tanhed, Q * f + k + 1)
                if k >= 2:
                    e.wait_ge(f_mult, Q * f + k - 1)
                nc.vector.scalar_tensor_tensor(out=f_gate[k % 2][0:w], in0=f_tanh[k % 2][0:w], scalar=1.0,
                                               in1=psum[0:w, f_slot(k)], op0=ALU.add,
                                               op1=ALU.mult).then_inc(f_gated, 1)
                e.wait_ge(f_gated, Q * f + k + 1)
                if k >= 2:
                    e.wait_ge(hid_lo, Q * f + k - 1)
                nc.vector.tensor_tensor(f_prod[k % 2][0:w], f_gate[k % 2][0:w], psum[0:w, f_slot(k) + 1],
                                        ALU.mult).then_inc(f_mult, 1)
                if k >= 1:
                    hid_low(e, f, k - 1)
                if k == FM + 1:
                    for i in range(4):
                        down(i)
                if f == 0 and k == 2:
                    for g in (2, 3):
                        add_out(e, 2 * g)
                        add_out(e, 2 * g + 1)
                        ln_statistics(e, 1, g, lambda i: (res1, i + 1))
                    ln_normalise(e, 1, 2)
                    ln_normalise(e, 1, 3)
                if f == 0 and k == 4:
                    turned_low(e, 1, 2)
                    turned_low(e, 1, 3)
                if f == 0 and k == FM + 2:
                    for g in range(2):
                        ln_statistics(e, 2, g, lambda i: (f_res, i + 1))
                    for g in range(2):
                        ln_normalise(e, 2, g)
            if f == 0:
                turned_low(e, 2, 0)
            hid_low(e, f, Q - 1)
            if f == 0:
                turned_low(e, 2, 1)
            for i in range(4, NT):
                down(i)
                if f == 0 and i % 2:
                    ln_statistics(e, 2, i // 2, lambda i: (f_res, i + 1))
            if f == 0:
                ln_normalise(e, 2, 2)
                ln_normalise(e, 2, 3)

        def hid_low(e, f, k):
            n, m = divmod(k, FM)
            w = MW[m]
            e.wait_ge(hid_hi, 2 * FM * f + k + 1)
            nc.vector.scalar_tensor_tensor(out=hid[n][1][0:w, m], in0=f_prod[k % 2][0:w], scalar=0.5,
                                           in1=f32(hid[n][0][0:w, m]), op0=ALU.mult,
                                           op1=ALU.subtract).then_inc(hid_lo, 1)

        def dve_attention(e):
            def unit(u):
                kind, a, b = u
                k = unit_no[u]
                acc = psum[:, unit_bank(k)]
                if kind == "Q":
                    e.wait_ge(unit_made, k + 1)
                    nc.vector.tensor_scalar(qstage[a][:, :, b], acc.rearrange("p (h t) -> p h t", t=HTOK), bq_t[:, b:b + 1], SCALE,
                                            ALU.add, ALU.mult).then_inc(unit_done, 1)
                elif kind == "O":
                    e.wait_ge(unit_made, k + 1)
                    if a == 0:
                        e.wait_ge(bo_added, NT)
                    else:
                        e.wait_ge(unit_done, unit_no[("O", a - 1, b)] + 1)
                    both = res[:, 2 * b:2 * b + 2].rearrange("p t c -> p (t c)")
                    nc.vector.tensor_tensor(both, both, acc, ALU.add).then_inc(unit_done, 1)
                else:
                    e.wait_ge(unit_hi, hi_no[u] + 1)
                    hi = f32(unit_target(u, 0))
                    if kind == "K":
                        nc.vector.scalar_tensor_tensor(out=unit_target(u, 1), in0=acc, scalar=bk_t[:, a:a + 1],
                                                       in1=hi, op0=ALU.add, op1=ALU.subtract).then_inc(unit_done, 1)
                    else:
                        nc.vector.tensor_tensor(unit_target(u, 1), acc, hi, ALU.subtract).then_inc(unit_done, 1)

            def row_max(n):
                h, i = divmod(n, NT)
                e.wait_ge(scored, n + 1)
                nc.vector.tensor_reduce(neg_max[:, h, i:i + 1],
                                        psum[:, 2 * (n % 2):2 * (n % 2) + 2].rearrange("p a b -> p (a b)")[:, 0:(i + 1) * P],
                                        AX_X, ALU.max, negate=True).then_inc(max_done, 1)

            def inverse(n):
                h, i = divmod(n, NT)
                e.wait_ge(exp_done, n + 1)
                nc.vector.reciprocal(row_inv[:, h, i:i + 1], row_sum[:, h, i:i + 1]).then_inc(inv_done, 1)

            def turned_lo(n):
                h, i = divmod(n, NT)
                for g, (a, b) in enumerate(groups(i)):
                    t = turned_before(n) + g
                    e.wait_ge(pT_hi, t + 1)
                    dst, src = turned_views(n, t, a, b)
                    nc.vector.tensor_tensor(dst[1], src, f32(dst[0]), ALU.subtract).then_inc(pT_lo, 1)

            def value_lo(n):
                s = n // 2
                e.wait_ge(oT_hi, s + 1)
                dst, src = value_views(s)
                nc.vector.scalar_tensor_tensor(out=dst[1], in0=src, scalar=bv_t[:, n // NT:n // NT + 1],
                                               in1=f32(dst[0]), op0=ALU.add, op1=ALU.subtract).then_inc(oT_lo, 1)

            e.wait_ge(ld["bias"], 64)
            for k, u in enumerate(first_units):
                unit(u)
                if k in (1, 3):
                    turned_low(e, 2, 2 + k // 2)
            for n in range(2):
                row_max(n)
            inverse(0)
            inverse(1)
            for n in range(NH * NT):
                if n + 2 < NH * NT:
                    row_max(n + 2)
                turned_lo(n)
                for u in units_at[n]:
                    unit(u)
                if n + 2 < NH * NT:
                    inverse(n + 2)
                if n % 2 == 0 and n:
                    value_lo(n - 1)
                if n < NT:
                    nc.vector.tensor_tensor(res[:, n], res[:, n], bo_row[:], ALU.add).then_inc(bo_added, 1)
            value_lo(NH * NT - 1)
            dve_layer_norm(e, 3, lambda i: (unit_done, unit_no[("O", NP - 1, i // 2)] + 1),
                           lambda i: None if i % 2 else unit(("O", NP - 1, i // 2)))

        @block.vector
        def _(e):
            nc.vector.memset(ones_col[:], 1.0).then_inc(ones_made, 1)
            dve_layer_norm(e, 0, lambda i: (ld["x"], 16))
            e.wait_ge(win_hi, 1)
            split_lo(nc.vector, win[1][:, :, 0:DI], win_raw[:, :, 0:DI], win[0][:, :, 0:DI]).then_inc(win_x_lo, 1)
            e.wait_ge(ld["lut"], 16)
            pairs = lut_row[:].rearrange("p (a b) -> p a b", b=2)
            nc.vector.tensor_tensor(lut_step[:], pairs[:, :, 1], pairs[:, :, 0], ALU.subtract).then_inc(small_done, 1)
            dve_bits(e, 0)
            e.wait_ge(ld["small"], 32)
            nc.vector.tensor_scalar(convw_half[:], convw[:], 0.5, None, ALU.mult).then_inc(dve_own, 1)
            own[0] += 1
            nc.vector.tensor_scalar(convb_half[:], convb[:], 0.5, None, ALU.mult).then_inc(small_done, 1)
            e.wait_ge(consts_made, 3)
            nc.vector.tensor_copy(ident_r[:], ident[:]).then_inc(consts_cast, 1)
            nc.vector.tensor_copy(ident_b[:], ident[:]).then_inc(consts_cast, 1)
            nc.vector.tensor_copy(causal_b[:], causal[:]).then_inc(consts_cast, 1)
            dve_mamba(e)
            dve_ffn(e, 0)
            dve_attention(e)
            dve_ffn(e, 1)

        def pool_rstd(e, L, g):
            two = slice(2 * g, 2 * g + 2)
            e.wait_ge(ln_mv, NT * L + 2 * g + 2)
            nc.gpsimd.tensor_scalar(var_eps[:, two], mean_var[:, two, 1], 1.0, EPS,
                                    ALU.mult, ALU.add).then_inc(pool_own, 1)
            pown[0] += 1
            e.wait_ge(pool_own, pown[0])
            nc.gpsimd.tensor_tensor(rstd[:, two], var_eps[:, two], half_neg[:, two], ALU.pow).then_inc(ln_rstd, 1)

        def pool_layer_norm(e, L):
            e.wait_ge(consts_made, 3)
            for g in range(NT // 2):
                pool_rstd(e, L, g)

        pown = [0]

        def pool_lo(e, lo, src, hi, s):
            split_lo(nc.gpsimd, lo, src, hi).then_inc(s, 1)

        def pool_attention(e):
            def split(name, r, part):
                pair = {"wk": wk, "wv": wv, "wo": wo}[name]
                if part:
                    e.wait_ge(w_split, split_no[(name, r)] - 1)
                    split_lo(nc.gpsimd, pair[1][:], w_raw[:], pair[0][:]).then_inc(w_split, 1)
                    return
                e.wait_ge(ld["w"], 8 * split_no[(name, r)])
                if r >= 1:
                    last = {"wk": ("K", 2 * r - 1, NB - 1), "wv": ("V", r - 1, NT // 2 - 1),
                            "wo": ("O", r - 1, NT // 2 - 1)}[name]
                    e.wait_ge(unit_made, unit_no[last] + 1)
                split_hi_pool(nc.gpsimd, pair[0][:], w_raw[:]).then_inc(w_split, 1)

            def split_wq(k):
                src, (hi, lo) = wq_raw[k % 2], wq[k % 3]
                e.wait_ge(ld[f"wq{k % 2}"], 16 * (k // 2 + 1))
                if k < 3:
                    split_hi_pool(nc.gpsimd, hi[:], src[:]).then_inc(wq_hi, 1)
                e.wait_ge(wq_hi, k + 1)
                split_lo(nc.gpsimd, lo[:], src[:], hi[:]).then_inc(wq_split, 1)

            def q_piece(h, pc):
                npc = TOK // SLAB
                if h >= 2:
                    e.wait_ge(scored, NT * (h - 1))
                if h == 1:
                    e.wait_ge(q_half_stored, 16)
                tok = SLAB // NH
                if pc == 0:
                    e.wait_ge(ld[f"q{h % 2}"], 16 * (h // 2 + 1))
                src = q_raw[h % 2][:, :, pc * tok:(pc + 1) * tok].rearrange("p c t -> p t c")
                hi, lo = (t[:, pc * SLAB:(pc + 1) * SLAB].rearrange("p (t c) -> p t c", c=NH) for t in q[h % 2])
                split_hi_pool(nc.gpsimd, hi, src).then_inc(q_hi, 1)
                e.wait_ge(q_hi, npc * h + pc + 1)
                split_lo(nc.gpsimd, lo, src, hi).then_inc(q_split, 1)

            def norm(n):
                h, i = divmod(n, NT)
                e.wait_ge(inv_done, n + 1)
                pr = probs[n % 2][:, 0:(i + 1) * P]
                nc.gpsimd.tensor_scalar(pr, pr, row_inv[:, h, i:i + 1], 0.0, ALU.mult, ALU.add).then_inc(normed, 1)

            split_wq(0)
            split("wk", 0, 0)
            split("wk", 0, 1)
            split_wq(1)
            split("wv", 0, 0)
            split("wv", 0, 1)
            split_wq(2)
            pool_layer_norm(e, 2)
            for k in range(3, 2 * NH // 4):
                split_wq(k)
            for pc in range(TOK // SLAB):
                q_piece(0, pc)
            norm(0)
            norm(1)
            for n in range(NH * NT):
                h, i = divmod(n, NT)
                r, st = h // 2, (h % 2) * NT + i
                if n + 2 < NH * NT:
                    norm(n + 2)
                if i < TOK // SLAB and h + 1 < NH:
                    q_piece(h + 1, i)
                if st in (4, 5) and r + 1 < NP:
                    split("wk", r + 1, st - 4)
                if st in (6, 7) and r + 1 < NP:
                    split("wv", r + 1, st - 6)
                if st in (12, 13):
                    split("wo", r, st - 12)

        @block.gpsimd
        def _(e):
            nc.gpsimd.memset(ident[:], 0.0).then_inc(pool_own, 1)
            nc.gpsimd.memset(causal[:], 0.0).then_inc(pool_own, 1)
            nc.gpsimd.memset(half_neg[:], -0.5).then_inc(consts_made, 1)
            e.wait_ge(pool_own, 2)
            pown[0] += 2
            nc.gpsimd.affine_select(out=ident[:], in_=ident[:], compare_op=ALU.not_equal, fill=1.0, base=0,
                                    pattern=[[-1, P]], channel_multiplier=1).then_inc(consts_made, 1)
            nc.gpsimd.affine_select(out=causal[:], in_=causal[:], compare_op=ALU.is_ge, fill=MASKED, base=0,
                                    pattern=[[-1, P]], channel_multiplier=1).then_inc(consts_made, 1)
            pool_layer_norm(e, 0)
            e.wait_ge(small_done, 1)
            mamba_weights = ((wx, wx_raw), (wdt, wdt_raw), (wout, wout_raw))
            for b in range(NBUILD + 2):
                if b < NBUILD:
                    _, _, _, parts, cols = builds[b]
                    a = lambda t: t[0:parts, 0:cols]
                    e.wait_ge(bits_done, 4 * b + 1)
                    if b >= 2:
                        e.wait_ge(weight_picked, 7 * (b - 1))
                    for k in range(act_share[b], PICKS):
                        nc.gpsimd.tensor_scalar(a(pick(b)[k]), a(bits[b % 2][0]), lut_step[0:parts, k:k + 1],
                                                lut_row[0:parts, 2 * k:2 * k + 1], ALU.mult,
                                                ALU.add).then_inc(pool_picks, 1)
                if b >= 2:
                    _, _, _, parts, cols = builds[b - 2]
                    a = lambda t: t[0:parts, 0:cols]
                    e.wait_ge(weight_hi, b - 1)
                    src = built[(b - 2) % 3]
                    pool_lo(e, a(src[1]), a(picked[(b - 2) % 3]), a(src[0]), weight_lo)
                if b == 0:
                    e.wait_ge(win_hi, 2)
                    pool_lo(e, win[1][:, :, DI:2 * DI], win_raw[:, :, DI:2 * DI], win[0][:, :, DI:2 * DI], win_z_lo)
                if b < 3:
                    w, raw = mamba_weights[b]
                    e.wait_ge(mw_hi, b + 1)
                    pool_lo(e, w[1][:], raw[:], w[0][:], mw_lo)
                if 3 <= b < 3 + CT:
                    if b == 3:
                        e.wait_ge(mw_lo, 3)
                    e.wait_ge(xc_hi, b - 2)
                    pool_lo(e, inner[1][:, b - 3], xc[:, b - 3], inner[0][:, b - 3], xc_lo)
            all_spilled(e)
            def inner_low(c, half):
                e.wait_ge(inner_hi, CT * half + c + 1)
                cols = slice(half * HALF, (half + 1) * HALF)
                pool_lo(e, inner[1][:, c, cols], dtu[:, c, cols], inner[0][:, c, cols], inner_a_lo)

            for j in range(2 * CT * NS):
                s, c = divmod(j, CT)
                half = s // NS
                if c == 0:
                    e.wait_ge(row_copied, 2 * s + 1)
                if s % NS == 0:
                    e.wait_ge(dtu_done, CT * half + c + 1)
                if j >= 3:
                    e.wait_ge(scanned, j - 2)
                nc.gpsimd.tensor_tensor(drive[j % 3], dtu[:, c, half * HALF:(half + 1) * HALF], b_row[s % 3],
                                        ALU.mult).then_inc(drive_done, 1)
                if s == NS + 4:
                    inner_low(c, 0)
                if s == NS + 9 and c == 3:
                    pool_rstd(e, 1, 0)
                    pool_rstd(e, 1, 1)
            inner_low(0, 1)
            inner_low(1, 1)
            pool_rstd(e, 1, 2)
            pool_rstd(e, 1, 3)
            pool_attention(e)
            pool_layer_norm(e, 3)


INPUTS = [
    "L0_attn_a_x", "L0_attn_a_W_in", "L0_attn_a_conv_w", "L0_attn_a_conv_b", "L0_attn_a_W_x", "L0_attn_a_W_dt",
    "L0_attn_a_b_dt", "L0_attn_a_A_log", "L0_attn_a_D", "L0_attn_a_W_out", "L0_attn_b_Wq", "L0_attn_b_bq",
    "L0_attn_b_Wk", "L0_attn_b_bk", "L0_attn_b_Wv", "L0_attn_b_bv", "L0_attn_b_Wo", "L0_attn_b_bo",
    "L0_ffn_lut", "L0_ffn_gate_idx", "L0_ffn_up_idx", "L0_ffn_down_idx",
]


def kernel(**inputs):
    import concourse.bacc as bacc
    from concourse.bass_utils import run_bass_kernel_spmd

    nc = bacc.Bacc("TRN2", target_bir_lowering=False, num_devices=1)
    arrays, args = {}, []
    for name in INPUTS:
        a = np.asarray(inputs[name])
        shape = a.shape
        if name == "L0_attn_a_x":
            a = a.reshape(shape[-2:])
        if name.endswith("_idx"):
            a = a.T
        a = np.ascontiguousarray(a)
        arrays["in_" + name] = a
        args.append(nc.dram_tensor("in_" + name, list(a.shape), mybir.dt.from_np(a.dtype), kind="ExternalInput").ap())
    x_shape = np.asarray(inputs["L0_attn_a_x"]).shape
    out = nc.dram_tensor("out_x", list(x_shape[-2:]), F32, kind="ExternalOutput").ap()
    hybrid_block(nc, *args, out)
    got = run_bass_kernel_spmd(nc, [arrays], core_ids=[0])
    return got.results[0]["out_x"].reshape(x_shape)
```
